# Optimizing a Trainium2 kernel written in Bass

```python
import numpy as np
import jax
import jax.numpy as jnp

def _softmax(x, axis=-1):
    return jax.nn.softmax(x, axis=axis)

def _gelu(x):
    return jax.nn.gelu(x, approximate=True)

def _silu(x):
    return jax.nn.silu(x)

def _sigmoid(x):
    return jax.nn.sigmoid(x)

def _layernorm(x, axis=-1, eps=1e-05):
    m = jnp.mean(x, axis=axis, keepdims=True)
    v = jnp.var(x, axis=axis, keepdims=True)
    return (x - m) / jnp.sqrt(v + eps)

def _scatter_add(tgt, idx, src, axis=0):
    return tgt.at[idx].add(src)

def _segment_sum(src, seg, n):
    return jax.ops.segment_sum(src, seg, n)
kernel_name = 'mk_xattn_ffn_d2_seqx_r8_9b44a0'

def setup_inputs(seed: int=0):
    np.random.seed(seed)
    _w = jnp.asarray

    def _rec_inputs():
        import jax
        import jax.numpy as jnp
        _rk = jax.random.key(seed)
        x = -0.0002928 + 1 * jax.random.normal(jax.random.fold_in(_rk, 1), (8, 256, 128), jnp.float32)
        _lenS = 256 - jax.random.randint(jax.random.fold_in(_rk, 7), (8,), 0, max(1, 256 // 4) + 1, jnp.int32)
        _lenS2 = 256 - jax.random.randint(jax.random.fold_in(_rk, 8), (8,), 0, max(1, 256 // 4) + 1, jnp.int32)
        _ctx_1024P = jax.random.normal(jax.random.fold_in(_rk, 11), (8, 16, 128), jnp.float32)
        _ctx_1024c = jax.random.dirichlet(jax.random.fold_in(_rk, 511), 0.3 * jnp.ones((16,), jnp.float32), (8, 256))
        _ctx_1024t = jnp.einsum('bsk,bkd->bsd', _ctx_1024c, _ctx_1024P)
        _ctx_1024t = _ctx_1024t * jax.lax.rsqrt(jnp.mean(jnp.square(_ctx_1024t)) + 1e-12) * 0.953939
        ctx_1024 = -1.39393e-06 + 0.999914 * (_ctx_1024t + 0.3 * jax.random.normal(jax.random.fold_in(_rk, 611), (8, 256, 128), jnp.float32))
        return (x, ctx_1024)
    x, ctx_1024 = _rec_inputs()

    def _L0_xattn_setup():
        import jax, jax.numpy as jnp
        import numpy as np
        import math
        D_MODEL = 128
        NUM_HEADS = 16
        MAX_LEN = 256
        D_HEAD = D_MODEL // NUM_HEADS
        BATCH = 2
        SEQ = 256

        def _skew(QEr):
            B, H, R, C = QEr.shape
            padded = jnp.pad(QEr, ((0, 0), (0, 0), (0, 0), (1, 0)))
            reshaped = padded.reshape(B, H, C + 1, R)
            return reshaped[:, :, 1:, :]
        root = jax.random.key(seed)
        ks = jax.random.split(root, 10)
        s = 1.0 / math.sqrt(D_MODEL)
        return {'query': jax.random.normal(ks[0], (BATCH, SEQ, D_MODEL), jnp.float32), 'key': jax.random.normal(ks[1], (BATCH, SEQ, D_MODEL), jnp.float32), 'value': jax.random.normal(ks[2], (BATCH, SEQ, D_MODEL), jnp.float32), 'Wq': jax.random.normal(ks[3], (D_MODEL, D_MODEL), jnp.float32) * s, 'bq': jax.random.normal(ks[4], (D_MODEL,), jnp.float32) * s, 'Wk': jax.random.normal(ks[5], (D_MODEL, D_MODEL), jnp.float32) * s, 'bk': jax.random.normal(ks[6], (D_MODEL,), jnp.float32) * s, 'Wv': jax.random.normal(ks[7], (D_MODEL, D_MODEL), jnp.float32) * s, 'bv': jax.random.normal(ks[8], (D_MODEL,), jnp.float32) * s, 'Er': jax.random.normal(ks[9], (MAX_LEN, D_HEAD), jnp.float32)}
    _L0_xattn_all = _L0_xattn_setup()
    _L0_xattn_in = {k: v for k, v in _L0_xattn_all.items() if k in ('Wq', 'bq', 'Wk', 'bk', 'Wv', 'bv', 'Er')}
    del _L0_xattn_all

    def _L0_ffn_setup():
        import jax, jax.numpy as jnp
        import numpy as np
        DIM = 128
        NUM_EXPERTS = 8
        TOP_K = 2
        HIDDEN = int(DIM * 1.5)
        key = jax.random.key(seed)
        k_x, k_r, k_w1, k_w2, k_w3 = jax.random.split(key, 5)
        B, T = (2, 512)
        s_in = 1.0 / np.sqrt(DIM)
        s_h = 1.0 / np.sqrt(HIDDEN)
        return {'x': jax.random.normal(k_x, (B, T, DIM), dtype=jnp.float32), 'Wr': jax.random.uniform(k_r, (DIM, NUM_EXPERTS), minval=-s_in, maxval=s_in, dtype=jnp.float32), 'W1': jax.random.uniform(k_w1, (NUM_EXPERTS, DIM, HIDDEN), minval=-s_in, maxval=s_in, dtype=jnp.float32), 'W2': jax.random.uniform(k_w2, (NUM_EXPERTS, HIDDEN, DIM), minval=-s_h, maxval=s_h, dtype=jnp.float32), 'W3': jax.random.uniform(k_w3, (NUM_EXPERTS, DIM, HIDDEN), minval=-s_in, maxval=s_in, dtype=jnp.float32)}
    _L0_ffn_all = _L0_ffn_setup()
    _L0_ffn_in = {k: v for k, v in _L0_ffn_all.items() if k in ('Wr', 'W1', 'W2', 'W3')}
    del _L0_ffn_all

    def _L1_xattn_setup():
        import jax, jax.numpy as jnp
        import numpy as np
        D_MODEL = 128
        NUM_HEADS = 16
        D_K = D_MODEL // NUM_HEADS

        def _split_heads(x, B):
            return x.reshape(B, -1, NUM_HEADS, D_K).transpose(0, 2, 1, 3)
        key = jax.random.key(seed)
        ks = jax.random.split(key, 11)
        B, S = (2, 256)
        s = 1.0 / np.sqrt(D_MODEL)
        inp = {'Q': jax.random.normal(ks[0], (B, S, D_MODEL), jnp.float32), 'K': jax.random.normal(ks[1], (B, S, D_MODEL), jnp.float32), 'V': jax.random.normal(ks[2], (B, S, D_MODEL), jnp.float32), 'Wq': jax.random.normal(ks[3], (D_MODEL, D_MODEL), jnp.float32) * s, 'bq': jnp.zeros((D_MODEL,), jnp.float32), 'Wk': jax.random.normal(ks[4], (D_MODEL, D_MODEL), jnp.float32) * s, 'bk': jnp.zeros((D_MODEL,), jnp.float32), 'Wv': jax.random.normal(ks[5], (D_MODEL, D_MODEL), jnp.float32) * s, 'bv': jnp.zeros((D_MODEL,), jnp.float32), 'Wo': jax.random.normal(ks[6], (D_MODEL, D_MODEL), jnp.float32) * s, 'bo': jnp.zeros((D_MODEL,), jnp.float32)}
        return inp
    _L1_xattn_all = _L1_xattn_setup()
    _L1_xattn_in = {k: v for k, v in _L1_xattn_all.items() if k in ('Wq', 'bq', 'Wk', 'bk', 'Wv', 'bv', 'Wo', 'bo')}
    del _L1_xattn_all

    def _L1_ffn_setup():
        import jax, jax.numpy as jnp
        import numpy as np
        H = 128
        M = 64
        E = 16
        TOP_K = 2
        SCALE = 2.5
        NORM_TOPK = True
        B, S = (1, 128)

        def _moe(x, gate_w, w_gate, w_up, w_down, ws_gate, ws_up, ws_down):
            T = x.shape[0]
            shared = jax.nn.silu(x @ ws_gate) * (x @ ws_up) @ ws_down
            scores = jax.nn.sigmoid(x.astype(jnp.float32) @ gate_w.T.astype(jnp.float32))
            topk_w, topk_idx = jax.lax.top_k(scores, TOP_K)
            if NORM_TOPK and TOP_K > 1:
                topk_w = topk_w / (topk_w.sum(-1, keepdims=True) + 1e-20)
            topk_w = topk_w * SCALE
            route = jnp.zeros((T, E), topk_w.dtype).at[jnp.arange(T)[:, None], topk_idx].set(topk_w)
            g = jnp.einsum('th,ehm->etm', x, w_gate)
            u = jnp.einsum('th,ehm->etm', x, w_up)
            eo = jnp.einsum('etm,emh->eth', jax.nn.silu(g) * u, w_down)
            routed = jnp.einsum('te,eth->th', route.astype(x.dtype), eo)
            return routed + shared
        key = jax.random.key(seed)
        ks = jax.random.split(key, 8)
        std = 0.02
        return {'hidden_states': jax.random.normal(ks[0], (B, S, H), jnp.float32), 'gate_w': jax.random.normal(ks[1], (E, H), jnp.float32) * std, 'w_gate': jax.random.normal(ks[2], (E, H, M), jnp.float32) * std, 'w_up': jax.random.normal(ks[3], (E, H, M), jnp.float32) * std, 'w_down': jax.random.normal(ks[4], (E, M, H), jnp.float32) * std, 'ws_gate': jax.random.normal(ks[5], (H, M), jnp.float32) * std, 'ws_up': jax.random.normal(ks[6], (H, M), jnp.float32) * std, 'ws_down': jax.random.normal(ks[7], (M, H), jnp.float32) * std}
    _L1_ffn_all = _L1_ffn_setup()
    _L1_ffn_in = {k: v for k, v in _L1_ffn_all.items() if k in ('gate_w', 'w_gate', 'w_up', 'w_down', 'ws_gate', 'ws_up', 'ws_down')}
    del _L1_ffn_all
    return {'x': x, 'ctx_1024': ctx_1024, 'L0_xattn_Wq': _L0_xattn_in['Wq'], 'L0_xattn_bq': _L0_xattn_in['bq'], 'L0_xattn_Wk': _L0_xattn_in['Wk'], 'L0_xattn_bk': _L0_xattn_in['bk'], 'L0_xattn_Wv': _L0_xattn_in['Wv'], 'L0_xattn_bv': _L0_xattn_in['bv'], 'L0_xattn_Er': _L0_xattn_in['Er'], 'L0_ffn_Wr': _L0_ffn_in['Wr'], 'L0_ffn_W1': _L0_ffn_in['W1'], 'L0_ffn_W2': _L0_ffn_in['W2'], 'L0_ffn_W3': _L0_ffn_in['W3'], 'L1_xattn_Wq': _L1_xattn_in['Wq'], 'L1_xattn_bq': _L1_xattn_in['bq'], 'L1_xattn_Wk': _L1_xattn_in['Wk'], 'L1_xattn_bk': _L1_xattn_in['bk'], 'L1_xattn_Wv': _L1_xattn_in['Wv'], 'L1_xattn_bv': _L1_xattn_in['bv'], 'L1_xattn_Wo': _L1_xattn_in['Wo'], 'L1_xattn_bo': _L1_xattn_in['bo'], 'L1_ffn_gate_w': _L1_ffn_in['gate_w'], 'L1_ffn_w_gate': _L1_ffn_in['w_gate'], 'L1_ffn_w_up': _L1_ffn_in['w_up'], 'L1_ffn_w_down': _L1_ffn_in['w_down'], 'L1_ffn_ws_gate': _L1_ffn_in['ws_gate'], 'L1_ffn_ws_up': _L1_ffn_in['ws_up'], 'L1_ffn_ws_down': _L1_ffn_in['ws_down']}

def reference(x, ctx_1024, L0_xattn_Wq, L0_xattn_bq, L0_xattn_Wk, L0_xattn_bk, L0_xattn_Wv, L0_xattn_bv, L0_xattn_Er, L0_ffn_Wr, L0_ffn_W1, L0_ffn_W2, L0_ffn_W3, L1_xattn_Wq, L1_xattn_bq, L1_xattn_Wk, L1_xattn_bk, L1_xattn_Wv, L1_xattn_bv, L1_xattn_Wo, L1_xattn_bo, L1_ffn_gate_w, L1_ffn_w_gate, L1_ffn_w_up, L1_ffn_w_down, L1_ffn_ws_gate, L1_ffn_ws_up, L1_ffn_ws_down):
    import jax
    import jax.numpy as jnp

    def _L0_xattn_ref(query, key, value, Wq, bq, Wk, bk, Wv, bv, Er):
        import jax, jax.numpy as jnp
        import numpy as np
        import math
        D_MODEL = 128
        NUM_HEADS = 16
        MAX_LEN = 256
        D_HEAD = D_MODEL // NUM_HEADS
        BATCH = 2
        SEQ = 256

        def _skew(QEr):
            B, H, R, C = QEr.shape
            padded = jnp.pad(QEr, ((0, 0), (0, 0), (0, 0), (1, 0)))
            reshaped = padded.reshape(B, H, C + 1, R)
            return reshaped[:, :, 1:, :]
        B, S, D = query.shape
        H, dh = (NUM_HEADS, D_HEAD)
        q = (jnp.einsum('bsd,ed->bse', query, Wq) + bq).reshape(B, S, H, dh).transpose(0, 2, 1, 3)
        k = (jnp.einsum('bsd,ed->bse', key, Wk) + bk).reshape(B, S, H, dh).transpose(0, 2, 1, 3)
        v = (jnp.einsum('bsd,ed->bse', value, Wv) + bv).reshape(B, S, H, dh).transpose(0, 2, 1, 3)
        start = MAX_LEN - S
        Er_s = Er[start:, :]
        QEr = jnp.einsum('bhsd,ld->bhsl', q, Er_s)
        Srel = _skew(QEr)
        QK = jnp.einsum('bhsd,bhtd->bhst', q, k)
        attn = (QK + Srel) / math.sqrt(dh)
        causal = jnp.tril(jnp.ones((S, S), dtype=bool))
        attn = jnp.where(causal[None, None], attn, -jnp.inf)
        attn = jax.nn.softmax(attn, axis=-1)
        out = jnp.einsum('bhst,bhtd->bhsd', attn, v)
        out = out.transpose(0, 2, 1, 3).reshape(B, S, D)
        return out

    def _L0_ffn_ref(x, Wr, W1, W2, W3):
        import jax, jax.numpy as jnp
        import numpy as np
        DIM = 128
        NUM_EXPERTS = 8
        TOP_K = 2
        HIDDEN = int(DIM * 1.5)
        B, T, C = x.shape
        xf = x.reshape(-1, C)
        gate_logits = xf @ Wr
        w, idx = jax.lax.top_k(gate_logits, TOP_K)
        w = jax.nn.softmax(w, axis=-1)
        comb = jnp.sum(w[:, :, None] * jax.nn.one_hot(idx, NUM_EXPERTS, dtype=w.dtype), axis=1)
        h = jnp.einsum('nc,ech->neh', xf, W1)
        g = jnp.einsum('nc,ech->neh', xf, W3)
        y = jnp.einsum('neh,ehc->nec', jax.nn.silu(h) * g, W2)
        out = jnp.einsum('nec,ne->nc', y, comb)
        return out.reshape(B, T, C)

    def _L1_xattn_ref(Q, K, V, Wq, bq, Wk, bk, Wv, bv, Wo, bo):
        import jax, jax.numpy as jnp
        import numpy as np
        D_MODEL = 128
        NUM_HEADS = 16
        D_K = D_MODEL // NUM_HEADS

        def _split_heads(x, B):
            return x.reshape(B, -1, NUM_HEADS, D_K).transpose(0, 2, 1, 3)
        B, S, _ = Q.shape
        q = _split_heads(Q @ Wq.T + bq, B)
        k = _split_heads(K @ Wk.T + bk, B)
        v = _split_heads(V @ Wv.T + bv, B)
        scale = 1.0 / jnp.sqrt(jnp.asarray(D_K, q.dtype))
        scores = jnp.einsum('bhqd,bhkd->bhqk', q, k) * scale
        attn = jax.nn.softmax(scores, axis=-1)
        ctx = jnp.einsum('bhqk,bhkd->bhqd', attn, v)
        ctx = ctx.transpose(0, 2, 1, 3).reshape(B, S, D_MODEL)
        out = ctx @ Wo.T + bo
        return out

    def _L1_ffn_ref(hidden_states, gate_w, w_gate, w_up, w_down, ws_gate, ws_up, ws_down):
        import jax, jax.numpy as jnp
        import numpy as np
        H = 128
        M = 64
        E = 16
        TOP_K = 2
        SCALE = 2.5
        NORM_TOPK = True
        B, S = (1, 128)

        def _moe(x, gate_w, w_gate, w_up, w_down, ws_gate, ws_up, ws_down):
            T = x.shape[0]
            shared = jax.nn.silu(x @ ws_gate) * (x @ ws_up) @ ws_down
            scores = jax.nn.sigmoid(x.astype(jnp.float32) @ gate_w.T.astype(jnp.float32))
            topk_w, topk_idx = jax.lax.top_k(scores, TOP_K)
            if NORM_TOPK and TOP_K > 1:
                topk_w = topk_w / (topk_w.sum(-1, keepdims=True) + 1e-20)
            topk_w = topk_w * SCALE
            route = jnp.zeros((T, E), topk_w.dtype).at[jnp.arange(T)[:, None], topk_idx].set(topk_w)
            g = jnp.einsum('th,ehm->etm', x, w_gate)
            u = jnp.einsum('th,ehm->etm', x, w_up)
            eo = jnp.einsum('etm,emh->eth', jax.nn.silu(g) * u, w_down)
            routed = jnp.einsum('te,eth->th', route.astype(x.dtype), eo)
            return routed + shared
        b, s, h = hidden_states.shape
        x = hidden_states.reshape(-1, h)
        out = _moe(x, gate_w, w_gate, w_up, w_down, ws_gate, ws_up, ws_down)
        return out.reshape(b, s, h)
    x = x + _L0_xattn_ref(_layernorm(x, axis=-1), ctx_1024, ctx_1024, L0_xattn_Wq, L0_xattn_bq, L0_xattn_Wk, L0_xattn_bk, L0_xattn_Wv, L0_xattn_bv, L0_xattn_Er)
    x = x + _L0_ffn_ref(_layernorm(x, axis=-1), L0_ffn_Wr, L0_ffn_W1, L0_ffn_W2, L0_ffn_W3)
    x = x + _L1_xattn_ref(_layernorm(x, axis=-1), ctx_1024, ctx_1024, L1_xattn_Wq, L1_xattn_bq, L1_xattn_Wk, L1_xattn_bk, L1_xattn_Wv, L1_xattn_bv, L1_xattn_Wo, L1_xattn_bo)
    x = x + _L1_ffn_ref(_layernorm(x, axis=-1), L1_ffn_gate_w, L1_ffn_w_gate, L1_ffn_w_up, L1_ffn_w_down, L1_ffn_ws_gate, L1_ffn_ws_up, L1_ffn_ws_down)
    return x

_drawn_inputs = setup_inputs


def setup_inputs(seed=0):
    import zlib

    import numpy as np

    out = dict(_drawn_inputs(seed))
    spreads = {'L1_xattn_bq': (0.0, 0.468),
     'L1_xattn_bk': (0.0, 0.8),
     'L1_xattn_bv': (0.0, 0.1),
     'L1_xattn_bo': (0.0, 0.1)}
    factors = {'L0_xattn_bk': 8.0,
     'L1_ffn_gate_w': 8.0,
     'L1_ffn_w_gate': 8.0,
     'L1_ffn_w_up': 8.0,
     'L1_ffn_w_down': 8.0,
     'L1_ffn_ws_gate': 8.0,
     'L1_ffn_ws_up': 8.0,
     'L1_ffn_ws_down': 8.0}
    for name, (base, spread) in spreads.items():
        noise = np.random.default_rng([zlib.crc32(name.encode()), seed]).standard_normal(out[name].shape)
        drawn = base * np.exp(spread * noise) if base else spread * noise
        out[name] = jnp.asarray(drawn.astype(out[name].dtype))
    for name, factor in factors.items():
        out[name] = (out[name] * factor).astype(out[name].dtype)
    return out
```

```python
from contextlib import ExitStack

import numpy as np
import concourse.bass as bass
from concourse import mybir

F32 = mybir.dt.float32
F32R = mybir.dt.float32r
ALU = mybir.AluOpType
ACT = mybir.ActivationFunctionType
AX = mybir.AxisListType

P = 128
B, S, D = 8, 256, 128
H, DH = 16, 8
HH = 4
G = H // HH
QUAD = P // HH
IT = S // P
EPS = 1e-5
SCALE = float(DH) ** -0.5
MASKED = -1.0e30
LOWEST = -3.0e38
BANK = 512
PITCH = S + P
MAXROW = 3 * DH


def after(eng, sem, count):
    if not (isinstance(count, int) and count <= 0):
        eng.wait_ge(sem, count)


def every_batch(eng, first, both, last):
    first(0, 0)
    both(0, 0)
    both(1, 1)
    for turn in range(1, B // 2 - 1):
        both(turn * 2, 0)
        both(turn * 2 + 1, 1)
    both(B - 2, 0)
    last(B - 1, 1)


def tokens(X, b, t=0, n=1):
    return X[:, bass.ds(b * S + t * D, n * D)]


def relative_attention(nc, X, ident, x_dram, d, rel):
    with ExitStack() as ctx:
        def sb(name, shape, dt=F32):
            return ctx.enter_context(nc.sbuf_tensor("a0_" + name, shape, dt))

        def sem(name):
            return ctx.enter_context(nc.semaphore("a0_" + name))

        ctxT = sb("ctxT", [P, 2, S])
        WqR = sb("WqR", [P, G, P])
        WkR = sb("WkR", [P, G, P])
        WvT = sb("WvT", [P, D])
        bqR = sb("bqR", [P, G])
        bkR = sb("bkR", [P, G])
        lo = sb("lo", [P, 2])
        bv = sb("bv", [P, D])
        ErM = sb("ErM", [P, HH, S], F32R)
        mask = sb("mask", [P, P])
        half = sb("half", [P, IT])
        stats = sb("stats", [P, 2, IT, 6])
        mv = sb("mv", [P, 2, IT, 2])
        veps = sb("veps", [P, 2, IT])
        rstd = sb("rstd", [P, 2, IT])
        xn = sb("xn", [P, 2, IT, D])
        xnT = sb("xnT", [P, 2, S])
        full = sb("full", [P, 4, 2, S])
        high = sb("high", [P, 2, 2, S], F32R)
        qst = sb("qst", [P, 2, G, S], F32R)
        kst = sb("kst", [P, 2, G, S], F32R)
        kmask = sb("kmask", [P, 2, HH, G, S], F32R)
        vaug = sb("vaug", [P, 2, IT, H, QUAD])
        qe = sb("qe", [P, 4, HH, S])
        tr = sb("tr", [P, 2, G, HH, P + S])
        T = sb("T", [P, 2, HH, P + S])
        rowmax = sb("rowmax", [P, 2, IT, HH])
        Tm = sb("Tm", [P, 2, HH, P + S])
        PT = sb("PT", [P, 2, IT, HH, S])
        OT = sb("OT", [P, G, S])
        rden = sb("rden", [P, IT, H])
        att = sb("att", [P, IT, D])

        bank = [ctx.enter_context(nc.psum_tensor(f"a0_bank{i}", [P, BANK], F32)) for i in range(8)]
        proj, outp, qeb, scb, ttb = bank[0], bank[1], bank[2:4], bank[4:6], bank[6:8]

        weights = sem("weights")
        x_in = sem("x_in")
        ctx_in = [sem("ctx_in0"), sem("ctx_in1")]
        consts = sem("consts")
        maskrow, er_high = sem("maskrow"), sem("er_high")
        bn_raw, bn_mean, var_ready = sem("bn_raw"), sem("bn_mean"), sem("var_ready")
        half_set, rstd_ready = sem("half_set"), sem("rstd_ready")
        xn_ready = sem("xn_ready")
        proj_full, proj_read = sem("proj_full"), sem("proj_read")
        high_ready, stack_ready = sem("high_ready"), sem("stack_ready")
        kmask_in = sem("kmask_in")
        v_full, v_read = sem("v_full"), sem("v_read")
        qe_full, qe_read = sem("qe_full"), sem("qe_read")
        qe_out = [sem(f"qe_out{i}") for i in range(4)]
        tr_in = [[sem(f"tr_in{p}{g}") for g in range(G)] for p in range(2)]
        sc_full, t_ready, tm_ready = sem("sc_full"), sem("t_ready"), sem("tm_ready")
        tt_full, pt_ready, pv_done = sem("tt_full"), sem("pt_ready"), sem("pv_done")
        ot_ready, o_full, rden_ready, att_ready, x_new = (
            sem("ot_ready"), sem("o_full"), sem("rden_ready"), sem("att_ready"), sem("x_new"))

        block = ctx.enter_context(nc.Block())

        @block.sync
        def _(sp):
            loads = ((X[:], x_dram.rearrange("(t p) d -> p t d", p=P)),)
            sp.dma_start(X[:].rearrange("p (t d) -> p t d", d=D), loads[0][1]).then_inc(x_in, 16)
            for dst, src in ((WqR, "WqR0"), (WkR, "WkR0"), (WvT, "WvT0"), (bqR, "bqR0"), (bkR, "bkR0"), (lo, "lo"),
                             (ident, "ident")):
                sp.dma_start(dst[:], d[src]).then_inc(weights, 16)
            sp.dma_start(bv[:], d["bv0"].partition_broadcast(P)).then_inc(weights, 16)
            sp.dma_start(qe[:, 0], d["ErR"]).then_inc(weights, 16)
            for b in range(2):
                sp.dma_start(ctxT[:, b, :], d["ctxT"][:, b * S:(b + 1) * S]).then_inc(ctx_in[b], 16)
            sp.wait_ge(consts, 1)
            for p in range(2):
                for h in range(H):
                    sp.dma_start(rel[p, h, :, S:PITCH].rearrange("(t i) l -> i t l", i=P),
                                 mask[:].unsqueeze(1).to_broadcast([P, IT, P])).then_inc(maskrow, 16)
            sp.wait_ge(maskrow, 16 * 2 * H)

            def first(b, p):
                sp.wait_ge(stack_ready, 4 * b + 4)
                after(sp, consts, 4 if isinstance(b, int) and b < 2 else 4)
                after(sp, sc_full, 12 * (b - 1))
                for hh in range(HH):
                    q = slice(QUAD * hh, QUAD * hh + QUAD)
                    sp.dma_start(kmask[q, p, hh, :, :].bitcast(F32), kst[q, p, :, :].bitcast(F32)).then_inc(kmask_in, 16)
                for g in range(G + 1):
                    if g < G:
                        for t in range(IT):
                            n = (2 * g + t) % 4
                            l0 = S - P * (t + 1)
                            sp.wait_ge(qe_read, 12 * b + 3 * g + 1 + 2 * t)
                            after(sp, t_ready, 12 * (b - 2) + 3 * g + 3)
                            sp.dma_start(
                                rel[p, HH * g:HH * g + HH, P * t:P * t + P, l0:S].rearrange("h i l -> i h l"),
                                qe[:, n, :, l0:S]).then_inc(qe_out[n], 16)
                    if g >= 1:
                        r = g - 1
                        for t in range(IT):
                            sp.wait_ge(qe_out[(2 * r + t) % 4], 16 * (2 * b + r // 2 + 1))
                        for t in range(IT):
                            i0 = P * t
                            at = rel[p, HH * r, i0:i0 + 1, S - 1 - i0:S]
                            src = bass.AP(tensor=at.tensor, offset=at.offset,
                                          ap=[[PITCH - 1, P], [S * PITCH, HH], [1, P * (t + 1)]])
                            dst = tr[:, p, r, :, 0:P] if t == 0 else tr[:, p, r, :, P:P + S]
                            sp.dma_start(dst, src).then_inc(tr_in[p][r], 16)

            def both(b, p):
                if not isinstance(b, int) or b + 2 < B:
                    sp.wait_ge(v_read, b + 1)
                    sp.wait_ge(proj_read, 5 * b + 5)
                    sp.wait_ge(consts, 4)
                    sp.dma_start(ctxT[:, p, :], d["ctxT"][:, bass.ds((b + 2) * S, S)]).then_inc(ctx_in[p], 16)
                first(b + 1, 1 - p)

            every_batch(sp, first, both, lambda b, p: None)

        @block.gpsimd
        def _(pool):
            nc.gpsimd.memset(half[:], -0.5).then_inc(half_set, 1)
            pool.wait_ge(half_set, 1)

            def first(b, p):
                pool.wait_ge(var_ready, b + 1)
                after(pool, xn_ready, b - 1)
                nc.gpsimd.tensor_tensor(rstd[:, p, :], veps[:, p, :], half[:], ALU.pow).then_inc(rstd_ready, 1)

            def main(b, p, g):
                u = 4 * b + g
                after(pool, tt_full, 3 * (u - 1))
                for t in range(IT):
                    c = slice(0, P) if t == 0 else slice(P, P + S)
                    pool.wait_ge(t_ready, 3 * u + 1 + 2 * t)
                    nc.gpsimd.tensor_tensor(
                        Tm[:, g % 2, :, c], T[:, g % 2, :, c],
                        rowmax[:, g % 2, t, :].unsqueeze(2).to_broadcast([P, HH, P * (t + 1)]),
                        ALU.subtract).then_inc(tm_ready, 1)

            def both(b, p):
                for g in range(G):
                    main(b, p, g)
                    if g == 0:
                        first(b + 1, 1 - p)

            def last(b, p):
                for g in range(G):
                    main(b, p, g)

            every_batch(pool, first, both, last)

        @block.vector
        def _(dve):
            nc.vector.memset(mask[:], MASKED).then_inc(consts, 1)
            dve.wait_ge(weights, 16 * 9)
            erh = high[:].rearrange("p a b s -> p (a b s)")
            nc.vector.tensor_copy(erh, qe[:, 0].rearrange("p h s -> p (h s)")).then_inc(er_high, 1)
            dve.wait_ge(er_high, 1)
            nc.vector.scalar_tensor_tensor(ErM[:].rearrange("p h s -> p (h s)"), erh.bitcast(F32), lo[:, 1:2],
                                           qe[:, 0].rearrange("p h s -> p (h s)"),
                                           ALU.mult, ALU.add).then_inc(consts, 1)
            for p in range(2):
                nc.vector.memset(kmask[:, p].bitcast(F32), 0.0).then_inc(consts, 1)
            for p in range(2):
                nc.vector.memset(vaug[:, p], 0.0).then_inc(consts, 1)
            dve.wait_ge(consts, 6)
            for p in range(2):
                nc.vector.memset(vaug[:, p, :, :, DH:DH + 1], 1.0).then_inc(consts, 1)
            dve.wait_ge(consts, 8)
            dve.wait_ge(x_in, 16)

            def statistics(b, p):
                after(dve, rstd_ready, b - 1)
                for t in range(IT):
                    ins = nc.vector.bn_stats(stats[:, p, t, :], tokens(X, b, t))
                ins.then_inc(bn_raw, 1)
                dve.wait_ge(bn_raw, b + 1)
                dve.wait_ge(consts, 8)
                for t in range(IT):
                    ins = nc.vector.bn_aggr(mv[:, p, t, :], stats[:, p, t, :])
                ins.then_inc(bn_mean, 1)
                dve.wait_ge(bn_mean, b + 1)
                nc.vector.tensor_scalar(veps[:, p, :], mv[:, p, :, 1], EPS, None, ALU.add).then_inc(var_ready, 1)

            def normalize(b, p):
                dve.wait_ge(rstd_ready, b + 1)
                after(dve, proj_full, 5 * (b - 2) + 1)
                for t in range(IT):
                    ins = nc.vector.tensor_scalar(xn[:, p, t, :], tokens(X, b, t), mv[:, p, t, 0:1],
                                                  rstd[:, p, t:t + 1], ALU.subtract, ALU.mult)
                ins.then_inc(xn_ready, 1)

            def stack(b, p, c):
                n = 4 * b + c
                dve.wait_ge(proj_read, 5 * b + c + 2)
                after(dve, stack_ready, n - 1)
                nc.vector.tensor_copy(high[:, c % 2], full[:, c]).then_inc(high_ready, 1)
                dve.wait_ge(high_ready, n + 1)
                to = (qst if c < 2 else kst)[:, p, 2 * (c % 2):2 * (c % 2) + 2, :]
                if c < 2:
                    after(dve, sc_full, 12 * (b - 1))
                else:
                    after(dve, kmask_in, 64 * (b - 1))
                nc.vector.scalar_tensor_tensor(
                    to, high[:, c % 2].bitcast(F32), lo[:, c // 2:c // 2 + 1], full[:, c],
                    ALU.mult, ALU.add).then_inc(stack_ready, 1)

            def values(b, p):
                dve.wait_ge(v_full, b + 1)
                after(dve, pv_done, 4 * (b - 1))
                for t in range(IT):
                    ins = nc.vector.tensor_tensor(
                        vaug[:, p, t, :, 0:DH], outp[:, t * P:t * P + P].rearrange("p (h e) -> p h e", e=DH),
                        bv[:].rearrange("p (h e) -> p h e", e=DH), ALU.add)
                ins.then_inc(v_read, 1)

            def scores(b, p, g):
                u = 4 * b + g
                after(dve, tm_ready, 2 * (u - 1))
                dve.wait_ge(tr_in[p][g], 16 * (b - p) + 32)
                for f in range(3):
                    dve.wait_ge(sc_full, 3 * u + f + 1)
                    dve.wait_ge(consts, 8)
                    src = scb[(g + f) % 2]
                    for k in range(HH if f == 0 else 2):
                        hh = k if f == 0 else 2 * (f - 1) + k
                        n = P if f == 0 else S
                        c = slice(0, P) if f == 0 else slice(P, P + S)
                        ins = nc.vector.tensor_tensor_reduce(
                            out=T[:, g % 2, hh, c], in0=src[:, k * n:k * n + n], in1=tr[:, p, g, hh, c],
                            scale=1.0, scalar=LOWEST, op0=ALU.add, op1=ALU.max,
                            accum_out=rowmax[:, g % 2, min(f, 1), hh:hh + 1])
                    ins.then_inc(t_ready, 1)

            def output(b, p):
                for t in range(IT):
                    dve.wait_ge(o_full, IT * b + t + 1)
                    o = outp[:].rearrange("p (h e) -> p h e", e=QUAD)
                    after(dve, x_new, b)
                    nc.vector.reciprocal(rden[:, t, :], o[:, :, DH]).then_inc(rden_ready, 1)
                    dve.wait_ge(rden_ready, IT * b + t + 1)
                    nc.vector.tensor_tensor(att[:, t, :].rearrange("p (h e) -> p h e", e=DH), o[:, :, 0:DH],
                                            rden[:, t, :].unsqueeze(2).to_broadcast([P, H, DH]),
                                            ALU.mult).then_inc(att_ready, 1)
                dve.wait_ge(att_ready, IT * b + IT)
                nc.vector.tensor_tensor(tokens(X, b, 0, IT), tokens(X, b, 0, IT),
                                        att[:].rearrange("p t d -> p (t d)"), ALU.add).then_inc(x_new, 1)

            def first(b, p):
                statistics(b, p)
                normalize(b, p)
                for c in range(4):
                    stack(b, p, c)
                values(b, p)

            def both(b, p):
                n = b + 1, 1 - p
                statistics(*n)
                scores(b, p, 0)
                normalize(*n)
                stack(*n, 0)
                scores(b, p, 1)
                stack(*n, 1)
                stack(*n, 2)
                values(*n)
                scores(b, p, 2)
                stack(*n, 3)
                scores(b, p, 3)
                output(b, p)

            def last(b, p):
                for g in range(G):
                    scores(b, p, g)
                output(b, p)

            every_batch(dve, first, both, last)

        @block.scalar
        def _(act):
            act.wait_ge(weights, 16 * 9)

            def xT(b, p):
                act.wait_ge(proj_full, 5 * b + 1)
                after(act, proj_full, 5 * (b - 2) + 3)
                nc.scalar.copy(xnT[:, p, :], proj[:, 0:S]).then_inc(proj_read, 1)

            def chunk(b, c):
                act.wait_ge(proj_full, 5 * b + c + 2)
                after(act, stack_ready, 4 * (b - 1) + c + 1)
                for j in range(2):
                    g = 2 * (c % 2) + j
                    ins = nc.scalar.activation(full[:, c, j, :], proj[:, j * S:j * S + S], ACT.Identity,
                                               bias=(bqR if c < 2 else bkR)[:, g:g + 1])
                ins.then_inc(proj_read, 1)

            def relative(b, g):
                for f in range(3):
                    t = min(f, 1)
                    n = (2 * g + t) % 4
                    act.wait_ge(qe_full, 12 * b + 3 * g + f + 1)
                    after(act, qe_out[n], 16 * (2 * b + g // 2))
                    if isinstance(b, int) and b == 0 and g == 0:
                        act.wait_ge(consts, 2)
                    src = qeb[(g + f) % 2][:].rearrange("p (h l) -> p h l", l=P if f == 0 else S)
                    to = qe[:, n, :, P:S] if f == 0 else qe[:, n, 2 * (f - 1):2 * f, :]
                    nc.scalar.copy(to, src).then_inc(qe_read, 1)

            def exps(b, g):
                u = 4 * b + g
                after(act, pv_done, u - 1)
                for f in range(3):
                    act.wait_ge(tt_full, 3 * u + f + 1)
                    to = PT[:, g % 2, 0, :, 0:P] if f == 0 else PT[:, g % 2, f - 1, :, P:S]
                    nc.scalar.activation(to, ttb[(g + f) % 2][:].rearrange("p (h i) -> p h i", i=P), ACT.Exp,
                                         scale=SCALE).then_inc(pt_ready, 1)

            def oT(b, k):
                act.wait_ge(pv_done, 4 * b + 2 * k + 2)
                after(act, o_full, IT * b)
                nc.scalar.copy(OT[:, 2 * k:2 * k + 2, :], outp[:].rearrange("p (g i) -> p g i", i=S)
                               ).then_inc(ot_ready, 1)

            def first(b, p):
                xT(b, p)
                for c in range(4):
                    chunk(b, c)
                for g in range(G):
                    relative(b, g)

            def both(b, p):
                n = b + 1
                xT(n, 1 - p)
                chunk(n, 0)
                chunk(n, 1)
                chunk(n, 2)
                exps(b, 0)
                chunk(n, 3)
                relative(n, 0)
                exps(b, 1)
                relative(n, 1)
                relative(n, 2)
                exps(b, 2)
                oT(b, 0)
                relative(n, 3)
                exps(b, 3)
                oT(b, 1)

            def last(b, p):
                for g in range(G):
                    exps(b, g)
                    if g >= 2:
                        oT(b, g - 2)

            every_batch(act, first, both, last)

        @block.tensor
        def _(pe):
            pe.wait_ge(weights, 16 * 9)
            pe.wait_ge(consts, 2)

            def xT(b, p):
                pe.wait_ge(xn_ready, b + 1)
                after(pe, proj_read, 5 * b)
                for t in range(IT):
                    ins = nc.tensor.transpose(proj[:, t * P:t * P + P], xn[:, p, t, :], ident[:])
                ins.then_inc(proj_full, 1)

            def chunk(b, p, c):
                pe.wait_ge(proj_read, 5 * b + c + 1)
                if c >= 2:
                    pe.wait_ge(ctx_in[p], 8 * (b - p) + 16)
                for j in range(2):
                    g = 2 * (c % 2) + j
                    w, x = (WqR, xnT) if c < 2 else (WkR, ctxT)
                    ins = nc.tensor.matmul(proj[:, j * S:j * S + S], w[:, g, :], x[:, p, :], start=True, stop=True)
                ins.then_inc(proj_full, 1)

            def values(b, p):
                pe.wait_ge(ctx_in[p], 8 * (b - p) + 16)
                after(pe, v_read, b)
                after(pe, att_ready, IT * (b - 1))
                for t in range(IT):
                    ins = nc.tensor.matmul(outp[:, t * P:t * P + P], ctxT[:, p, t * P:t * P + P], WvT[:],
                                           start=True, stop=True)
                ins.then_inc(v_full, 1)

            def relative(b, p, g):
                pe.wait_ge(stack_ready, 4 * b + g // 2 + 1)
                for f in range(3):
                    n = 12 * b + 3 * g + f
                    after(pe, qe_read, n - 1)
                    t = min(f, 1)
                    er = ErM[:, :, P:S] if f == 0 else ErM[:, 2 * (f - 1):2 * f, :]
                    nc.tensor.matmul(qeb[(g + f) % 2][:], qst[:, p, g, t * P:t * P + P], er,
                                     start=True, stop=True).then_inc(qe_full, 1)

            def scores(b, p, g):
                pe.wait_ge(kmask_in, 64 * (b + 1))
                for f in range(3):
                    n = 12 * b + 3 * g + f
                    after(pe, t_ready, n - 1)
                    t = min(f, 1)
                    k = kmask[:, p, :, g, 0:P] if f == 0 else kmask[:, p, 2 * (f - 1):2 * f, g, :]
                    nc.tensor.matmul(scb[(g + f) % 2][:], qst[:, p, g, t * P:t * P + P], k,
                                     start=True, stop=True).then_inc(sc_full, 1)

            def transposed(b, p, g):
                u = 4 * b + g
                for f in range(3):
                    pe.wait_ge(tm_ready, 2 * u + 1 + min(f, 1))
                    after(pe, pt_ready, 3 * u + f - 1)
                    for hh in range(HH):
                        ins = nc.tensor.transpose(ttb[(g + f) % 2][:, hh * P:hh * P + P],
                                                  Tm[:, g % 2, hh, f * P:f * P + P], ident[:])
                    ins.then_inc(tt_full, 1)

            def weighted(b, p, g):
                u = 4 * b + g
                pe.wait_ge(pt_ready, 3 * u + 3)
                if g == 0:
                    pe.wait_ge(v_read, (b + 2) if not isinstance(b, int) or b + 2 <= B else B)
                    after(pe, att_ready, IT * b)
                if g == 2:
                    pe.wait_ge(ot_ready, 2 * b + 1)
                c = (g % 2) * S
                for jt in range(IT):
                    for hh in range(HH):
                        q = slice(QUAD * hh, QUAD * hh + QUAD)
                        ins = nc.tensor.matmul(outp[q, c + jt * P:c + S], vaug[:, p, jt, HH * g + hh, :],
                                               PT[:, g % 2, jt, hh, jt * P:S], start=(jt == 0), stop=(jt == IT - 1),
                                               skip_group_check=True)
                ins.then_inc(pv_done, 1)

            def output(b):
                for t in range(IT):
                    pe.wait_ge(ot_ready, 2 * b + 2)
                    after(pe, att_ready, IT * b + t)
                    for g in range(G):
                        ins = nc.tensor.transpose(outp[:, g * P:g * P + P], OT[:, g, t * P:t * P + P], ident[:])
                    ins.then_inc(o_full, 1)

            def first(b, p):
                xT(b, p)
                for c in range(4):
                    chunk(b, p, c)
                values(b, p)
                for g in range(G):
                    relative(b, p, g)

            def both(b, p):
                n = b + 1, 1 - p
                scores(b, p, 0)
                xT(*n)
                chunk(*n, 0)
                scores(b, p, 1)
                chunk(*n, 1)
                chunk(*n, 2)
                values(*n)
                transposed(b, p, 0)
                scores(b, p, 2)
                chunk(*n, 3)
                relative(*n, 0)
                transposed(b, p, 1)
                weighted(b, p, 0)
                scores(b, p, 3)
                relative(*n, 1)
                relative(*n, 2)
                transposed(b, p, 2)
                weighted(b, p, 1)
                relative(*n, 3)
                transposed(b, p, 3)
                weighted(b, p, 2)
                weighted(b, p, 3)
                output(b)

            def last(b, p):
                for g in range(G):
                    scores(b, p, g)
                    if g >= 1:
                        transposed(b, p, g - 1)
                    if g >= 2:
                        weighted(b, p, g - 2)
                transposed(b, p, 3)
                weighted(b, p, 2)
                weighted(b, p, 3)
                output(b)

            every_batch(pe, first, both, last)
def attention(nc, X, ident, d):
    with ExitStack() as ctx:
        def sb(name, shape, dt=F32):
            return ctx.enter_context(nc.sbuf_tensor("a1_" + name, shape, dt))

        def sem(name):
            return ctx.enter_context(nc.semaphore("a1_" + name))

        ctxT = sb("ctxT", [P, 2, S])
        WqR = sb("WqR", [P, G, P])
        WkR = sb("WkR", [P, G, P])
        WvT = sb("WvT", [P, D])
        WoT = sb("WoT", [P, D])
        bqR = sb("bqR", [P, G])
        bkR = sb("bkR", [P, G])
        lo = sb("lo", [P, 2])
        bv = sb("bv", [P, D])
        bo = sb("bo", [P, D])
        half = sb("half", [P, IT])
        stats = sb("stats", [P, 2, IT, 6])
        mv = sb("mv", [P, 2, IT, 2])
        veps = sb("veps", [P, 2, IT])
        rstd = sb("rstd", [P, 2, IT])
        xn = sb("xn", [P, 2, IT, D])
        xnT = sb("xnT", [P, 2, S])
        full = sb("full", [P, 4, 2, S])
        high = sb("high", [P, 2, 2, S], F32R)
        qst = sb("qst", [P, 2, G, S], F32R)
        kst = sb("kst", [P, 2, G, S], F32R)
        kmask = sb("kmask", [P, 2, HH, G, S], F32R)
        vaug = sb("vaug", [P, 2, IT, H, QUAD])
        nmax = sb("nmax", [P, 2, IT, P])
        qm = sb("qm", [P, 2, S], F32R)
        PT = sb("PT", [P, 2, HH, IT, S])
        OT = sb("OT", [P, G, S])
        rden = sb("rden", [P, IT, H])
        att = sb("att", [P, IT, D])
        attT = sb("attT", [P, S])
        xo = sb("xo", [P, IT, D])

        bank = [ctx.enter_context(nc.psum_tensor(f"a1_bank{i}", [P, BANK], F32)) for i in range(8)]
        proj, outp, scb, mxb, stb = bank[0], bank[1], bank[2:4], bank[4], bank[5:8]

        weights, consts = sem("weights"), sem("consts")
        ctx_in = [sem("ctx_in0"), sem("ctx_in1")]
        bn_raw, bn_mean, var_ready = sem("bn_raw"), sem("bn_mean"), sem("var_ready")
        half_set, rstd_ready = sem("half_set"), sem("rstd_ready")
        xn_ready, proj_full, proj_read = sem("xn_ready"), sem("proj_full"), sem("proj_read")
        high_ready, stack_ready, kmask_in = sem("high_ready"), sem("stack_ready"), sem("kmask_in")
        v_full, v_read = sem("v_full"), sem("v_read")
        sc_full, max_ready, mx_full, qm_ready = sem("sc_full"), sem("max_ready"), sem("mx_full"), sem("qm_ready")
        st_full, pt_ready, pv_done = sem("st_full"), sem("pt_ready"), sem("pv_done")
        ot_ready, o_full, rden_ready, att_ready = sem("ot_ready"), sem("o_full"), sem("rden_ready"), sem("att_ready")
        attT_full, attT_ready, wo_full, xo_ready, x_new = (
            sem("attT_full"), sem("attT_ready"), sem("wo_full"), sem("xo_ready"), sem("x_new"))

        NS = 4
        NT = HH

        block = ctx.enter_context(nc.Block())

        @block.sync
        def _(sp):
            for dst, src in ((WqR, "WqR1"), (WkR, "WkR1"), (WvT, "WvT1"), (WoT, "WoT1"), (bqR, "bqR1"),
                             (bkR, "bkR1"), (lo, "lo")):
                sp.dma_start(dst[:], d[src]).then_inc(weights, 16)
            for dst, src in ((bv, "bv1"), (bo, "bo1")):
                sp.dma_start(dst[:], d[src].partition_broadcast(P)).then_inc(weights, 16)
            for b in range(2):
                sp.dma_start(ctxT[:, b, :], d["ctxT"][:, b * S:(b + 1) * S]).then_inc(ctx_in[b], 16)
            sp.wait_ge(consts, 3)

            def first(b, p):
                sp.wait_ge(stack_ready, 4 * b + 4)
                after(sp, st_full, 4 * NT * (b - 1))
                for hh in range(HH):
                    q = slice(QUAD * hh, QUAD * hh + QUAD)
                    sp.dma_start(kmask[q, p, hh, :, :].bitcast(F32), kst[q, p, :, :].bitcast(F32)
                                 ).then_inc(kmask_in, 16)

            def both(b, p):
                if b + 2 < B:
                    sp.wait_ge(v_read, b + 1)
                    sp.wait_ge(proj_read, 5 * b + 5)
                    sp.dma_start(ctxT[:, p, :], d["ctxT"][:, bass.ds((b + 2) * S, S)]).then_inc(ctx_in[p], 16)
                first(b + 1, 1 - p)

            every_batch(sp, first, both, lambda b, p: None)

        @block.gpsimd
        def _(pool):
            nc.gpsimd.memset(half[:], -0.5).then_inc(half_set, 1)
            pool.wait_ge(half_set, 1)

            def first(b, p):
                pool.wait_ge(var_ready, b + 1)
                after(pool, xn_ready, b - 1)
                nc.gpsimd.tensor_tensor(rstd[:, p, :], veps[:, p, :], half[:], ALU.pow).then_inc(rstd_ready, 1)

            def outer(b):
                after(pool, x_new, b)
                for t in range(IT):
                    ins = nc.gpsimd.tensor_tensor(xo[:, t, :], tokens(X, b, t), bo[:], ALU.add)
                ins.then_inc(xo_ready, 1)

            for b in range(B):
                first(b, b % 2)
                outer(b)

        @block.vector
        def _(dve):
            dve.wait_ge(weights, 16 * 9)
            for p in range(2):
                nc.vector.memset(kmask[:, p].bitcast(F32), 0.0).then_inc(consts, 1)
            nc.vector.memset(nmax[:], 0.0).then_inc(consts, 1)
            for p in range(2):
                nc.vector.memset(vaug[:, p], 0.0).then_inc(consts, 1)
            dve.wait_ge(consts, 5)
            for p in range(2):
                nc.vector.memset(vaug[:, p, :, :, DH:DH + 1], 1.0).then_inc(consts, 1)
            dve.wait_ge(consts, 7)

            def statistics(b, p):
                after(dve, rstd_ready, b - 1)
                for t in range(IT):
                    ins = nc.vector.bn_stats(stats[:, p, t, :], tokens(X, b, t))
                ins.then_inc(bn_raw, 1)
                dve.wait_ge(bn_raw, b + 1)
                for t in range(IT):
                    ins = nc.vector.bn_aggr(mv[:, p, t, :], stats[:, p, t, :])
                ins.then_inc(bn_mean, 1)
                dve.wait_ge(bn_mean, b + 1)
                nc.vector.tensor_scalar(veps[:, p, :], mv[:, p, :, 1], EPS, None, ALU.add).then_inc(var_ready, 1)

            def normalize(b, p):
                dve.wait_ge(rstd_ready, b + 1)
                after(dve, proj_full, 5 * (b - 2) + 1)
                for t in range(IT):
                    ins = nc.vector.tensor_scalar(xn[:, p, t, :], tokens(X, b, t), mv[:, p, t, 0:1],
                                                  rstd[:, p, t:t + 1], ALU.subtract, ALU.mult)
                ins.then_inc(xn_ready, 1)

            def stack(b, p, c):
                n = 4 * b + c
                dve.wait_ge(proj_read, 5 * b + c + 2)
                after(dve, stack_ready, n - 1)
                nc.vector.tensor_copy(high[:, c % 2], full[:, c]).then_inc(high_ready, 1)
                dve.wait_ge(high_ready, n + 1)
                to = (qst if c < 2 else kst)[:, p, 2 * (c % 2):2 * (c % 2) + 2, :]
                if c < 2:
                    after(dve, qm_ready, 4 * (b - 1))
                else:
                    after(dve, kmask_in, 64 * (b - 1))
                nc.vector.scalar_tensor_tensor(
                    to, high[:, c % 2].bitcast(F32), lo[:, c // 2:c // 2 + 1], full[:, c],
                    ALU.mult, ALU.add).then_inc(stack_ready, 1)

            def values(b, p):
                dve.wait_ge(v_full, b + 1)
                after(dve, pv_done, 4 * (b - 1))
                for t in range(IT):
                    ins = nc.vector.tensor_tensor(
                        vaug[:, p, t, :, 0:DH], outp[:, t * P:t * P + P].rearrange("p (h e) -> p h e", e=DH),
                        bv[:].rearrange("p (h e) -> p h e", e=DH), ALU.add)
                ins.then_inc(v_read, 1)

            def maxima(b, g):
                u = 4 * b + g
                after(dve, mx_full, u - 1)
                for f in range(NS):
                    dve.wait_ge(sc_full, NS * u + f + 1)
                    c = QUAD * 2 * (f % 2) + MAXROW
                    nc.vector.tensor_reduce(nmax[:, g % 2, f // 2, c:c + QUAD + 1:QUAD],
                                            scb[f % 2][:].rearrange("p (h j) -> p h j", j=S), AX.X, ALU.max,
                                            negate=True).then_inc(max_ready, 1)

            def less_max(b, p, g):
                u = 4 * b + g
                dve.wait_ge(mx_full, u + 1)
                after(dve, st_full, NT * (u - 1))
                nc.vector.tensor_tensor(qm[:, g % 2, :], mxb[:, 0:S], qst[:, p, g, :].bitcast(F32),
                                        ALU.add).then_inc(qm_ready, 1)

            def output(b):
                for t in range(IT):
                    dve.wait_ge(o_full, IT * b + t + 1)
                    o = outp[:].rearrange("p (h e) -> p h e", e=QUAD)
                    after(dve, attT_full, b)
                    nc.vector.reciprocal(rden[:, t, :], o[:, :, DH]).then_inc(rden_ready, 1)
                    dve.wait_ge(rden_ready, IT * b + t + 1)
                    nc.vector.tensor_tensor(att[:, t, :].rearrange("p (h e) -> p h e", e=DH), o[:, :, 0:DH],
                                            rden[:, t, :].unsqueeze(2).to_broadcast([P, H, DH]),
                                            ALU.mult).then_inc(att_ready, 1)

            def residual(b):
                dve.wait_ge(wo_full, b + 1)
                dve.wait_ge(xo_ready, b + 1)
                nc.vector.tensor_tensor(tokens(X, b, 0, IT), outp[:, 0:S], xo[:].rearrange("p t e -> p (t e)"),
                                        ALU.add).then_inc(x_new, 1)

            def first(b, p):
                statistics(b, p)
                normalize(b, p)
                for c in range(4):
                    stack(b, p, c)
                values(b, p)

            def both(b, p):
                n = b + 1, 1 - p
                statistics(*n)
                maxima(b, 0)
                normalize(*n)
                maxima(b, 1)
                less_max(b, p, 0)
                stack(*n, 0)
                stack(*n, 1)
                maxima(b, 2)
                less_max(b, p, 1)
                stack(*n, 2)
                values(*n)
                maxima(b, 3)
                less_max(b, p, 2)
                stack(*n, 3)
                less_max(b, p, 3)
                output(b)
                residual(b)

            def last(b, p):
                maxima(b, 0)
                for g in range(1, G):
                    maxima(b, g)
                    less_max(b, p, g - 1)
                less_max(b, p, 3)
                output(b)
                residual(b)

            every_batch(dve, first, both, last)

        @block.scalar
        def _(act):
            act.wait_ge(weights, 16 * 9)

            def xT(b, p):
                act.wait_ge(proj_full, 5 * b + 1)
                after(act, proj_full, 5 * (b - 2) + 3)
                nc.scalar.copy(xnT[:, p, :], proj[:, 0:S]).then_inc(proj_read, 1)

            def chunk(b, c):
                act.wait_ge(proj_full, 5 * b + c + 2)
                after(act, stack_ready, 4 * (b - 1) + c + 1)
                for j in range(2):
                    g = 2 * (c % 2) + j
                    ins = nc.scalar.activation(full[:, c, j, :], proj[:, j * S:j * S + S], ACT.Identity,
                                               bias=(bqR if c < 2 else bkR)[:, g:g + 1])
                ins.then_inc(proj_read, 1)

            def exps(b, g):
                u = 4 * b + g
                after(act, pv_done, u - 1)
                for f in range(NT):
                    n = NT * u + f
                    act.wait_ge(st_full, n + 1)
                    nc.scalar.activation(PT[:, g % 2, f].rearrange("p j i -> p (j i)"), stb[n % 3][:], ACT.Exp,
                                         scale=SCALE).then_inc(pt_ready, 1)

            def oT(b, k):
                act.wait_ge(pv_done, 4 * b + 2 * k + 2)
                after(act, o_full, IT * b)
                nc.scalar.copy(OT[:, 2 * k:2 * k + 2, :], outp[:].rearrange("p (g i) -> p g i", i=S)
                               ).then_inc(ot_ready, 1)

            def attended(b):
                act.wait_ge(attT_full, b + 1)
                after(act, wo_full, b)
                nc.scalar.copy(attT[:], outp[:, 0:S]).then_inc(attT_ready, 1)

            def first(b, p):
                xT(b, p)
                for c in range(4):
                    chunk(b, c)

            def both(b, p):
                n = b + 1
                xT(n, 1 - p)
                chunk(n, 0)
                exps(b, 0)
                chunk(n, 1)
                chunk(n, 2)
                exps(b, 1)
                chunk(n, 3)
                exps(b, 2)
                oT(b, 0)
                exps(b, 3)
                oT(b, 1)
                attended(b)

            def last(b, p):
                exps(b, 0)
                exps(b, 1)
                exps(b, 2)
                oT(b, 0)
                exps(b, 3)
                oT(b, 1)
                attended(b)

            every_batch(act, first, both, last)

        @block.tensor
        def _(pe):
            pe.wait_ge(weights, 16 * 9)

            def xT(b, p):
                pe.wait_ge(xn_ready, b + 1)
                after(pe, proj_read, 5 * b)
                for t in range(IT):
                    ins = nc.tensor.transpose(proj[:, t * P:t * P + P], xn[:, p, t, :], ident[:])
                ins.then_inc(proj_full, 1)

            def chunk(b, p, c):
                pe.wait_ge(proj_read, 5 * b + c + 1)
                if c >= 2:
                    pe.wait_ge(ctx_in[p], 8 * (b - p) + 16)
                for j in range(2):
                    g = 2 * (c % 2) + j
                    w, x = (WqR, xnT) if c < 2 else (WkR, ctxT)
                    ins = nc.tensor.matmul(proj[:, j * S:j * S + S], w[:, g, :], x[:, p, :], start=True, stop=True)
                ins.then_inc(proj_full, 1)

            def values(b, p):
                pe.wait_ge(ctx_in[p], 8 * (b - p) + 16)
                after(pe, v_read, b)
                after(pe, x_new, b - 1)
                for t in range(IT):
                    ins = nc.tensor.matmul(outp[:, t * P:t * P + P], ctxT[:, p, t * P:t * P + P], WvT[:],
                                           start=True, stop=True)
                ins.then_inc(v_full, 1)

            def scores(b, p, g):
                if g == 0:
                    pe.wait_ge(kmask_in, 64 * (b + 1))
                for f in range(NS):
                    n = NS * (4 * b + g) + f
                    after(pe, max_ready, n - 1)
                    t, k = f // 2, f % 2
                    nc.tensor.matmul(scb[f % 2][:], qst[:, p, g, t * P:t * P + P], kmask[:, p, 2 * k:2 * k + 2, g, :],
                                     start=True, stop=True).then_inc(sc_full, 1)

            def maxima(b, g):
                u = 4 * b + g
                pe.wait_ge(max_ready, NS * u + NS)
                after(pe, qm_ready, u)
                for t in range(IT):
                    ins = nc.tensor.transpose(mxb[:, t * P:t * P + P], nmax[:, g % 2, t, :], ident[:])
                ins.then_inc(mx_full, 1)

            def by_key(b, p, g):
                u = 4 * b + g
                pe.wait_ge(qm_ready, u + 1)
                for f in range(NT):
                    n = NT * u + f
                    after(pe, pt_ready, n - 2)
                    for jt in range(IT):
                        ins = nc.tensor.matmul(stb[n % 3][:, jt * S:jt * S + S], kmask[:, p, f, g, jt * P:jt * P + P],
                                               qm[:, g % 2, :], start=True, stop=True)
                    ins.then_inc(st_full, 1)

            def weighted(b, p, g):
                u = 4 * b + g
                pe.wait_ge(pt_ready, NT * (u + 1))
                if g == 0:
                    pe.wait_ge(v_read, min(b + 2, B))
                    after(pe, x_new, b)
                if g == 2:
                    pe.wait_ge(ot_ready, 2 * b + 1)
                c = (g % 2) * S
                for jt in range(IT):
                    for hh in range(HH):
                        q = slice(QUAD * hh, QUAD * hh + QUAD)
                        ins = nc.tensor.matmul(outp[q, c:c + S], vaug[:, p, jt, HH * g + hh, :],
                                               PT[:, g % 2, hh, jt, :], start=(jt == 0), stop=(jt == IT - 1),
                                               skip_group_check=True)
                ins.then_inc(pv_done, 1)

            def output(b):
                for t in range(IT):
                    pe.wait_ge(ot_ready, 2 * b + 2)
                    after(pe, att_ready, IT * b + t)
                    for g in range(G):
                        ins = nc.tensor.transpose(outp[:, g * P:g * P + P], OT[:, g, t * P:t * P + P], ident[:])
                    ins.then_inc(o_full, 1)
                pe.wait_ge(att_ready, IT * b + IT)
                for t in range(IT):
                    ins = nc.tensor.transpose(outp[:, t * P:t * P + P], att[:, t, :], ident[:])
                ins.then_inc(attT_full, 1)
                pe.wait_ge(attT_ready, b + 1)
                for t in range(IT):
                    ins = nc.tensor.matmul(outp[:, t * P:t * P + P], attT[:, t * P:t * P + P], WoT[:],
                                           start=True, stop=True)
                ins.then_inc(wo_full, 1)

            def first(b, p):
                xT(b, p)
                for c in range(4):
                    chunk(b, p, c)
                values(b, p)

            def both(b, p):
                n = b + 1, 1 - p
                scores(b, p, 0)
                xT(*n)
                chunk(*n, 0)
                maxima(b, 0)
                scores(b, p, 1)
                by_key(b, p, 0)
                chunk(*n, 1)
                chunk(*n, 2)
                maxima(b, 1)
                scores(b, p, 2)
                by_key(b, p, 1)
                values(*n)
                chunk(*n, 3)
                weighted(b, p, 0)
                maxima(b, 2)
                scores(b, p, 3)
                by_key(b, p, 2)
                weighted(b, p, 1)
                maxima(b, 3)
                by_key(b, p, 3)
                weighted(b, p, 2)
                weighted(b, p, 3)
                output(b)

            def last(b, p):
                scores(b, p, 0)
                maxima(b, 0)
                for g in range(1, G):
                    scores(b, p, g)
                    by_key(b, p, g - 1)
                    if g >= 2:
                        weighted(b, p, g - 2)
                    maxima(b, g)
                by_key(b, p, 3)
                weighted(b, p, 2)
                weighted(b, p, 3)
                output(b)

            every_batch(pe, first, both, last)



def experts(nc, X, ident, d, tag, E, blocks, shared, n_scaled):
    with ExitStack() as ctx:
        def sb(name, shape, dt=F32):
            return ctx.enter_context(nc.sbuf_tensor(tag + "s_" + name, shape, dt))

        def sem(name):
            return ctx.enter_context(nc.semaphore(tag + name))

        pairs = E // 2
        per_pair = 3 if n_scaled else 1
        NHG, NHID = 3, 4
        PAD = 6

        Wr = sb("Wr", [P, E])
        Wg = sb("Wg", [P, blocks, P])
        Wu = sb("Wu", [P, blocks, P])
        Wd = sb("Wd", [P, blocks, P])
        selF = sb("selF", [2 * E, pairs, 2 if n_scaled else 1, P])
        sel = sb("sel", [2 * E, pairs, 2 if n_scaled else 1, P], F32R)
        half = sb("half", [P, IT])
        stats = sb("stats", [P, 2, IT, 6])
        mv = sb("mv", [P, 2, IT, 2])
        veps = sb("veps", [P, 2, IT])
        rstd = sb("rstd", [P, 2, IT])
        xn = sb("xn", [P, 2, IT, D])
        xnT = sb("xnT", [P, 2, S])
        lg = sb("lg", [P, IT, E + PAD])
        top = sb("top", [P, IT, 8])
        match = sb("match", [P, IT, 8])
        rep = sb("rep", [P, IT, E + PAD])
        chosen = sb("chosen", [P, IT, E])
        diff = sb("diff", [P, IT])
        th = sb("th", [P, IT])
        w2 = sb("w2", [P, IT])
        ez = sb("ez", [P, IT, E])
        cw = sb("cw", [P, IT, E])
        split = sb("split", [P, IT, 2 * E], F32R)
        combT = sb("combT", [2 * E, 2, S], F32R)
        xs = sb("xs", [P, 4, S])
        tanh = sb("tanh", [P, NHG, S])
        gated = sb("gated", [P, 2, S])
        scaled = sb("scaled", [P, 2, S])
        hid = sb("hid", [P, NHID, S])
        outT = sb("outT", [P, S])

        bank = [ctx.enter_context(nc.psum_tensor(f"{tag}bank{i}", [P, BANK], F32)) for i in range(8)]
        hg, bc, acc, misc, route = bank[0:3], bank[3:5], bank[5], bank[6], bank[7]

        weights, consts = sem("weights"), sem("consts")
        bn_raw, bn_mean, var_ready = sem("bn_raw"), sem("bn_mean"), sem("var_ready")
        half_set, rstd_ready = sem("half_set"), sem("rstd_ready")
        xn_ready, xT_full, xT_read = sem("xn_ready"), sem("xT_full"), sem("xT_read")
        logits_full, logits_read = sem("logits_full"), sem("logits_read")
        gate_in, gate_out = sem("gate_in"), sem("gate_out")
        chain, split_ready = sem("chain"), sem("split_ready")
        combT_full, combT_read = sem("combT_full"), sem("combT_read")
        bc_full, bc_read = sem("bc_full"), sem("bc_read")
        hg_full, tanh_ready, gated_ready = sem("hg_full"), sem("tanh_ready"), sem("gated_ready")
        scaled_ready, hid_ready, hid_used = sem("scaled_ready"), sem("hid_ready"), sem("hid_used")
        outT_read, out_full, x_new = sem("outT_read"), sem("out_full"), sem("x_new")

        block = ctx.enter_context(nc.Block())

        def scaled_block(i):
            return i < blocks - shared

        @block.sync
        def _(sp):
            for dst, name in ((Wr, "Wr"), (selF, "sel"), (Wg, "Wg"), (Wu, "Wu"), (Wd, "Wd")):
                sp.dma_start(dst[:], d[tag + name]).then_inc(weights, 16)
            sp.wait_ge(weights, 16 * 5)

        @block.gpsimd
        def _(pool):
            nc.gpsimd.memset(half[:], -0.5).then_inc(half_set, 1)
            pool.wait_ge(half_set, 1)
            for b in range(B):
                pool.wait_ge(var_ready, b + 1)
                after(pool, xn_ready, b - 1)
                nc.gpsimd.tensor_tensor(rstd[:, b % 2, :], veps[:, b % 2, :], half[:], ALU.pow).then_inc(rstd_ready, 1)

        @block.vector
        def _(dve):
            nc.vector.memset(lg[:], LOWEST).then_inc(consts, 1)
            nc.vector.memset(match[:], LOWEST).then_inc(consts, 1)
            dve.wait_ge(weights, 16 * 5)
            nc.vector.tensor_copy(sel[:], selF[:]).then_inc(consts, 1)
            dve.wait_ge(consts, 3)
            links = [0]

            def link(ins):
                links[0] += 1
                ins.then_inc(chain, 1)
                dve.wait_ge(chain, links[0])

            def statistics(b, p):
                after(dve, rstd_ready, b - 1)
                for t in range(IT):
                    ins = nc.vector.bn_stats(stats[:, p, t, :], tokens(X, b, t))
                ins.then_inc(bn_raw, 1)
                dve.wait_ge(bn_raw, b + 1)
                for t in range(IT):
                    ins = nc.vector.bn_aggr(mv[:, p, t, :], stats[:, p, t, :])
                ins.then_inc(bn_mean, 1)
                dve.wait_ge(bn_mean, b + 1)
                nc.vector.tensor_scalar(veps[:, p, :], mv[:, p, :, 1], EPS, None, ALU.add).then_inc(var_ready, 1)

            def normalize(b, p):
                dve.wait_ge(rstd_ready, b + 1)
                after(dve, xT_full, b - 1)
                for t in range(IT):
                    ins = nc.vector.tensor_scalar(xn[:, p, t, :], tokens(X, b, t), mv[:, p, t, 0:1],
                                                  rstd[:, p, t:t + 1], ALU.subtract, ALU.mult)
                ins.then_inc(xn_ready, 1)

            def choose():
                for t in range(IT):
                    ins = nc.vector.max(top[:, t, :], lg[:, t, 0:E])
                link(ins)
                link(nc.vector.tensor_copy(match[:, :, 0:2], top[:, :, 0:2]))
                for t in range(IT):
                    ins = nc.vector.match_replace(rep[:, t, :], match[:, t, :], lg[:, t, :], -LOWEST)
                link(ins)
                link(nc.vector.tensor_tensor(chosen[:], rep[:, :, 0:E], lg[:, :, 0:E], ALU.not_equal))

            def wide(x):
                return x.unsqueeze(2).to_broadcast([P, IT, E])

            def route_start(b, p):
                dve.wait_ge(logits_full, b + 1)
                z = route[:, 0:IT * E].rearrange("p (t e) -> p t e", e=E)
                if n_scaled:
                    ins = nc.vector.tensor_copy(lg[:, :, 0:E], z)
                    ins.then_inc(logits_read, 1)
                    dve.wait_ge(logits_read, b + 1)
                    choose()
                    nc.vector.tensor_tensor(diff[:], top[:, :, 0], top[:, :, 1], ALU.subtract).then_inc(gate_in, 1)

            def route_end(b, p):
                dve.wait_ge(gate_out, b + 1)
                if n_scaled:
                    link(nc.vector.tensor_scalar(w2[:], th[:], -0.25, 0.25, ALU.mult, ALU.add))
                    link(nc.vector.tensor_tensor(cw[:], lg[:, :, 0:E], wide(top[:, :, 0]), ALU.is_ge))
                    link(nc.vector.tensor_tensor(cw[:], cw[:], wide(th[:]), ALU.mult))
                    link(nc.vector.tensor_scalar(cw[:], cw[:], 0.5, None, ALU.mult))
                    link(nc.vector.tensor_tensor(cw[:], cw[:], wide(w2[:]), ALU.add))
                    link(nc.vector.tensor_tensor(cw[:], cw[:], chosen[:], ALU.mult))
                else:
                    link(nc.vector.tensor_scalar(ez[:], ez[:], 1.0, None, ALU.add))
                    link(nc.vector.reciprocal(lg[:, :, 0:E], ez[:]))
                    choose()
                    link(nc.vector.tensor_tensor(diff[:], top[:, :, 0], top[:, :, 1], ALU.add))
                    link(nc.vector.tensor_scalar(diff[:], diff[:], 1e-20, None, ALU.add))
                    link(nc.vector.reciprocal(w2[:], diff[:]))
                    link(nc.vector.tensor_tensor(cw[:], lg[:, :, 0:E], chosen[:], ALU.mult))
                    link(nc.vector.tensor_tensor(cw[:], cw[:], wide(w2[:]), ALU.mult))
                    link(nc.vector.tensor_scalar(cw[:], cw[:], 0.5 * 2.5, None, ALU.mult))
                after(dve, combT_full, b)
                link(nc.vector.tensor_copy(split[:, :, 0:E], cw[:]))
                nc.vector.tensor_tensor(split[:, :, E:2 * E], cw[:], split[:, :, 0:E].bitcast(F32),
                                        ALU.subtract).then_inc(split_ready, 1)

            def scale_input(b, p, q):
                n = pairs * b + q
                dve.wait_ge(bc_full, n + 1)
                after(dve, hg_full, blocks * b + per_pair * (q - 1))
                nc.vector.tensor_tensor(
                    xs[:, 2 * (q % 2):2 * (q % 2) + 2, :], bc[n % 2][:].rearrange("p (e s) -> p e s", s=S),
                    xnT[:, p, :].unsqueeze(1).to_broadcast([P, 2, S]), ALU.mult).then_inc(bc_read, 1)

            def hidden(b, i):
                n = blocks * b + i
                ps = hg[n % NHG]
                dve.wait_ge(tanh_ready, n + 1)
                after(dve, hid_ready, n - 1)
                nc.vector.scalar_tensor_tensor(gated[:, n % 2, :], tanh[:, n % NHG, :], 1.0, ps[:, 0:S],
                                               ALU.add, ALU.mult).then_inc(gated_ready, 1)
                dve.wait_ge(gated_ready, n + 1)
                after(dve, hid_used, n - NHID + 1)
                if n_scaled or not scaled_block(i):
                    nc.vector.scalar_tensor_tensor(hid[:, n % NHID, :], gated[:, n % 2, :], 1.0 if n_scaled else 0.5,
                                                   ps[:, S:2 * S], ALU.mult, ALU.mult).then_inc(hid_ready, 1)
                else:
                    m = (blocks - shared) * b + i
                    nc.vector.tensor_tensor(scaled[:, m % 2, :], gated[:, n % 2, :], ps[:, S:2 * S],
                                            ALU.mult).then_inc(scaled_ready, 1)
                    dve.wait_ge(scaled_ready, m + 1)
                    dve.wait_ge(bc_full, (pairs * b + i) // 2 + 1)
                    nc.vector.tensor_tensor(hid[:, n % NHID, :], scaled[:, m % 2, :],
                                            bc[m // 2 % 2][:, (m % 2) * S:(m % 2) * S + S],
                                            ALU.mult).then_inc(hid_ready, 1)

            def output(b):
                dve.wait_ge(out_full, b + 1)
                nc.vector.tensor_tensor(tokens(X, b, 0, IT), tokens(X, b, 0, IT), misc[:, 0:S],
                                        ALU.add).then_inc(x_new, 1)

            statistics(0, 0)
            normalize(0, 0)
            route_start(0, 0)
            route_end(0, 0)
            for b in range(B):
                p = b % 2
                if n_scaled:
                    scale_input(b, p, 0)
                for i in range(blocks):
                    if n_scaled and i % per_pair == 0 and i // per_pair + 1 < pairs:
                        scale_input(b, p, i // per_pair + 1)
                    hidden(b, i)
                    if b + 1 < B:
                        if i == 0:
                            statistics(b + 1, 1 - p)
                            normalize(b + 1, 1 - p)
                        if i == 3:
                            route_start(b + 1, 1 - p)
                        if i == 5:
                            route_end(b + 1, 1 - p)
                    if i == 1 and b >= 1:
                        output(b - 1)
            output(B - 1)

        @block.scalar
        def _(act):
            def xT(b, p):
                act.wait_ge(xT_full, b + 1)
                if b >= 2:
                    act.wait_ge(hg_full, blocks * (b - 1))
                    if n_scaled:
                        act.wait_ge(bc_read, pairs * (b - 1))
                nc.scalar.copy(xnT[:, p, :], misc[:, S:2 * S]).then_inc(xT_read, 1)

            def gate(b):
                if n_scaled:
                    act.wait_ge(gate_in, b + 1)
                    nc.scalar.activation(th[:], diff[:], ACT.Tanh, scale=0.5).then_inc(gate_out, 1)
                else:
                    act.wait_ge(logits_full, b + 1)
                    after(act, split_ready, b)
                    nc.scalar.activation(ez[:].rearrange("p t e -> p (t e)"), route[:, 0:IT * E], ACT.Exp,
                                         scale=-1.0).then_inc(gate_out, 1)

            def comb(b, p):
                act.wait_ge(combT_full, b + 1)
                if b >= 2:
                    act.wait_ge(bc_full, (pairs if n_scaled else pairs // 2) * (b - 1))
                nc.scalar.copy(combT[:, p, :], route[0:2 * E, S:2 * S]).then_inc(combT_read, 1)

            def tanhs(b, i):
                n = blocks * b + i
                act.wait_ge(hg_full, n + 1)
                after(act, gated_ready, n - NHG + 1)
                nc.scalar.activation(tanh[:, n % NHG, :], hg[n % NHG][:, 0:S], ACT.Tanh, scale=0.5).then_inc(tanh_ready, 1)

            def out(b):
                act.wait_ge(hid_used, blocks * (b + 1))
                after(act, out_full, b)
                nc.scalar.copy(outT[:], acc[:, 0:S]).then_inc(outT_read, 1)

            xT(0, 0)
            gate(0)
            comb(0, 0)
            for b in range(B):
                for i in range(blocks):
                    tanhs(b, i)
                    if i == 1 and b >= 1:
                        out(b - 1)
                    if b + 1 < B:
                        if i == 2:
                            xT(b + 1, 1 - b % 2)
                        if i == 5:
                            gate(b + 1)
                        if i == 7:
                            comb(b + 1, 1 - b % 2)
            out(B - 1)

        @block.tensor
        def _(pe):
            pe.wait_ge(weights, 16 * 5)
            pe.wait_ge(consts, 3)

            def xT(b, p):
                pe.wait_ge(xn_ready, b + 1)
                after(pe, xT_read, b)
                after(pe, x_new, b - 1)
                for t in range(IT):
                    ins = nc.tensor.transpose(misc[:, S + t * P:S + t * P + P], xn[:, p, t, :], ident[:])
                ins.then_inc(xT_full, 1)

            def logits(b, p):
                pe.wait_ge(xT_read, b + 1)
                after(pe, combT_read, b)
                for t in range(IT):
                    ins = nc.tensor.matmul(route[:, t * E:t * E + E], xnT[:, p, t * P:t * P + P], Wr[:],
                                           start=True, stop=True)
                ins.then_inc(logits_full, 1)

            def comb(b, p):
                pe.wait_ge(split_ready, b + 1)
                for t in range(IT):
                    ins = nc.tensor.transpose(route[0:2 * E, S + t * P:S + t * P + P], split[:, t, :].bitcast(F32),
                                              ident[:])
                ins.then_inc(combT_full, 1)

            def spread(b, p, q):
                n = (pairs if n_scaled else pairs // 2) * b + q
                pe.wait_ge(combT_read, b + 1)
                if n_scaled:
                    after(pe, bc_read, n - 1)
                else:
                    after(pe, hid_ready, hid_count(n - 2))
                for j in range(2):
                    w = sel[:, q, j, :] if n_scaled else sel[:, 2 * q + j, 0, :]
                    ins = nc.tensor.matmul(bc[n % 2][:, j * S:j * S + S], w, combT[:, p, :], start=True, stop=True)
                ins.then_inc(bc_full, 1)

            def hid_count(n):
                if n < 0:
                    return 0
                return blocks * (n // (pairs // 2)) + 2 * (n % (pairs // 2)) + 2

            def up(b, p, i):
                n = blocks * b + i
                ps = hg[n % NHG]
                after(pe, hid_ready if n_scaled else hid_ready, n - NHG + 1)
                nc.tensor.matmul(ps[:, 0:S], Wg[:, i, :], xnT[:, p, :], start=True, stop=True)
                if not n_scaled:
                    nc.tensor.matmul(ps[:, S:2 * S], Wu[:, i, :], xnT[:, p, :], start=True, stop=True).then_inc(hg_full, 1)
                    return
                q, part = i // per_pair, i % per_pair
                pe.wait_ge(bc_read, pairs * b + q + 1)
                s0 = 2 * (q % 2)
                if part < 2:
                    nc.tensor.matmul(ps[:, S:2 * S], Wu[:, i, :], xs[:, s0 + part, :], start=True,
                                     stop=True).then_inc(hg_full, 1)
                else:
                    nc.tensor.matmul(ps[0:64, S:2 * S], Wu[:, i, 0:64], xs[:, s0, :], start=True, stop=True)
                    nc.tensor.matmul(ps[64:P, S:2 * S], Wu[:, i, 64:P], xs[:, s0 + 1, :], start=True,
                                     stop=True).then_inc(hg_full, 1)

            def down(b, i):
                n = blocks * b + i
                pe.wait_ge(hid_ready, n + 1)
                if i == 0:
                    after(pe, outT_read, b)
                nc.tensor.matmul(acc[:, 0:S], Wd[:, i, :], hid[:, n % NHID, :], start=(i == 0),
                                 stop=(i == blocks - 1)).then_inc(hid_used, 1)

            def out(b):
                pe.wait_ge(outT_read, b + 1)
                after(pe, x_new, b)
                for t in range(IT):
                    ins = nc.tensor.transpose(misc[:, t * P:t * P + P], outT[:, t * P:t * P + P], ident[:])
                ins.then_inc(out_full, 1)

            xT(0, 0)
            logits(0, 0)
            comb(0, 0)
            LAG = 2
            fills = pairs if n_scaled else pairs // 2
            step = blocks // fills
            for b in range(B):
                p = b % 2
                spread(b, p, 0)
                for i in range(blocks + LAG):
                    if i < blocks:
                        if i % step == 0 and i // step + 1 < fills:
                            spread(b, p, i // step + 1)
                        up(b, p, i)
                    if i >= LAG:
                        down(b, i - LAG)
                    if b + 1 < B:
                        if i == 3:
                            xT(b + 1, 1 - p)
                        if i == 4:
                            logits(b + 1, 1 - p)
                        if i == 8:
                            comb(b + 1, 1 - p)
                    if i == 2 and b >= 1:
                        out(b - 1)
            out(B - 1)


def expert_pairs(w):
    w = w.transpose(1, 0, 2).reshape(D, -1, 2, w.shape[2])
    rest = w[..., P:].reshape(D, w.shape[1], 1, P)
    return np.ascontiguousarray(np.concatenate([w[..., :P], rest], 2).reshape(D, -1, P))


def selectors(E, half_blocks):
    out = np.zeros((2, E, E // 2, 2, P), np.float32)
    for e in range(E):
        out[:, e, e // 2, e % 2] = 1.0
    if half_blocks:
        half = np.zeros((2, E, E // 2, 1, P), np.float32)
        for j in range(2):
            half[:, :, :, 0, j * P // 2:(j + 1) * P // 2] = out[:, :, :, j, 0:P // 2]
        out = half
    return out.reshape((2 * E,) + out.shape[2:])


def quadrants(w):
    w = w.reshape(G, HH, DH, -1)
    out = np.zeros((w.shape[-1], G, HH, QUAD), np.float32)
    for r in range(3):
        out[:, :, :, r * DH:(r + 1) * DH] = w.transpose(3, 0, 1, 2)
    return out.reshape(w.shape[-1], G, P)


def low_rows(r):
    out = np.zeros((HH, QUAD), np.float32)
    out[:, r * DH:(r + 1) * DH] = -1.0
    return out.reshape(P)


def er_quadrants(Er):
    out = np.zeros((HH, QUAD, HH, S), np.float32)
    for hh in range(HH):
        for r in range(3):
            out[hh, r * DH:(r + 1) * DH, hh] = Er.T
    return out.reshape(P, HH, S)


def xattn_ffn_twice_kernel(nc, x, out, **d):
    rel = nc.dram_tensor("relative_scores", [2, H, S, PITCH], F32).ap()
    with ExitStack() as ctx:
        X = ctx.enter_context(nc.sbuf_tensor("X", [P, B * IT * D], F32))
        ident = ctx.enter_context(nc.sbuf_tensor("identity", [P, P], F32))
        stored = ctx.enter_context(nc.semaphore("stored"))
        relative_attention(nc, X, ident, x, d, rel)
        experts(nc, X, ident, d, "m0_", 8, 12, 0, True)
        attention(nc, X, ident, d)
        experts(nc, X, ident, d, "m1_", 16, 9, 1, False)
        block = ctx.enter_context(nc.Block())

        @block.sync
        def _(sp):
            sp.dma_start(out.rearrange("(t p) d -> p t d", p=P),
                         X[:].rearrange("p (t d) -> p t d", d=D)).then_inc(stored, 16)
            sp.wait_ge(stored, 16)


def laid_out(inputs):
    def quad_bias(b):
        return quadrants(b[:, None])[0].T

    def halves(w, ws):
        blocks = np.zeros((D, E1 // 2 + 1, P), np.float32)
        blocks[:, :-1] = w.transpose(1, 0, 2).reshape(D, E1 // 2, P)
        blocks[:, -1, :P // 2] = ws
        return blocks

    i = inputs
    E0, E1 = i["L0_ffn_Wr"].shape[1], i["L1_ffn_gate_w"].shape[0]
    bk1 = quad_bias(i["L1_xattn_bk"]).copy()
    bk1[MAXROW::QUAD] = 1.0
    return dict(
        x=i["x"].reshape(B * S, D), ctxT=i["ctx_1024"].reshape(B * S, D).T,
        ident=np.eye(P, dtype=np.float32), lo=np.stack([low_rows(1), low_rows(2)], 1),
        WqR0=quadrants(i["L0_xattn_Wq"]), bqR0=quad_bias(i["L0_xattn_bq"]),
        WkR0=quadrants(i["L0_xattn_Wk"]), bkR0=quad_bias(i["L0_xattn_bk"]),
        WvT0=i["L0_xattn_Wv"].T, bv0=i["L0_xattn_bv"], ErR=er_quadrants(i["L0_xattn_Er"]),
        m0_Wr=i["L0_ffn_Wr"], m0_sel=selectors(E0, False), m0_Wg=expert_pairs(i["L0_ffn_W1"]),
        m0_Wu=expert_pairs(i["L0_ffn_W3"]),
        m0_Wd=expert_pairs(i["L0_ffn_W2"].transpose(0, 2, 1)).transpose(2, 1, 0),
        WqR1=quadrants(i["L1_xattn_Wq"]), bqR1=quad_bias(i["L1_xattn_bq"]),
        WkR1=quadrants(i["L1_xattn_Wk"]), bkR1=bk1,
        WvT1=i["L1_xattn_Wv"].T, bv1=i["L1_xattn_bv"], WoT1=i["L1_xattn_Wo"].T, bo1=i["L1_xattn_bo"],
        m1_Wr=i["L1_ffn_gate_w"].T, m1_sel=selectors(E1, True),
        m1_Wg=halves(i["L1_ffn_w_gate"], i["L1_ffn_ws_gate"]),
        m1_Wu=halves(i["L1_ffn_w_up"], i["L1_ffn_ws_up"]),
        m1_Wd=halves(i["L1_ffn_w_down"].transpose(0, 2, 1), i["L1_ffn_ws_down"].T).transpose(2, 1, 0))


def kernel(**inputs):
    import numpy as _np
    import concourse.bacc as _bacc
    from concourse import mybir as _mybir
    from concourse.bass_utils import run_bass_kernel_spmd as _run

    nc = _bacc.Bacc("TRN2", target_bir_lowering=False, num_devices=1)
    arrays, args = {}, {}
    for name, a in laid_out({k: _np.asarray(v) for k, v in inputs.items()}).items():
        a = _np.ascontiguousarray(a)
        arrays[f"in_{name}_dram"] = a
        args[name] = nc.dram_tensor(f"in_{name}_dram", a.shape, _mybir.dt.from_np(a.dtype), kind="ExternalInput").ap()
    out = nc.dram_tensor("out_0_dram", (B * S, D), F32, kind="ExternalOutput").ap()
    xattn_ffn_twice_kernel(nc, out=out, **args)
    r = _run(nc, [arrays], core_ids=[0])
    return r.results[0]["out_0_dram"].reshape(B, S, D)
```

```python
from contextlib import ExitStack

import numpy as np
import concourse.bass as bass
from concourse import mybir

F32 = mybir.dt.float32
F32R = mybir.dt.float32r
ALU = mybir.AluOpType
ACT = mybir.ActivationFunctionType
AX = mybir.AxisListType

P = 128
B, S, D = 8, 256, 128
H, DH = 16, 8
HH = 4
G = H // HH
QUAD = P // HH
IT = S // P
EPS = 1e-5
SCALE = float(DH) ** -0.5
MASKED = -1.0e30
LOWEST = -3.0e38
BANK = 512
PITCH = S + P
MAXROW = 3 * DH


def after(eng, sem, count):
    if not (isinstance(count, int) and count <= 0):
        eng.wait_ge(sem, count)


def every_batch(eng, first, both, last):
    first(0, 0)
    both(0, 0)
    both(1, 1)
    for turn in range(1, B // 2 - 1):
        both(turn * 2, 0)
        both(turn * 2 + 1, 1)
    both(B - 2, 0)
    last(B - 1, 1)


def tokens(X, b, t=0, n=1):
    return X[:, bass.ds(b * S + t * D, n * D)]


def relative_attention(nc, X, ident, x_dram, d, rel):
    with ExitStack() as ctx:
        def sb(name, shape, dt=F32):
            return ctx.enter_context(nc.sbuf_tensor("a0_" + name, shape, dt))

        def sem(name):
            return ctx.enter_context(nc.semaphore("a0_" + name))

        ctxT = sb("ctxT", [P, 2, S])
        WqR = sb("WqR", [P, G, P])
        WkR = sb("WkR", [P, G, P])
        WvT = sb("WvT", [P, D])
        bqR = sb("bqR", [P, G])
        bkR = sb("bkR", [P, G])
        lo = sb("lo", [P, 2])
        bv = sb("bv", [1, D])
        ones = sb("ones", [1, P])
        table = sb("table", [1, 1])
        ErM = sb("ErM", [P, HH, S], F32R)
        mask = sb("mask", [P, P])
        half = sb("half", [P, IT])
        stats = sb("stats", [P, 2, IT, 6])
        mv = sb("mv", [P, 2, IT, 2])
        veps = sb("veps", [P, 2, IT])
        rstd = sb("rstd", [P, 2, IT])
        xn = sb("xn", [P, 2, IT, D])
        xnT = sb("xnT", [P, 2, S])
        full = sb("full", [P, 4, 2, S])
        high = sb("high", [P, 2, 2, S], F32R)
        qst = sb("qst", [P, 2, G, S], F32R)
        kst = sb("kst", [P, 2, G, S], F32R)
        kmask = sb("kmask", [P, 2, HH, G, S], F32R)
        vaug = sb("vaug", [P, 2, IT, H, QUAD])
        qe = sb("qe", [P, 4, HH, S])
        tr = sb("tr", [P, G, HH, P + S])
        T = sb("T", [P, 2, HH, P + S])
        rowmax = sb("rowmax", [P, 2, IT, HH])
        Tm = sb("Tm", [P, 2, HH, P + S])
        PT = sb("PT", [P, 2, IT, HH, S])
        OT = sb("OT", [P, G, S])
        rden = sb("rden", [P, IT, H])
        att = sb("att", [P, IT, D])

        bank = [ctx.enter_context(nc.psum_tensor(f"a0_bank{i}", [P, BANK], F32)) for i in range(8)]
        ring, outp, scb, ttb = bank[0:2], bank[2:4], bank[4:6], bank[6:8]

        weights = sem("weights")
        extras, wv_in, er_in, ones_set = sem("extras"), sem("wv_in"), sem("er_in"), sem("ones_set")
        mask_set, kmask_zero, vaug_set, er_ready = sem("mask_set"), sem("kmask_zero"), sem("vaug_set"), sem("er_ready")
        x_in = [sem("x_in0"), sem("x_in1")]
        ctx_in = [sem("ctx_in0"), sem("ctx_in1")]
        er_high = sem("er_high")
        maskrow = [[sem(f"maskrow{p}{g}") for g in range(G)] for p in range(2)]
        bn_raw, bn_mean, var_ready = sem("bn_raw"), sem("bn_mean"), sem("var_ready")
        half_set, rstd_ready = sem("half_set"), sem("rstd_ready")
        xn_ready = sem("xn_ready")
        ring_full, ring_read = sem("ring_full"), sem("ring_read")
        high_ready, stack_ready = sem("high_ready"), sem("stack_ready")
        kmask_in = sem("kmask_in")
        qe_out = [sem(f"qe_out{i}") for i in range(4)]
        tr_in = [sem(f"tr_in{g}") for g in range(G)]
        sc_full, t_ready, tm_ready = sem("sc_full"), sem("t_ready"), sem("tm_ready")
        tt_full, pt_ready, pv_done = sem("tt_full"), sem("pt_ready"), sem("pv_done")
        ot_ready, o_full, rden_ready, att_ready, x_new = (
            sem("ot_ready"), sem("o_full"), sem("rden_ready"), sem("att_ready"), sem("x_new"))

        XT, CHUNK, RELATIVE, VALUES, FILLS = 0, 1, 5, 5 + 3 * G, 6 + 3 * G

        def bank_of(fill):
            return ring[fill % 2]

        block = ctx.enter_context(nc.Block())

        @block.sync
        def _(sp):
            x_tiles = x_dram.rearrange("(t p) d -> p t d", p=P)
            X_tiles = X[:].rearrange("p (t d) -> p t d", d=D)
            sp.dma_start(X_tiles[:, 0:IT], x_tiles[:, 0:IT]).then_inc(x_in[0], 16)
            sp.dma_start(ident[:], d["ident"]).then_inc(weights, 16)
            sp.dma_start(WqR[:], d["WqR0"]).then_inc(weights, 16)
            sp.dma_start(bqR[:], d["bqR0"]).then_inc(weights, 16)
            sp.dma_start(WkR[:], d["WkR0"]).then_inc(weights, 16)
            sp.dma_start(ctxT[:, 0, :], d["ctxT"][:, 0:S]).then_inc(ctx_in[0], 16)
            sp.dma_start(X_tiles[:, IT:], x_tiles[:, IT:]).then_inc(x_in[1], 16)
            sp.dma_start(ctxT[:, 1, :], d["ctxT"][:, S:2 * S]).then_inc(ctx_in[1], 16)

            def mask_rows(p):
                for g in range(G):
                    sp.dma_start(
                        rel[p, HH * g:HH * g + HH, :, S:PITCH].rearrange("h (t i) l -> i (h t) l", i=P),
                        mask[:].unsqueeze(1).to_broadcast([P, HH * IT, P])).then_inc(maskrow[p][g], 16)

            def keys(b, p):
                sp.wait_ge(stack_ready, 4 * b + 4)
                sp.wait_ge(kmask_zero, 2)
                after(sp, sc_full, 12 * (b - 1))
                for hh in range(HH):
                    q = slice(QUAD * hh, QUAD * hh + QUAD)
                    sp.dma_start(kmask[q, p, hh, :, :].bitcast(F32), kst[q, p, :, :].bitcast(F32)
                                  ).then_inc(kmask_in, 16)

            def rows_out(b, p, g):
                for t in range(IT):
                    n = (2 * g + t) % 4
                    l0 = S - P * (t + 1)
                    sp.wait_ge(ring_read, FILLS * b + RELATIVE + 3 * g + 1 + 2 * t)
                    after(sp, t_ready, 12 * (b - 2) + 3 * g + 3)
                    sp.dma_start(
                        rel[p, HH * g:HH * g + HH, P * t:P * t + P, l0:S].rearrange("h i l -> i h l"),
                        qe[:, n, :, l0:S]).then_inc(qe_out[n], 16)

            def rows_in(b, p, g):
                for t in range(IT):
                    sp.wait_ge(qe_out[(2 * g + t) % 4], 16 * (2 * b + g // 2 + 1))
                sp.wait_ge(maskrow[p][g], 16)
                after(sp, t_ready, 12 * (b - 1) + 3 * g + 3)
                for t in range(IT):
                    i0 = P * t
                    at = rel[p, HH * g, i0:i0 + 1, S - 1 - i0:S]
                    src = bass.AP(tensor=at.tensor, offset=at.offset,
                                  ap=[[PITCH - 1, P], [S * PITCH, HH], [1, P * (t + 1)]])
                    dst = tr[:, g, :, 0:P] if t == 0 else tr[:, g, :, P:P + S]
                    sp.dma_start(dst, src).then_inc(tr_in[g], 16)

            def ahead(b, p):
                rows_out(b, p, 0)
                rows_out(b, p, 1)
                rows_in(b, p, 0)
                keys(b, p)
                rows_out(b, p, 2)
                rows_in(b, p, 1)
                rows_out(b, p, 3)
                rows_in(b, p, 2)
                rows_in(b, p, 3)

            sp.wait_ge(mask_set, 1)
            mask_rows(0)
            ahead(0, 0)
            mask_rows(1)
            for b in range(B - 1):
                p = b % 2
                if b + 2 < B:
                    sp.wait_ge(ring_read, FILLS * b + VALUES + 1)
                    sp.dma_start(ctxT[:, p, :], d["ctxT"][:, bass.ds((b + 2) * S, S)]).then_inc(ctx_in[p], 16)
                ahead(b + 1, 1 - p)

        @block.gpsimd
        def _(pool):
            nc.gpsimd.memset(mask[:], MASKED).then_inc(mask_set, 1)
            nc.gpsimd.memset(half[:], -0.5).then_inc(half_set, 1)
            pool.dma_start(qe[:, 0], d["ErR"]).then_inc(er_in, 16)
            nc.gpsimd.memset(vaug[:], 0.0).then_inc(vaug_set, 1)
            pool.wait_ge(vaug_set, 1)
            nc.gpsimd.memset(vaug[:, :, :, :, DH:DH + 1], 1.0).then_inc(vaug_set, 1)
            pool.wait_ge(half_set, 1)

            def inverse_deviation(b, p):
                pool.wait_ge(var_ready, b + 1)
                after(pool, xn_ready, b - 1)
                nc.gpsimd.tensor_tensor(rstd[:, p, :], veps[:, p, :], half[:], ALU.pow).then_inc(rstd_ready, 1)

            def less_max(b, g):
                u = 4 * b + g
                after(pool, tt_full, 3 * (u - 1))
                for t in range(IT):
                    c = slice(0, P) if t == 0 else slice(P, P + S)
                    pool.wait_ge(t_ready, 3 * u + 1 + 2 * t)
                    nc.gpsimd.tensor_tensor(
                        Tm[:, g % 2, :, c], T[:, g % 2, :, c],
                        rowmax[:, g % 2, t, :].unsqueeze(2).to_broadcast([P, HH, P * (t + 1)]),
                        ALU.subtract).then_inc(tm_ready, 1)

            inverse_deviation(0, 0)
            for p in range(2):
                nc.gpsimd.memset(kmask[:, p].bitcast(F32), 0.0).then_inc(kmask_zero, 1)
            inverse_deviation(1, 1)
            for b in range(B):
                for g in range(G):
                    less_max(b, g)
                    if g == 1 and b + 2 < B:
                        inverse_deviation(b + 2, b % 2)

        @block.vector
        def _(dve):
            def statistics(b, p):
                dve.wait_ge(x_in[min(b, 1)], 16)
                after(dve, rstd_ready, b - 1)
                for t in range(IT):
                    ins = nc.vector.bn_stats(stats[:, p, t, :], tokens(X, b, t))
                ins.then_inc(bn_raw, 1)
                dve.wait_ge(bn_raw, b + 1)
                for t in range(IT):
                    ins = nc.vector.bn_aggr(mv[:, p, t, :], stats[:, p, t, :])
                ins.then_inc(bn_mean, 1)
                dve.wait_ge(bn_mean, b + 1)
                nc.vector.tensor_scalar(veps[:, p, :], mv[:, p, :, 1], EPS, None, ALU.add).then_inc(var_ready, 1)

            def normalize(b, p):
                dve.wait_ge(rstd_ready, b + 1)
                after(dve, ring_full, FILLS * (b - 2) + XT + 1)
                for t in range(IT):
                    ins = nc.vector.tensor_scalar(xn[:, p, t, :], tokens(X, b, t), mv[:, p, t, 0:1],
                                                  rstd[:, p, t:t + 1], ALU.subtract, ALU.mult)
                ins.then_inc(xn_ready, 1)

            def stack(b, p, c):
                n = 4 * b + c
                dve.wait_ge(ring_read, FILLS * b + CHUNK + c + 1)
                after(dve, stack_ready, n - 1)
                nc.vector.tensor_copy(high[:, c % 2], full[:, c]).then_inc(high_ready, 1)
                dve.wait_ge(high_ready, n + 1)
                to = (qst if c < 2 else kst)[:, p, 2 * (c % 2):2 * (c % 2) + 2, :]
                if c < 2:
                    after(dve, sc_full, 12 * (b - 1))
                else:
                    after(dve, kmask_in, 64 * (b - 1))
                nc.vector.scalar_tensor_tensor(
                    to, high[:, c % 2].bitcast(F32), lo[:, c // 2:c // 2 + 1], full[:, c],
                    ALU.mult, ALU.add).then_inc(stack_ready, 1)

            def scores(b, p, g):
                u = 4 * b + g
                after(dve, tm_ready, 2 * (u - 1))
                dve.wait_ge(tr_in[g], 16 * IT * (b + 1))
                for f in range(3):
                    dve.wait_ge(sc_full, 3 * u + f + 1)
                    src = scb[(g + f) % 2]
                    for k in range(HH if f == 0 else 2):
                        hh = k if f == 0 else 2 * (f - 1) + k
                        n = P if f == 0 else S
                        c = slice(0, P) if f == 0 else slice(P, P + S)
                        ins = nc.vector.tensor_tensor_reduce(
                            out=T[:, g % 2, hh, c], in0=src[:, k * n:k * n + n], in1=tr[:, g, hh, c],
                            scale=1.0, scalar=LOWEST, op0=ALU.add, op1=ALU.max,
                            accum_out=rowmax[:, g % 2, min(f, 1), hh:hh + 1])
                    ins.then_inc(t_ready, 1)

            def output(b, p):
                after(dve, x_new, b)
                for t in range(IT):
                    dve.wait_ge(o_full, IT * b + t + 1)
                    o = outp[t][:].rearrange("p (h e) -> p h e", e=QUAD)
                    nc.vector.reciprocal(rden[:, t, :], o[:, :, DH]).then_inc(rden_ready, 1)
                    dve.wait_ge(rden_ready, IT * b + t + 1)
                    nc.vector.tensor_tensor(att[:, t, :].rearrange("p (h e) -> p h e", e=DH), o[:, :, 0:DH],
                                            rden[:, t, :].unsqueeze(2).to_broadcast([P, H, DH]),
                                            ALU.mult).then_inc(att_ready, 1)
                dve.wait_ge(att_ready, IT * b + IT)
                nc.vector.tensor_tensor(tokens(X, b, 0, IT), tokens(X, b, 0, IT),
                                        att[:].rearrange("p t d -> p (t d)"), ALU.add).then_inc(x_new, 1)

            nc.vector.memset(ones[:], 1.0).then_inc(ones_set, 1)
            statistics(0, 0)
            normalize(0, 0)
            dve.wait_ge(er_in, 16)
            erh = high[:].rearrange("p a b s -> p (a b s)")
            nc.vector.tensor_copy(erh, qe[:, 0].rearrange("p h s -> p (h s)")).then_inc(er_high, 1)
            dve.wait_ge(er_high, 1)
            dve.wait_ge(extras, 16 * 2)
            nc.vector.scalar_tensor_tensor(ErM[:].rearrange("p h s -> p (h s)"), erh.bitcast(F32), lo[:, 1:2],
                                           qe[:, 0].rearrange("p h s -> p (h s)"),
                                           ALU.mult, ALU.add).then_inc(er_ready, 1)
            dve.wait_ge(er_ready, 1)
            for c in range(4):
                stack(0, 0, c)
            statistics(1, 1)
            normalize(1, 1)
            for b in range(B):
                p = b % 2
                begun, more, further = b >= 1, b + 1 < B, b + 2 < B
                scores(b, p, 0)
                if more:
                    stack(b + 1, 1 - p, 0)
                    stack(b + 1, 1 - p, 1)
                scores(b, p, 1)
                if more:
                    stack(b + 1, 1 - p, 2)
                    stack(b + 1, 1 - p, 3)
                if further:
                    statistics(b + 2, p)
                scores(b, p, 2)
                if further:
                    normalize(b + 2, p)
                if begun:
                    output(b - 1, 1 - p)
                scores(b, p, 3)
            output(B - 1, 1)

        @block.scalar
        def _(act):
            act.dma_start(bkR[:], d["bkR0"]).then_inc(extras, 16)
            act.dma_start(lo[:], d["lo"]).then_inc(extras, 16)
            act.dma_start(WvT[:], d["WvT0"]).then_inc(wv_in, 16)
            act.dma_start(bv[:], d["bv0"].unsqueeze(0)).then_inc(wv_in, 16)
            act.wait_ge(ones_set, 1)
            nc.scalar.activation(table[:], ones[:, 0:1], ACT.Exp)
            act.wait_ge(weights, 16 * 4)

            def read(b, fill):
                return act.wait_ge(ring_full, FILLS * b + fill + 1)

            def xT(b, p):
                read(b, XT)
                after(act, ring_full, FILLS * (b - 2) + CHUNK + 2)
                nc.scalar.copy(xnT[:, p, :], bank_of(XT)[:, 0:S]).then_inc(ring_read, 1)

            def chunk(b, c):
                read(b, CHUNK + c)
                after(act, stack_ready, 4 * (b - 1) + c + 1)
                if c == 2:
                    act.wait_ge(extras, 16 * 2)
                for j in range(2):
                    g = 2 * (c % 2) + j
                    ins = nc.scalar.activation(full[:, c, j, :], bank_of(CHUNK + c)[:, j * S:j * S + S], ACT.Identity,
                                               bias=(bqR if c < 2 else bkR)[:, g:g + 1])
                ins.then_inc(ring_read, 1)

            def values(b, p):
                read(b, VALUES)
                if b == 0:
                    act.wait_ge(vaug_set, 2)
                after(act, pv_done, 4 * (b - 1))
                nc.scalar.copy(vaug[:, p, :, :, 0:DH],
                               bank_of(VALUES)[:, 0:S].rearrange("p (t h e) -> p t h e", h=H, e=DH)
                               ).then_inc(ring_read, 1)

            def relative(b, g, fills):
                for f in fills:
                    t = min(f, 1)
                    n = (2 * g + t) % 4
                    fill = RELATIVE + 3 * g + f
                    read(b, fill)
                    after(act, qe_out[n], 16 * (2 * b + g // 2))
                    if b == 0 and g == 0:
                        act.wait_ge(er_ready, 1)
                    src = bank_of(fill)[:].rearrange("p (h l) -> p h l", l=P if f == 0 else S)
                    to = qe[:, n, :, P:S] if f == 0 else qe[:, n, 2 * (f - 1):2 * f, :]
                    nc.scalar.copy(to, src).then_inc(ring_read, 1)

            def exps(b, g, fills):
                u = 4 * b + g
                after(act, pv_done, u - 1)
                for f in fills:
                    act.wait_ge(tt_full, 3 * u + f + 1)
                    to = PT[:, g % 2, 0, :, 0:P] if f == 0 else PT[:, g % 2, f - 1, :, P:S]
                    nc.scalar.activation(to, ttb[(g + f) % 2][:].rearrange("p (h i) -> p h i", i=P), ACT.Exp,
                                         scale=SCALE).then_inc(pt_ready, 1)

            def oT(b, k):
                act.wait_ge(pv_done, 4 * b + 2 * k + 2)
                after(act, o_full, IT * b)
                nc.scalar.copy(OT[:, 2 * k:2 * k + 2, :], outp[k][:].rearrange("p (g i) -> p g i", i=S)
                               ).then_inc(ot_ready, 1)

            xT(0, 0)
            for c in range(4):
                chunk(0, c)
            for g in range(G):
                relative(0, g, range(3))
            values(0, 0)
            xT(1, 1)
            chunk(1, 0)
            chunk(1, 1)
            two, third = range(2), range(2, 3)
            for b in range(B):
                p = b % 2
                begun, more, further = b >= 1, b + 1 < B, b + 2 < B
                if begun:
                    oT(b - 1, 0)
                    exps(b - 1, 3, two)
                if more:
                    chunk(b + 1, 2)
                if begun:
                    exps(b - 1, 3, third)
                if more:
                    chunk(b + 1, 3)
                    relative(b + 1, 0, two)
                exps(b, 0, two)
                if more:
                    relative(b + 1, 0, third)
                exps(b, 0, third)
                if more:
                    relative(b + 1, 1, range(3))
                if begun:
                    oT(b - 1, 1)
                if more:
                    relative(b + 1, 2, two)
                exps(b, 1, two)
                if more:
                    relative(b + 1, 2, third)
                exps(b, 1, third)
                if more:
                    relative(b + 1, 3, two)
                exps(b, 2, two)
                if more:
                    relative(b + 1, 3, third)
                    values(b + 1, 1 - p)
                if further:
                    xT(b + 2, p)
                exps(b, 2, third)
                if further:
                    chunk(b + 2, 0)
                    chunk(b + 2, 1)
            oT(B - 1, 0)
            exps(B - 1, 3, range(3))
            oT(B - 1, 1)

        @block.tensor
        def _(pe):
            def fill(b, n):
                after(pe, ring_read, FILLS * b + n - 1)
                return bank_of(n)

            def xT(b, p):
                pe.wait_ge(xn_ready, b + 1)
                to = fill(b, XT)
                for t in range(IT):
                    ins = nc.tensor.transpose(to[:, t * P:t * P + P], xn[:, p, t, :], ident[:])
                ins.then_inc(ring_full, 1)

            def chunk(b, p, c):
                to = fill(b, CHUNK + c)
                if c == 0:
                    pe.wait_ge(ring_read, FILLS * b + XT + 1)
                if c == 2:
                    pe.wait_ge(ctx_in[p], 8 * (b - p) + 16)
                for j in range(2):
                    g = 2 * (c % 2) + j
                    w, x = (WqR, xnT) if c < 2 else (WkR, ctxT)
                    ins = nc.tensor.matmul(to[:, j * S:j * S + S], w[:, g, :], x[:, p, :], start=True, stop=True)
                ins.then_inc(ring_full, 1)

            def values(b, p):
                to = fill(b, VALUES)
                for t in range(IT):
                    nc.tensor.matmul(to[:, t * P:t * P + P], ctxT[:, p, t * P:t * P + P], WvT[:],
                                     start=True, stop=False)
                    ins = nc.tensor.matmul(to[:, t * P:t * P + P], ones[:], bv[:], start=False, stop=True)
                ins.then_inc(ring_full, 1)

            def relative(b, p, g, fills):
                pe.wait_ge(stack_ready, 4 * b + g // 2 + 1)
                for f in fills:
                    to = fill(b, RELATIVE + 3 * g + f)
                    t = min(f, 1)
                    er = ErM[:, :, P:S] if f == 0 else ErM[:, 2 * (f - 1):2 * f, :]
                    nc.tensor.matmul(to[:], qst[:, p, g, t * P:t * P + P], er,
                                     start=True, stop=True).then_inc(ring_full, 1)

            def scores(b, p, g, fills):
                if g == 0:
                    pe.wait_ge(kmask_in, 64 * (b + 1))
                for f in fills:
                    n = 12 * b + 3 * g + f
                    after(pe, t_ready, n - 1)
                    t = min(f, 1)
                    k = kmask[:, p, :, g, 0:P] if f == 0 else kmask[:, p, 2 * (f - 1):2 * f, g, :]
                    nc.tensor.matmul(scb[(g + f) % 2][:], qst[:, p, g, t * P:t * P + P], k,
                                     start=True, stop=True).then_inc(sc_full, 1)

            def transposed(b, g, fills):
                u = 4 * b + g
                for f in fills:
                    pe.wait_ge(tm_ready, 2 * u + 1 + min(f, 1))
                    after(pe, pt_ready, 3 * u + f - 1)
                    for hh in range(HH):
                        ins = nc.tensor.transpose(ttb[(g + f) % 2][:, hh * P:hh * P + P],
                                                  Tm[:, g % 2, hh, f * P:f * P + P], ident[:])
                    ins.then_inc(tt_full, 1)

            def weighted(b, p, g):
                u = 4 * b + g
                pe.wait_ge(pt_ready, 3 * u + 3)
                if g == 0:
                    pe.wait_ge(ring_read, FILLS * b + VALUES + 1)
                if g % 2 == 0:
                    after(pe, att_ready, IT * (b - 1) + g // 2 + 1)
                c = (g % 2) * S
                for jt in range(IT):
                    for hh in range(HH):
                        q = slice(QUAD * hh, QUAD * hh + QUAD)
                        ins = nc.tensor.matmul(outp[g // 2][q, c + jt * P:c + S], vaug[:, p, jt, HH * g + hh, :],
                                               PT[:, g % 2, jt, hh, jt * P:S], start=(jt == 0), stop=(jt == IT - 1),
                                               skip_group_check=True)
                ins.then_inc(pv_done, 1)

            def output(b):
                pe.wait_ge(ot_ready, 2 * b + 2)
                for t in range(IT):
                    for g in range(G):
                        ins = nc.tensor.transpose(outp[t][:, g * P:g * P + P], OT[:, g, t * P:t * P + P], ident[:])
                    ins.then_inc(o_full, 1)

            pe.wait_ge(weights, 16 * 4)
            xT(0, 0)
            for c in range(4):
                chunk(0, 0, c)
            pe.wait_ge(er_ready, 1)
            for g in range(G):
                relative(0, 0, g, range(3))
            pe.wait_ge(wv_in, 32)
            pe.wait_ge(ones_set, 1)
            values(0, 0)
            xT(1, 1)
            chunk(1, 1, 0)
            chunk(1, 1, 1)
            two, third = range(2), range(2, 3)
            for b in range(B):
                p = b % 2
                begun, more, further = b >= 1, b + 1 < B, b + 2 < B
                n = b + 1, 1 - p
                scores(b, p, 0, two)
                if begun:
                    transposed(b - 1, 3, two)
                if more:
                    chunk(*n, 2)
                scores(b, p, 0, third)
                if begun:
                    transposed(b - 1, 3, third)
                if more:
                    chunk(*n, 3)
                if begun:
                    weighted(b - 1, 1 - p, 2)
                scores(b, p, 1, two)
                if more:
                    relative(*n, 0, two)
                transposed(b, 0, two)
                scores(b, p, 1, third)
                if more:
                    relative(*n, 0, third)
                transposed(b, 0, third)
                if more:
                    relative(*n, 1, two)
                if begun:
                    weighted(b - 1, 1 - p, 3)
                if more:
                    relative(*n, 1, third)
                scores(b, p, 2, two)
                if more:
                    relative(*n, 2, two)
                transposed(b, 1, two)
                scores(b, p, 2, third)
                if more:
                    relative(*n, 2, third)
                transposed(b, 1, third)
                if begun:
                    output(b - 1)
                weighted(b, p, 0)
                scores(b, p, 3, two)
                if more:
                    relative(*n, 3, two)
                transposed(b, 2, two)
                scores(b, p, 3, third)
                if more:
                    relative(*n, 3, third)
                    values(*n)
                if further:
                    xT(b + 2, p)
                transposed(b, 2, third)
                if further:
                    chunk(b + 2, p, 0)
                weighted(b, p, 1)
                if further:
                    chunk(b + 2, p, 1)
            transposed(B - 1, 3, range(3))
            weighted(B - 1, 1, 2)
            weighted(B - 1, 1, 3)
            output(B - 1)


def attention(nc, X, ident, d):
    with ExitStack() as ctx:
        def sb(name, shape, dt=F32):
            return ctx.enter_context(nc.sbuf_tensor("a1_" + name, shape, dt))

        def sem(name):
            return ctx.enter_context(nc.semaphore("a1_" + name))

        ctxT = sb("ctxT", [P, 2, S])
        WqR = sb("WqR", [P, G, P])
        WkR = sb("WkR", [P, G, P])
        WvT = sb("WvT", [P, D])
        WoT = sb("WoT", [P, D])
        bqR = sb("bqR", [P, G])
        bkR = sb("bkR", [P, G])
        lo = sb("lo", [P, 2])
        bv = sb("bv", [1, D])
        bo = sb("bo", [1, D])
        ones = sb("ones", [1, P])
        half = sb("half", [P, IT])
        stats = sb("stats", [P, 2, IT, 6])
        mv = sb("mv", [P, 2, IT, 2])
        veps = sb("veps", [P, 2, IT])
        rstd = sb("rstd", [P, 2, IT])
        xn = sb("xn", [P, 2, IT, D])
        xnT = sb("xnT", [P, 2, S])
        full = sb("full", [P, 4, 2, S])
        high = sb("high", [P, 2, 2, S], F32R)
        qst = sb("qst", [P, 2, G, S], F32R)
        kst = sb("kst", [P, 2, G, S], F32R)
        kmask = sb("kmask", [P, 2, HH, G, S], F32R)
        vaug = sb("vaug", [P, 2, IT, H, QUAD])
        nmax = sb("nmax", [P, 2, IT, P])
        qm = sb("qm", [P, 2, S], F32R)
        PT = sb("PT", [P, 2, HH, IT, S])
        OT = sb("OT", [P, G, S])
        rden = sb("rden", [P, IT, H])
        att = sb("att", [P, IT, D])
        attT = sb("attT", [P, S])

        bank = [ctx.enter_context(nc.psum_tensor(f"a1_bank{i}", [P, BANK], F32)) for i in range(8)]
        ring, outp, scb, stb = bank[0:2], bank[2:4], bank[4:6], bank[6:8]

        XT, CHUNK, VALUES, FILLS = 0, 1, 5, 6
        NS = 4
        MAXIMA, UNIT = NS, NS + 1
        NT = HH

        weights, out_weights = sem("weights"), sem("out_weights")
        ones_set, vaug_set, half_set, kmask_zero, nmax_zero = (
            sem("ones_set"), sem("vaug_set"), sem("half_set"), sem("kmask_zero"), sem("nmax_zero"))
        ctx_in = [sem("ctx_in0"), sem("ctx_in1")]
        bn_raw, bn_mean, var_ready, rstd_ready = sem("bn_raw"), sem("bn_mean"), sem("var_ready"), sem("rstd_ready")
        xn_ready, ring_full, ring_read = sem("xn_ready"), sem("ring_full"), sem("ring_read")
        high_ready, stack_ready, kmask_in = sem("high_ready"), sem("stack_ready"), sem("kmask_in")
        sc_full, sc_read = sem("sc_full"), sem("sc_read")
        st_full, pt_ready, pv_done = sem("st_full"), sem("pt_ready"), sem("pv_done")
        ot_ready, o_full, rden_ready, att_ready = sem("ot_ready"), sem("o_full"), sem("rden_ready"), sem("att_ready")
        attT_full, attT_ready, wo_full, x_new = sem("attT_full"), sem("attT_ready"), sem("wo_full"), sem("x_new")

        def bank_of(fill):
            return ring[fill % 2]

        def score_bank(b, g, f):
            return scb[(UNIT * g + f) % 2]

        block = ctx.enter_context(nc.Block())

        @block.sync
        def _(sp):
            for dst, src in ((WqR, "WqR1"), (bqR, "bqR1"), (WkR, "WkR1"), (bkR, "bkR1"), (lo, "lo")):
                sp.dma_start(dst[:], d[src]).then_inc(weights, 16)
            for b in range(2):
                sp.dma_start(ctxT[:, b, :], d["ctxT"][:, b * S:(b + 1) * S]).then_inc(ctx_in[b], 16)
            for dst, src in ((WvT, "WvT1"), (WoT, "WoT1")):
                sp.dma_start(dst[:], d[src]).then_inc(out_weights, 16)
            for dst, src in ((bv, "bv1"), (bo, "bo1")):
                sp.dma_start(dst[:], d[src].unsqueeze(0)).then_inc(out_weights, 16)

            def keys(b, p):
                sp.wait_ge(stack_ready, 4 * b + 4)
                sp.wait_ge(kmask_zero, 2)
                after(sp, st_full, 4 * NT * (b - 1))
                for hh in range(HH):
                    q = slice(QUAD * hh, QUAD * hh + QUAD)
                    sp.dma_start(kmask[q, p, hh, :, :].bitcast(F32), kst[q, p, :, :].bitcast(F32)
                                 ).then_inc(kmask_in, 16)

            keys(0, 0)
            for b in range(B - 1):
                p = b % 2
                if b + 2 < B:
                    sp.wait_ge(ring_read, FILLS * b + VALUES + 1)
                    sp.dma_start(ctxT[:, p, :], d["ctxT"][:, bass.ds((b + 2) * S, S)]).then_inc(ctx_in[p], 16)
                keys(b + 1, 1 - p)

        @block.gpsimd
        def _(pool):
            nc.gpsimd.memset(half[:], -0.5).then_inc(half_set, 1)
            pool.wait_ge(half_set, 1)

            def inverse_deviation(b, p):
                pool.wait_ge(var_ready, b + 1)
                after(pool, xn_ready, b - 1)
                nc.gpsimd.tensor_tensor(rstd[:, p, :], veps[:, p, :], half[:], ALU.pow).then_inc(rstd_ready, 1)

            inverse_deviation(0, 0)
            for p in range(2):
                nc.gpsimd.memset(kmask[:, p].bitcast(F32), 0.0).then_inc(kmask_zero, 1)
            nc.gpsimd.memset(nmax[:], 0.0).then_inc(nmax_zero, 1)
            nc.gpsimd.memset(vaug[:], 0.0).then_inc(vaug_set, 1)
            pool.wait_ge(vaug_set, 1)
            nc.gpsimd.memset(vaug[:, :, :, :, DH:DH + 1], 1.0).then_inc(vaug_set, 1)
            for b in range(1, B):
                inverse_deviation(b, b % 2)

        @block.vector
        def _(dve):
            nc.vector.memset(ones[:], 1.0).then_inc(ones_set, 1)

            def statistics(b, p):
                after(dve, rstd_ready, b - 1)
                for t in range(IT):
                    ins = nc.vector.bn_stats(stats[:, p, t, :], tokens(X, b, t))
                ins.then_inc(bn_raw, 1)
                dve.wait_ge(bn_raw, b + 1)
                for t in range(IT):
                    ins = nc.vector.bn_aggr(mv[:, p, t, :], stats[:, p, t, :])
                ins.then_inc(bn_mean, 1)
                dve.wait_ge(bn_mean, b + 1)
                nc.vector.tensor_scalar(veps[:, p, :], mv[:, p, :, 1], EPS, None, ALU.add).then_inc(var_ready, 1)

            def normalize(b, p):
                dve.wait_ge(rstd_ready, b + 1)
                after(dve, ring_full, FILLS * (b - 2) + XT + 1)
                for t in range(IT):
                    ins = nc.vector.tensor_scalar(xn[:, p, t, :], tokens(X, b, t), mv[:, p, t, 0:1],
                                                  rstd[:, p, t:t + 1], ALU.subtract, ALU.mult)
                ins.then_inc(xn_ready, 1)

            def stack(b, p, c):
                n = 4 * b + c
                dve.wait_ge(ring_read, FILLS * b + CHUNK + c + 1)
                after(dve, stack_ready, n - 1)
                nc.vector.tensor_copy(high[:, c % 2], full[:, c]).then_inc(high_ready, 1)
                dve.wait_ge(high_ready, n + 1)
                to = (qst if c < 2 else kst)[:, p, 2 * (c % 2):2 * (c % 2) + 2, :]
                if c < 2:
                    after(dve, sc_full, 4 * UNIT * (b - 1))
                    after(dve, sc_read, 4 * UNIT * (b - 1))
                else:
                    after(dve, kmask_in, 64 * (b - 1))
                nc.vector.scalar_tensor_tensor(
                    to, high[:, c % 2].bitcast(F32), lo[:, c // 2:c // 2 + 1], full[:, c],
                    ALU.mult, ALU.add).then_inc(stack_ready, 1)

            def maxima(b, g):
                u = 4 * b + g
                if u == 0:
                    dve.wait_ge(nmax_zero, 1)
                after(dve, sc_full, UNIT * (u - 1))
                for f in range(NS):
                    dve.wait_ge(sc_full, UNIT * u + f + 1)
                    c = QUAD * 2 * (f % 2) + MAXROW
                    nc.vector.tensor_reduce(nmax[:, g % 2, f // 2, c:c + QUAD + 1:QUAD],
                                            score_bank(b, g, f)[:].rearrange("p (h j) -> p h j", j=S), AX.X, ALU.max,
                                            negate=True).then_inc(sc_read, 1)

            def less_max(b, p, g):
                u = 4 * b + g
                dve.wait_ge(sc_full, UNIT * u + MAXIMA + 1)
                after(dve, st_full, NT * (u - 1))
                nc.vector.tensor_tensor(qm[:, g % 2, :], score_bank(b, g, MAXIMA)[:, 0:S],
                                        qst[:, p, g, :].bitcast(F32), ALU.add).then_inc(sc_read, 1)

            def output(b):
                after(dve, attT_full, b)
                for t in range(IT):
                    dve.wait_ge(o_full, IT * b + t + 1)
                    o = outp[t][:].rearrange("p (h e) -> p h e", e=QUAD)
                    nc.vector.reciprocal(rden[:, t, :], o[:, :, DH]).then_inc(rden_ready, 1)
                    dve.wait_ge(rden_ready, IT * b + t + 1)
                    nc.vector.tensor_tensor(att[:, t, :].rearrange("p (h e) -> p h e", e=DH), o[:, :, 0:DH],
                                            rden[:, t, :].unsqueeze(2).to_broadcast([P, H, DH]),
                                            ALU.mult).then_inc(att_ready, 1)

            def residual(b):
                dve.wait_ge(wo_full, b + 1)
                nc.vector.tensor_tensor(tokens(X, b, 0, IT), outp[1][:, 0:S], tokens(X, b, 0, IT),
                                        ALU.add).then_inc(x_new, 1)

            statistics(0, 0)
            normalize(0, 0)
            dve.wait_ge(weights, 16 * 5)
            for c in range(4):
                stack(0, 0, c)
            statistics(1, 1)
            normalize(1, 1)
            for b in range(B):
                p = b % 2
                begun, more, further = b >= 1, b + 1 < B, b + 2 < B
                maxima(b, 0)
                if more:
                    stack(b + 1, 1 - p, 0)
                less_max(b, p, 0)
                if more:
                    stack(b + 1, 1 - p, 1)
                maxima(b, 1)
                if more:
                    stack(b + 1, 1 - p, 2)
                less_max(b, p, 1)
                if more:
                    stack(b + 1, 1 - p, 3)
                if further:
                    statistics(b + 2, p)
                maxima(b, 2)
                if begun:
                    output(b - 1)
                less_max(b, p, 2)
                if further:
                    normalize(b + 2, p)
                maxima(b, 3)
                if begun:
                    residual(b - 1)
                less_max(b, p, 3)
            output(B - 1)
            residual(B - 1)

        @block.scalar
        def _(act):
            act.wait_ge(weights, 16 * 5)

            def read(b, fill):
                act.wait_ge(ring_full, FILLS * b + fill + 1)

            def xT(b, p):
                read(b, XT)
                after(act, ring_full, FILLS * (b - 2) + CHUNK + 2)
                nc.scalar.copy(xnT[:, p, :], bank_of(XT)[:, 0:S]).then_inc(ring_read, 1)

            def chunk(b, c):
                read(b, CHUNK + c)
                after(act, stack_ready, 4 * (b - 1) + c + 1)
                for j in range(2):
                    g = 2 * (c % 2) + j
                    ins = nc.scalar.activation(full[:, c, j, :], bank_of(CHUNK + c)[:, j * S:j * S + S], ACT.Identity,
                                               bias=(bqR if c < 2 else bkR)[:, g:g + 1])
                ins.then_inc(ring_read, 1)

            def values(b, p):
                read(b, VALUES)
                if b == 0:
                    act.wait_ge(vaug_set, 2)
                after(act, pv_done, 4 * (b - 1))
                nc.scalar.copy(vaug[:, p, :, :, 0:DH],
                               bank_of(VALUES)[:, 0:S].rearrange("p (t h e) -> p t h e", h=H, e=DH)
                               ).then_inc(ring_read, 1)

            def exps(b, g):
                u = 4 * b + g
                after(act, pv_done, u - 1)
                for f in range(NT):
                    act.wait_ge(st_full, NT * u + f + 1)
                    nc.scalar.activation(PT[:, g % 2, f].rearrange("p j i -> p (j i)"), stb[f % 2][:], ACT.Exp,
                                         scale=SCALE).then_inc(pt_ready, 1)

            def oT(b, k):
                act.wait_ge(pv_done, 4 * b + 2 * k + 2)
                after(act, o_full, IT * b)
                nc.scalar.copy(OT[:, 2 * k:2 * k + 2, :], outp[k][:].rearrange("p (g i) -> p g i", i=S)
                               ).then_inc(ot_ready, 1)

            def attended(b):
                act.wait_ge(attT_full, b + 1)
                after(act, wo_full, b)
                nc.scalar.copy(attT[:], outp[0][:, 0:S]).then_inc(attT_ready, 1)

            xT(0, 0)
            for c in range(4):
                chunk(0, c)
            values(0, 0)
            xT(1, 1)
            chunk(1, 0)
            chunk(1, 1)
            for b in range(B):
                p = b % 2
                begun, more, further = b >= 1, b + 1 < B, b + 2 < B
                if begun:
                    oT(b - 1, 0)
                    exps(b - 1, 3)
                if more:
                    chunk(b + 1, 2)
                    chunk(b + 1, 3)
                exps(b, 0)
                if begun:
                    oT(b - 1, 1)
                if more:
                    values(b + 1, 1 - p)
                exps(b, 1)
                if begun:
                    attended(b - 1)
                exps(b, 2)
                if further:
                    xT(b + 2, p)
                    chunk(b + 2, 0)
                    chunk(b + 2, 1)
            oT(B - 1, 0)
            exps(B - 1, 3)
            oT(B - 1, 1)
            attended(B - 1)

        @block.tensor
        def _(pe):
            def fill(b, n):
                after(pe, ring_read, FILLS * b + n - 1)
                return bank_of(n)

            def xT(b, p):
                pe.wait_ge(xn_ready, b + 1)
                to = fill(b, XT)
                for t in range(IT):
                    ins = nc.tensor.transpose(to[:, t * P:t * P + P], xn[:, p, t, :], ident[:])
                ins.then_inc(ring_full, 1)

            def chunk(b, p, c):
                to = fill(b, CHUNK + c)
                if c == 0:
                    pe.wait_ge(ring_read, FILLS * b + XT + 1)
                if c == 2:
                    pe.wait_ge(ctx_in[p], 8 * (b - p) + 16)
                for j in range(2):
                    g = 2 * (c % 2) + j
                    w, x = (WqR, xnT) if c < 2 else (WkR, ctxT)
                    ins = nc.tensor.matmul(to[:, j * S:j * S + S], w[:, g, :], x[:, p, :], start=True, stop=True)
                ins.then_inc(ring_full, 1)

            def values(b, p):
                to = fill(b, VALUES)
                for t in range(IT):
                    nc.tensor.matmul(to[:, t * P:t * P + P], ctxT[:, p, t * P:t * P + P], WvT[:],
                                     start=True, stop=False)
                    ins = nc.tensor.matmul(to[:, t * P:t * P + P], ones[:], bv[:], start=False, stop=True)
                ins.then_inc(ring_full, 1)

            def scores(b, p, g, fills):
                if g == 0:
                    pe.wait_ge(kmask_in, 64 * (b + 1))
                for f in fills:
                    after(pe, sc_read, UNIT * (4 * b + g) + f - 1)
                    t, k = f // 2, f % 2
                    nc.tensor.matmul(score_bank(b, g, f)[:], qst[:, p, g, t * P:t * P + P],
                                     kmask[:, p, 2 * k:2 * k + 2, g, :], start=True, stop=True).then_inc(sc_full, 1)

            def maxima(b, g):
                u = 4 * b + g
                pe.wait_ge(sc_read, UNIT * u + NS)
                for t in range(IT):
                    ins = nc.tensor.transpose(score_bank(b, g, MAXIMA)[:, t * P:t * P + P], nmax[:, g % 2, t, :],
                                              ident[:])
                ins.then_inc(sc_full, 1)

            def by_key(b, p, g, fills):
                u = 4 * b + g
                pe.wait_ge(sc_read, UNIT * (u + 1))
                for f in fills:
                    after(pe, pt_ready, NT * u + f - 1)
                    for jt in range(IT):
                        ins = nc.tensor.matmul(stb[f % 2][:, jt * S:jt * S + S], kmask[:, p, f, g, jt * P:jt * P + P],
                                               qm[:, g % 2, :], start=True, stop=True)
                    ins.then_inc(st_full, 1)

            def weighted(b, p, g):
                u = 4 * b + g
                pe.wait_ge(pt_ready, NT * (u + 1))
                if g == 0:
                    pe.wait_ge(ring_read, FILLS * b + VALUES + 1)
                    after(pe, attT_ready, b)
                if g == 2:
                    after(pe, x_new, b)
                c = (g % 2) * S
                for jt in range(IT):
                    for hh in range(HH):
                        q = slice(QUAD * hh, QUAD * hh + QUAD)
                        ins = nc.tensor.matmul(outp[g // 2][q, c:c + S], vaug[:, p, jt, HH * g + hh, :],
                                               PT[:, g % 2, hh, jt, :], start=(jt == 0), stop=(jt == IT - 1),
                                               skip_group_check=True)
                ins.then_inc(pv_done, 1)

            def output(b):
                pe.wait_ge(ot_ready, 2 * b + 2)
                for t in range(IT):
                    for g in range(G):
                        ins = nc.tensor.transpose(outp[t][:, g * P:g * P + P], OT[:, g, t * P:t * P + P], ident[:])
                    ins.then_inc(o_full, 1)

            def attended(b):
                pe.wait_ge(att_ready, IT * b + IT)
                for t in range(IT):
                    ins = nc.tensor.transpose(outp[0][:, t * P:t * P + P], att[:, t, :], ident[:])
                ins.then_inc(attT_full, 1)

            def project(b):
                pe.wait_ge(attT_ready, b + 1)
                for t in range(IT):
                    nc.tensor.matmul(outp[1][:, t * P:t * P + P], attT[:, t * P:t * P + P], WoT[:],
                                     start=True, stop=False)
                    ins = nc.tensor.matmul(outp[1][:, t * P:t * P + P], ones[:], bo[:], start=False, stop=True)
                ins.then_inc(wo_full, 1)

            pe.wait_ge(weights, 16 * 5)
            xT(0, 0)
            for c in range(4):
                chunk(0, 0, c)
            pe.wait_ge(out_weights, 16 * 4)
            pe.wait_ge(ones_set, 1)
            values(0, 0)
            xT(1, 1)
            chunk(1, 1, 0)
            chunk(1, 1, 1)
            two, third, fourth = range(2), range(2, 3), range(3, 4)
            for b in range(B):
                p = b % 2
                begun, more, further = b >= 1, b + 1 < B, b + 2 < B
                n = b + 1, 1 - p
                scores(b, p, 0, two)
                if begun:
                    by_key(b - 1, 1 - p, 3, two)
                if more:
                    chunk(*n, 2)
                scores(b, p, 0, third)
                if begun:
                    by_key(b - 1, 1 - p, 3, third)
                    weighted(b - 1, 1 - p, 2)
                scores(b, p, 0, fourth)
                if begun:
                    by_key(b - 1, 1 - p, 3, fourth)
                if more:
                    chunk(*n, 3)
                maxima(b, 0)
                scores(b, p, 1, two)
                by_key(b, p, 0, two)
                scores(b, p, 1, third)
                by_key(b, p, 0, third)
                if begun:
                    weighted(b - 1, 1 - p, 3)
                scores(b, p, 1, fourth)
                by_key(b, p, 0, fourth)
                if more:
                    values(*n)
                maxima(b, 1)
                scores(b, p, 2, two)
                by_key(b, p, 1, two)
                if begun:
                    output(b - 1)
                scores(b, p, 2, third)
                by_key(b, p, 1, third)
                scores(b, p, 2, fourth)
                by_key(b, p, 1, fourth)
                if begun:
                    attended(b - 1)
                maxima(b, 2)
                weighted(b, p, 0)
                scores(b, p, 3, two)
                by_key(b, p, 2, two)
                if begun:
                    project(b - 1)
                if further:
                    xT(b + 2, p)
                scores(b, p, 3, third)
                by_key(b, p, 2, third)
                weighted(b, p, 1)
                scores(b, p, 3, fourth)
                by_key(b, p, 2, fourth)
                if further:
                    chunk(b + 2, p, 0)
                maxima(b, 3)
                if further:
                    chunk(b + 2, p, 1)
            by_key(B - 1, 1, 3, range(NT))
            weighted(B - 1, 1, 2)
            weighted(B - 1, 1, 3)
            output(B - 1)
            attended(B - 1)
            project(B - 1)


def experts(nc, X, ident, d, tag, E, blocks, shared, n_scaled):
    with ExitStack() as ctx:
        def sb(name, shape, dt=F32):
            return ctx.enter_context(nc.sbuf_tensor(tag + "s_" + name, shape, dt))

        def sem(name):
            return ctx.enter_context(nc.semaphore(tag + name))

        pairs = E // 2
        per_pair = 3 if n_scaled else 1
        NHG, NHID = 3, 4
        PAD = 6

        Wr = sb("Wr", [P, E])
        Wg = sb("Wg", [P, blocks, P])
        Wu = sb("Wu", [P, blocks, P])
        Wd = sb("Wd", [P, blocks, P])
        selF = sb("selF", [2 * E, pairs, 2 if n_scaled else 1, P])
        sel = sb("sel", [2 * E, pairs, 2 if n_scaled else 1, P], F32R)
        half = sb("half", [P, IT])
        stats = sb("stats", [P, 2, IT, 6])
        mv = sb("mv", [P, 2, IT, 2])
        veps = sb("veps", [P, 2, IT])
        rstd = sb("rstd", [P, 2, IT])
        xn = sb("xn", [P, 2, IT, D])
        xnT = sb("xnT", [P, 2, S])
        lg = sb("lg", [P, IT, E + PAD])
        top = sb("top", [P, IT, 8])
        match = sb("match", [P, IT, 8])
        rep = sb("rep", [P, IT, E + PAD])
        chosen = sb("chosen", [P, IT, E])
        diff = sb("diff", [P, IT])
        th = sb("th", [P, IT])
        w2 = sb("w2", [P, IT])
        ez = sb("ez", [P, IT, E])
        cw = sb("cw", [P, IT, E])
        split = sb("split", [P, IT, 2 * E], F32R)
        combT = sb("combT", [2 * E, 2, S], F32R)
        xs = sb("xs", [P, 4, S])
        tanh = sb("tanh", [P, NHG, S])
        gated = sb("gated", [P, 2, S])
        scaled = sb("scaled", [P, 2, S])
        hid = sb("hid", [P, NHID, S])
        outT = sb("outT", [P, S])

        bank = [ctx.enter_context(nc.psum_tensor(f"{tag}bank{i}", [P, BANK], F32)) for i in range(8)]
        hg, bc, acc, misc, route = bank[0:3], bank[3:5], bank[5], bank[6], bank[7]

        weights, consts = sem("weights"), sem("consts")
        bn_raw, bn_mean, var_ready = sem("bn_raw"), sem("bn_mean"), sem("var_ready")
        half_set, rstd_ready = sem("half_set"), sem("rstd_ready")
        xn_ready, xT_full, xT_read = sem("xn_ready"), sem("xT_full"), sem("xT_read")
        logits_full, logits_read = sem("logits_full"), sem("logits_read")
        gate_in, gate_out = sem("gate_in"), sem("gate_out")
        chain, split_ready = sem("chain"), sem("split_ready")
        combT_full, combT_read = sem("combT_full"), sem("combT_read")
        bc_full, bc_read = sem("bc_full"), sem("bc_read")
        hg_full, tanh_ready, gated_ready = sem("hg_full"), sem("tanh_ready"), sem("gated_ready")
        scaled_ready, hid_ready, hid_used = sem("scaled_ready"), sem("hid_ready"), sem("hid_used")
        outT_read, out_full, x_new = sem("outT_read"), sem("out_full"), sem("x_new")

        block = ctx.enter_context(nc.Block())

        def scaled_block(i):
            return i < blocks - shared

        @block.sync
        def _(sp):
            for dst, name in ((Wr, "Wr"), (selF, "sel"), (Wg, "Wg"), (Wu, "Wu"), (Wd, "Wd")):
                sp.dma_start(dst[:], d[tag + name]).then_inc(weights, 16)
            sp.wait_ge(weights, 16 * 5)

        @block.gpsimd
        def _(pool):
            nc.gpsimd.memset(half[:], -0.5).then_inc(half_set, 1)
            pool.wait_ge(half_set, 1)
            for b in range(B):
                pool.wait_ge(var_ready, b + 1)
                after(pool, xn_ready, b - 1)
                nc.gpsimd.tensor_tensor(rstd[:, b % 2, :], veps[:, b % 2, :], half[:], ALU.pow).then_inc(rstd_ready, 1)

        @block.vector
        def _(dve):
            nc.vector.memset(lg[:], LOWEST).then_inc(consts, 1)
            nc.vector.memset(match[:], LOWEST).then_inc(consts, 1)
            dve.wait_ge(weights, 16 * 5)
            nc.vector.tensor_copy(sel[:], selF[:]).then_inc(consts, 1)
            dve.wait_ge(consts, 3)
            links = [0]

            def link(ins):
                links[0] += 1
                ins.then_inc(chain, 1)
                dve.wait_ge(chain, links[0])

            def statistics(b, p):
                after(dve, rstd_ready, b - 1)
                for t in range(IT):
                    ins = nc.vector.bn_stats(stats[:, p, t, :], tokens(X, b, t))
                ins.then_inc(bn_raw, 1)
                dve.wait_ge(bn_raw, b + 1)
                for t in range(IT):
                    ins = nc.vector.bn_aggr(mv[:, p, t, :], stats[:, p, t, :])
                ins.then_inc(bn_mean, 1)
                dve.wait_ge(bn_mean, b + 1)
                nc.vector.tensor_scalar(veps[:, p, :], mv[:, p, :, 1], EPS, None, ALU.add).then_inc(var_ready, 1)

            def normalize(b, p):
                dve.wait_ge(rstd_ready, b + 1)
                after(dve, xT_full, b - 1)
                for t in range(IT):
                    ins = nc.vector.tensor_scalar(xn[:, p, t, :], tokens(X, b, t), mv[:, p, t, 0:1],
                                                  rstd[:, p, t:t + 1], ALU.subtract, ALU.mult)
                ins.then_inc(xn_ready, 1)

            def choose():
                for t in range(IT):
                    ins = nc.vector.max(top[:, t, :], lg[:, t, 0:E])
                link(ins)
                link(nc.vector.tensor_copy(match[:, :, 0:2], top[:, :, 0:2]))
                for t in range(IT):
                    ins = nc.vector.match_replace(rep[:, t, :], match[:, t, :], lg[:, t, :], -LOWEST)
                link(ins)
                link(nc.vector.tensor_tensor(chosen[:], rep[:, :, 0:E], lg[:, :, 0:E], ALU.not_equal))

            def wide(x):
                return x.unsqueeze(2).to_broadcast([P, IT, E])

            def route_start(b, p):
                dve.wait_ge(logits_full, b + 1)
                z = route[:, 0:IT * E].rearrange("p (t e) -> p t e", e=E)
                if n_scaled:
                    ins = nc.vector.tensor_copy(lg[:, :, 0:E], z)
                    ins.then_inc(logits_read, 1)
                    dve.wait_ge(logits_read, b + 1)
                    choose()
                    nc.vector.tensor_tensor(diff[:], top[:, :, 0], top[:, :, 1], ALU.subtract).then_inc(gate_in, 1)

            def route_end(b, p):
                dve.wait_ge(gate_out, b + 1)
                if n_scaled:
                    link(nc.vector.tensor_scalar(w2[:], th[:], -0.25, 0.25, ALU.mult, ALU.add))
                    link(nc.vector.tensor_tensor(cw[:], lg[:, :, 0:E], wide(top[:, :, 0]), ALU.is_ge))
                    link(nc.vector.tensor_tensor(cw[:], cw[:], wide(th[:]), ALU.mult))
                    link(nc.vector.tensor_scalar(cw[:], cw[:], 0.5, None, ALU.mult))
                    link(nc.vector.tensor_tensor(cw[:], cw[:], wide(w2[:]), ALU.add))
                    link(nc.vector.tensor_tensor(cw[:], cw[:], chosen[:], ALU.mult))
                else:
                    link(nc.vector.tensor_scalar(ez[:], ez[:], 1.0, None, ALU.add))
                    link(nc.vector.reciprocal(lg[:, :, 0:E], ez[:]))
                    choose()
                    link(nc.vector.tensor_tensor(diff[:], top[:, :, 0], top[:, :, 1], ALU.add))
                    link(nc.vector.tensor_scalar(diff[:], diff[:], 1e-20, None, ALU.add))
                    link(nc.vector.reciprocal(w2[:], diff[:]))
                    link(nc.vector.tensor_tensor(cw[:], lg[:, :, 0:E], chosen[:], ALU.mult))
                    link(nc.vector.tensor_tensor(cw[:], cw[:], wide(w2[:]), ALU.mult))
                    link(nc.vector.tensor_scalar(cw[:], cw[:], 0.5 * 2.5, None, ALU.mult))
                after(dve, combT_full, b)
                link(nc.vector.tensor_copy(split[:, :, 0:E], cw[:]))
                nc.vector.tensor_tensor(split[:, :, E:2 * E], cw[:], split[:, :, 0:E].bitcast(F32),
                                        ALU.subtract).then_inc(split_ready, 1)

            def scale_input(b, p, q):
                n = pairs * b + q
                dve.wait_ge(bc_full, n + 1)
                after(dve, hg_full, blocks * b + per_pair * (q - 1))
                nc.vector.tensor_tensor(
                    xs[:, 2 * (q % 2):2 * (q % 2) + 2, :], bc[n % 2][:].rearrange("p (e s) -> p e s", s=S),
                    xnT[:, p, :].unsqueeze(1).to_broadcast([P, 2, S]), ALU.mult).then_inc(bc_read, 1)

            def hidden(b, i):
                n = blocks * b + i
                ps = hg[n % NHG]
                dve.wait_ge(tanh_ready, n + 1)
                after(dve, hid_ready, n - 1)
                nc.vector.scalar_tensor_tensor(gated[:, n % 2, :], tanh[:, n % NHG, :], 1.0, ps[:, 0:S],
                                               ALU.add, ALU.mult).then_inc(gated_ready, 1)
                dve.wait_ge(gated_ready, n + 1)
                after(dve, hid_used, n - NHID + 1)
                if n_scaled or not scaled_block(i):
                    nc.vector.scalar_tensor_tensor(hid[:, n % NHID, :], gated[:, n % 2, :], 1.0 if n_scaled else 0.5,
                                                   ps[:, S:2 * S], ALU.mult, ALU.mult).then_inc(hid_ready, 1)
                else:
                    m = (blocks - shared) * b + i
                    nc.vector.tensor_tensor(scaled[:, m % 2, :], gated[:, n % 2, :], ps[:, S:2 * S],
                                            ALU.mult).then_inc(scaled_ready, 1)
                    dve.wait_ge(scaled_ready, m + 1)
                    dve.wait_ge(bc_full, (pairs * b + i) // 2 + 1)
                    nc.vector.tensor_tensor(hid[:, n % NHID, :], scaled[:, m % 2, :],
                                            bc[m // 2 % 2][:, (m % 2) * S:(m % 2) * S + S],
                                            ALU.mult).then_inc(hid_ready, 1)

            def output(b):
                dve.wait_ge(out_full, b + 1)
                nc.vector.tensor_tensor(tokens(X, b, 0, IT), tokens(X, b, 0, IT), misc[:, 0:S],
                                        ALU.add).then_inc(x_new, 1)

            statistics(0, 0)
            normalize(0, 0)
            route_start(0, 0)
            route_end(0, 0)
            for b in range(B):
                p = b % 2
                if n_scaled:
                    scale_input(b, p, 0)
                for i in range(blocks):
                    if n_scaled and i % per_pair == 0 and i // per_pair + 1 < pairs:
                        scale_input(b, p, i // per_pair + 1)
                    hidden(b, i)
                    if b + 1 < B:
                        if i == 0:
                            statistics(b + 1, 1 - p)
                            normalize(b + 1, 1 - p)
                        if i == 3:
                            route_start(b + 1, 1 - p)
                        if i == 5:
                            route_end(b + 1, 1 - p)
                    if i == 1 and b >= 1:
                        output(b - 1)
            output(B - 1)

        @block.scalar
        def _(act):
            def xT(b, p):
                act.wait_ge(xT_full, b + 1)
                if b >= 2:
                    act.wait_ge(hg_full, blocks * (b - 1))
                    if n_scaled:
                        act.wait_ge(bc_read, pairs * (b - 1))
                nc.scalar.copy(xnT[:, p, :], misc[:, S:2 * S]).then_inc(xT_read, 1)

            def gate(b):
                if n_scaled:
                    act.wait_ge(gate_in, b + 1)
                    nc.scalar.activation(th[:], diff[:], ACT.Tanh, scale=0.5).then_inc(gate_out, 1)
                else:
                    act.wait_ge(logits_full, b + 1)
                    after(act, split_ready, b)
                    nc.scalar.activation(ez[:].rearrange("p t e -> p (t e)"), route[:, 0:IT * E], ACT.Exp,
                                         scale=-1.0).then_inc(gate_out, 1)

            def comb(b, p):
                act.wait_ge(combT_full, b + 1)
                if b >= 2:
                    act.wait_ge(bc_full, (pairs if n_scaled else pairs // 2) * (b - 1))
                nc.scalar.copy(combT[:, p, :], route[0:2 * E, S:2 * S]).then_inc(combT_read, 1)

            def tanhs(b, i):
                n = blocks * b + i
                act.wait_ge(hg_full, n + 1)
                after(act, gated_ready, n - NHG + 1)
                nc.scalar.activation(tanh[:, n % NHG, :], hg[n % NHG][:, 0:S], ACT.Tanh, scale=0.5).then_inc(tanh_ready, 1)

            def out(b):
                act.wait_ge(hid_used, blocks * (b + 1))
                after(act, out_full, b)
                nc.scalar.copy(outT[:], acc[:, 0:S]).then_inc(outT_read, 1)

            xT(0, 0)
            gate(0)
            comb(0, 0)
            for b in range(B):
                for i in range(blocks):
                    tanhs(b, i)
                    if i == 1 and b >= 1:
                        out(b - 1)
                    if b + 1 < B:
                        if i == 2:
                            xT(b + 1, 1 - b % 2)
                        if i == 5:
                            gate(b + 1)
                        if i == 7:
                            comb(b + 1, 1 - b % 2)
            out(B - 1)

        @block.tensor
        def _(pe):
            pe.wait_ge(weights, 16 * 5)
            pe.wait_ge(consts, 3)

            def xT(b, p):
                pe.wait_ge(xn_ready, b + 1)
                after(pe, xT_read, b)
                after(pe, x_new, b - 1)
                for t in range(IT):
                    ins = nc.tensor.transpose(misc[:, S + t * P:S + t * P + P], xn[:, p, t, :], ident[:])
                ins.then_inc(xT_full, 1)

            def logits(b, p):
                pe.wait_ge(xT_read, b + 1)
                after(pe, combT_read, b)
                for t in range(IT):
                    ins = nc.tensor.matmul(route[:, t * E:t * E + E], xnT[:, p, t * P:t * P + P], Wr[:],
                                           start=True, stop=True)
                ins.then_inc(logits_full, 1)

            def comb(b, p):
                pe.wait_ge(split_ready, b + 1)
                for t in range(IT):
                    ins = nc.tensor.transpose(route[0:2 * E, S + t * P:S + t * P + P], split[:, t, :].bitcast(F32),
                                              ident[:])
                ins.then_inc(combT_full, 1)

            def spread(b, p, q):
                n = (pairs if n_scaled else pairs // 2) * b + q
                pe.wait_ge(combT_read, b + 1)
                if n_scaled:
                    after(pe, bc_read, n - 1)
                else:
                    after(pe, hid_ready, hid_count(n - 2))
                for j in range(2):
                    w = sel[:, q, j, :] if n_scaled else sel[:, 2 * q + j, 0, :]
                    ins = nc.tensor.matmul(bc[n % 2][:, j * S:j * S + S], w, combT[:, p, :], start=True, stop=True)
                ins.then_inc(bc_full, 1)

            def hid_count(n):
                if n < 0:
                    return 0
                return blocks * (n // (pairs // 2)) + 2 * (n % (pairs // 2)) + 2

            def up(b, p, i):
                n = blocks * b + i
                ps = hg[n % NHG]
                after(pe, hid_ready if n_scaled else hid_ready, n - NHG + 1)
                nc.tensor.matmul(ps[:, 0:S], Wg[:, i, :], xnT[:, p, :], start=True, stop=True)
                if not n_scaled:
                    nc.tensor.matmul(ps[:, S:2 * S], Wu[:, i, :], xnT[:, p, :], start=True, stop=True).then_inc(hg_full, 1)
                    return
                q, part = i // per_pair, i % per_pair
                pe.wait_ge(bc_read, pairs * b + q + 1)
                s0 = 2 * (q % 2)
                if part < 2:
                    nc.tensor.matmul(ps[:, S:2 * S], Wu[:, i, :], xs[:, s0 + part, :], start=True,
                                     stop=True).then_inc(hg_full, 1)
                else:
                    nc.tensor.matmul(ps[0:64, S:2 * S], Wu[:, i, 0:64], xs[:, s0, :], start=True, stop=True)
                    nc.tensor.matmul(ps[64:P, S:2 * S], Wu[:, i, 64:P], xs[:, s0 + 1, :], start=True,
                                     stop=True).then_inc(hg_full, 1)

            def down(b, i):
                n = blocks * b + i
                pe.wait_ge(hid_ready, n + 1)
                if i == 0:
                    after(pe, outT_read, b)
                nc.tensor.matmul(acc[:, 0:S], Wd[:, i, :], hid[:, n % NHID, :], start=(i == 0),
                                 stop=(i == blocks - 1)).then_inc(hid_used, 1)

            def out(b):
                pe.wait_ge(outT_read, b + 1)
                after(pe, x_new, b)
                for t in range(IT):
                    ins = nc.tensor.transpose(misc[:, t * P:t * P + P], outT[:, t * P:t * P + P], ident[:])
                ins.then_inc(out_full, 1)

            xT(0, 0)
            logits(0, 0)
            comb(0, 0)
            LAG = 2
            fills = pairs if n_scaled else pairs // 2
            step = blocks // fills
            for b in range(B):
                p = b % 2
                spread(b, p, 0)
                for i in range(blocks + LAG):
                    if i < blocks:
                        if i % step == 0 and i // step + 1 < fills:
                            spread(b, p, i // step + 1)
                        up(b, p, i)
                    if i >= LAG:
                        down(b, i - LAG)
                    if b + 1 < B:
                        if i == 3:
                            xT(b + 1, 1 - p)
                        if i == 4:
                            logits(b + 1, 1 - p)
                        if i == 8:
                            comb(b + 1, 1 - p)
                    if i == 2 and b >= 1:
                        out(b - 1)
            out(B - 1)


def expert_pairs(w):
    w = w.transpose(1, 0, 2).reshape(D, -1, 2, w.shape[2])
    rest = w[..., P:].reshape(D, w.shape[1], 1, P)
    return np.ascontiguousarray(np.concatenate([w[..., :P], rest], 2).reshape(D, -1, P))


def selectors(E, half_blocks):
    out = np.zeros((2, E, E // 2, 2, P), np.float32)
    for e in range(E):
        out[:, e, e // 2, e % 2] = 1.0
    if half_blocks:
        half = np.zeros((2, E, E // 2, 1, P), np.float32)
        for j in range(2):
            half[:, :, :, 0, j * P // 2:(j + 1) * P // 2] = out[:, :, :, j, 0:P // 2]
        out = half
    return out.reshape((2 * E,) + out.shape[2:])


def quadrants(w):
    w = w.reshape(G, HH, DH, -1)
    out = np.zeros((w.shape[-1], G, HH, QUAD), np.float32)
    for r in range(3):
        out[:, :, :, r * DH:(r + 1) * DH] = w.transpose(3, 0, 1, 2)
    return out.reshape(w.shape[-1], G, P)


def low_rows(r):
    out = np.zeros((HH, QUAD), np.float32)
    out[:, r * DH:(r + 1) * DH] = -1.0
    return out.reshape(P)


def er_quadrants(Er):
    out = np.zeros((HH, QUAD, HH, S), np.float32)
    for hh in range(HH):
        for r in range(3):
            out[hh, r * DH:(r + 1) * DH, hh] = Er.T
    return out.reshape(P, HH, S)


def xattn_ffn_twice_kernel(nc, x, out, **d):
    rel = nc.dram_tensor("relative_scores", [2, H, S, PITCH], F32).ap()
    with ExitStack() as ctx:
        X = ctx.enter_context(nc.sbuf_tensor("X", [P, B * IT * D], F32))
        ident = ctx.enter_context(nc.sbuf_tensor("identity", [P, P], F32))
        stored = ctx.enter_context(nc.semaphore("stored"))
        relative_attention(nc, X, ident, x, d, rel)
        experts(nc, X, ident, d, "m0_", 8, 12, 0, True)
        attention(nc, X, ident, d)
        experts(nc, X, ident, d, "m1_", 16, 9, 1, False)
        block = ctx.enter_context(nc.Block())

        @block.sync
        def _(sp):
            sp.dma_start(out.rearrange("(t p) d -> p t d", p=P),
                         X[:].rearrange("p (t d) -> p t d", d=D)).then_inc(stored, 16)
            sp.wait_ge(stored, 16)


def laid_out(inputs):
    def quad_bias(b):
        return quadrants(b[:, None])[0].T

    def halves(w, ws):
        blocks = np.zeros((D, E1 // 2 + 1, P), np.float32)
        blocks[:, :-1] = w.transpose(1, 0, 2).reshape(D, E1 // 2, P)
        blocks[:, -1, :P // 2] = ws
        return blocks

    i = inputs
    E0, E1 = i["L0_ffn_Wr"].shape[1], i["L1_ffn_gate_w"].shape[0]
    bk1 = quad_bias(i["L1_xattn_bk"]).copy()
    bk1[MAXROW::QUAD] = 1.0
    return dict(
        x=i["x"].reshape(B * S, D), ctxT=i["ctx_1024"].reshape(B * S, D).T,
        ident=np.eye(P, dtype=np.float32), lo=np.stack([low_rows(1), low_rows(2)], 1),
        WqR0=quadrants(i["L0_xattn_Wq"]), bqR0=quad_bias(i["L0_xattn_bq"]),
        WkR0=quadrants(i["L0_xattn_Wk"]), bkR0=quad_bias(i["L0_xattn_bk"]),
        WvT0=i["L0_xattn_Wv"].T, bv0=i["L0_xattn_bv"], ErR=er_quadrants(i["L0_xattn_Er"]),
        m0_Wr=i["L0_ffn_Wr"], m0_sel=selectors(E0, False), m0_Wg=expert_pairs(i["L0_ffn_W1"]),
        m0_Wu=expert_pairs(i["L0_ffn_W3"]),
        m0_Wd=expert_pairs(i["L0_ffn_W2"].transpose(0, 2, 1)).transpose(2, 1, 0),
        WqR1=quadrants(i["L1_xattn_Wq"]), bqR1=quad_bias(i["L1_xattn_bq"]),
        WkR1=quadrants(i["L1_xattn_Wk"]), bkR1=bk1,
        WvT1=i["L1_xattn_Wv"].T, bv1=i["L1_xattn_bv"], WoT1=i["L1_xattn_Wo"].T, bo1=i["L1_xattn_bo"],
        m1_Wr=i["L1_ffn_gate_w"].T, m1_sel=selectors(E1, True),
        m1_Wg=halves(i["L1_ffn_w_gate"], i["L1_ffn_ws_gate"]),
        m1_Wu=halves(i["L1_ffn_w_up"], i["L1_ffn_ws_up"]),
        m1_Wd=halves(i["L1_ffn_w_down"].transpose(0, 2, 1), i["L1_ffn_ws_down"].T).transpose(2, 1, 0))


def kernel(**inputs):
    import numpy as _np
    import concourse.bacc as _bacc
    from concourse import mybir as _mybir
    from concourse.bass_utils import run_bass_kernel_spmd as _run

    nc = _bacc.Bacc("TRN2", target_bir_lowering=False, num_devices=1)
    arrays, args = {}, {}
    for name, a in laid_out({k: _np.asarray(v) for k, v in inputs.items()}).items():
        a = _np.ascontiguousarray(a)
        arrays[f"in_{name}_dram"] = a
        args[name] = nc.dram_tensor(f"in_{name}_dram", a.shape, _mybir.dt.from_np(a.dtype), kind="ExternalInput").ap()
    out = nc.dram_tensor("out_0_dram", (B * S, D), F32, kind="ExternalOutput").ap()
    xattn_ffn_twice_kernel(nc, out=out, **args)
    r = _run(nc, [arrays], core_ids=[0])
    return r.results[0]["out_0_dram"].reshape(B, S, D)
```

```python
from contextlib import ExitStack

import numpy as np
import concourse.bass as bass
from concourse import mybir

F32 = mybir.dt.float32
F32R = mybir.dt.float32r
ALU = mybir.AluOpType
ACT = mybir.ActivationFunctionType
AX = mybir.AxisListType

P = 128
B, S, D = 8, 256, 128
H, DH = 16, 8
HH = 4
G = H // HH
QUAD = P // HH
IT = S // P
EPS = 1e-5
SCALE = float(DH) ** -0.5
MASKED = -1.0e30
LOWEST = -3.0e38
BANK = 512
PITCH = S + P
MAXROW = 3 * DH


def after(eng, sem, count):
    if not (isinstance(count, int) and count <= 0):
        eng.wait_ge(sem, count)



def rest_of(program):
    for _ in program:
        pass


def run_block(nc, ctx, programs):
    block = ctx.enter_context(nc.Block())

    @block.sync
    def _(sp):
        rest_of(programs["sync"])

    @block.gpsimd
    def _(pool):
        rest_of(programs["gpsimd"])

    @block.vector
    def _(dve):
        rest_of(programs["vector"])

    @block.scalar
    def _(act):
        rest_of(programs["scalar"])

    @block.tensor
    def _(pe):
        rest_of(programs["tensor"])


def tokens(X, b, t=0, n=1):
    return X[:, bass.ds(b * S + t * D, n * D)]


def relative_attention(nc, X, ident, bank, x_dram, d, rel, ahead):
    with ExitStack() as ctx:
        def sb(name, shape, dt=F32):
            return ctx.enter_context(nc.sbuf_tensor("a0_" + name, shape, dt))

        def sem(name):
            return ctx.enter_context(nc.semaphore("a0_" + name))

        ctxT = sb("ctxT", [P, 2, S])
        WqR = sb("WqR", [P, G, P])
        WkR = sb("WkR", [P, G, P])
        WvT = sb("WvT", [P, D])
        bqR = sb("bqR", [P, G])
        bkR = sb("bkR", [P, G])
        lo = sb("lo", [P, 2])
        bv = sb("bv", [1, D])
        ones = sb("ones", [1, P])
        table = sb("table", [1, 1])
        ErM = sb("ErM", [P, HH, S], F32R)
        mask = sb("mask", [P, P])
        half = sb("half", [P, IT])
        stats = sb("stats", [P, 2, IT, 6])
        mv = sb("mv", [P, 2, IT, 2])
        veps = sb("veps", [P, 2, IT])
        rstd = sb("rstd", [P, 2, IT])
        xn = sb("xn", [P, 2, IT, D])
        xnT = sb("xnT", [P, 2, S])
        full = sb("full", [P, 2, 2, S])
        high = sb("high", [P, 2, 2, S], F32R)
        qst = sb("qst", [P, 2, G, S], F32R)
        kst = sb("kst", [P, G, S], F32R)
        kmask = sb("kmask", [P, 2, HH, G, S], F32R)
        vaug = sb("vaug", [P, 2, IT, H, QUAD])
        qe = sb("qe", [P, 4, HH, S])
        tr = sb("tr", [P, G, HH, P + S])
        T = sb("T", [P, 2, HH, P + S])
        rowmax = sb("rowmax", [P, 2, IT, HH])
        Tm = sb("Tm", [P, 2, HH, P + S])
        PT = sb("PT", [P, 2, IT, HH, S])
        OT = sb("OT", [P, G, S])
        rden = sb("rden", [P, IT, H])
        att = sb("att", [P, IT, D])

        ring, outp, scb, ttb = bank[0:2], bank[2:4], bank[4:6], bank[6:8]

        weights = sem("weights")
        extras, wv_in, er_in, ones_set = sem("extras"), sem("wv_in"), sem("er_in"), sem("ones_set")
        mask_set, kmask_zero, vaug_set, er_ready = sem("mask_set"), sem("kmask_zero"), sem("vaug_set"), sem("er_ready")
        x_in = [sem("x_in0"), sem("x_in1")]
        ctx_in = [sem("ctx_in0"), sem("ctx_in1")]
        er_high = sem("er_high")
        mask_rows_out = [sem("mask_rows_out0"), sem("mask_rows_out1")]
        bn_raw, bn_mean, var_ready = sem("bn_raw"), sem("bn_mean"), sem("var_ready")
        half_set, rstd_ready = sem("half_set"), sem("rstd_ready")
        xn_ready = sem("xn_ready")
        ring_full, ring_read = sem("ring_full"), sem("ring_read")
        high_ready, stack_ready = sem("high_ready"), sem("stack_ready")
        kmask_in = sem("kmask_in")
        qe_out = [sem(f"qe_out{i}") for i in range(4)]
        tr_in = [sem(f"tr_in{g}") for g in range(G)]
        sc_full, t_ready, tm_ready = sem("sc_full"), sem("t_ready"), sem("tm_ready")
        tt_full, pt_ready, pv_done = sem("tt_full"), sem("pt_ready"), sem("pv_done")
        ot_ready, o_full, rden_ready, att_ready, x_new = (
            sem("ot_ready"), sem("o_full"), sem("rden_ready"), sem("att_ready"), sem("x_new"))

        XT, CHUNK, RELATIVE, VALUES, FILLS = 0, 1, 5, 5 + 3 * G, 6 + 3 * G

        def bank_of(fill):
            return ring[fill % 2]

        block = ctx.enter_context(nc.Block())

        @block.sync
        def _(sp):
            x_tiles = x_dram.rearrange("(t p) d -> p t d", p=P)
            X_tiles = X[:].rearrange("p (t d) -> p t d", d=D)
            sp.dma_start(X_tiles[:, 0:IT], x_tiles[:, 0:IT]).then_inc(x_in[0], 16)
            sp.dma_start(WqR[:], d["WqR0"]).then_inc(weights, 16)
            sp.dma_start(WkR[:], d["WkR0"]).then_inc(extras, 16)
            sp.dma_start(ctxT[:, 0, :], d["ctxT"][:, 0:S]).then_inc(ctx_in[0], 16)
            sp.dma_start(ctxT[:, 1, :], d["ctxT"][:, S:2 * S]).then_inc(ctx_in[1], 16)
            sp.dma_start(WvT[:], d["WvT0"]).then_inc(wv_in, 16)
            sp.dma_start(bv[:], d["bv0"].unsqueeze(0)).then_inc(wv_in, 16)

            def mask_rows(p, groups):
                for g in groups:
                    sp.dma_start(
                        rel[p, HH * g:HH * g + HH, :, S:PITCH].rearrange("h (t i) l -> i (h t) l", i=P),
                        mask[:].unsqueeze(1).to_broadcast([P, HH * IT, P])).then_inc(mask_rows_out[p], 16)

            def keys(b, p):
                sp.wait_ge(stack_ready, 4 * b + 4)
                sp.wait_ge(kmask_zero, 2)
                after(sp, sc_full, 12 * (b - 1))
                for hh in range(HH):
                    q = slice(QUAD * hh, QUAD * hh + QUAD)
                    sp.dma_start(kmask[q, p, hh, :, :].bitcast(F32), kst[q, :, :].bitcast(F32)
                                  ).then_inc(kmask_in, 16)

            def rows_out(b, p, g):
                for t in range(IT):
                    n = (2 * g + t) % 4
                    l0 = S - P * (t + 1)
                    sp.wait_ge(ring_read, FILLS * b + RELATIVE + 3 * g + 1 + 2 * t)
                    after(sp, t_ready, 12 * (b - 2) + 3 * g + 3)
                    sp.dma_start(
                        rel[p, HH * g:HH * g + HH, P * t:P * t + P, l0:S].rearrange("h i l -> i h l"),
                        qe[:, n, :, l0:S]).then_inc(qe_out[n], 16)

            def rows_in(b, p, g):
                for t in range(IT):
                    sp.wait_ge(qe_out[(2 * g + t) % 4], 16 * (2 * b + g // 2 + 1))
                sp.wait_ge(mask_rows_out[p], 16 * (G // 2 if b == 1 and g < G // 2 else G))
                after(sp, t_ready, 12 * (b - 1) + 3 * g + 3)
                for t in range(IT):
                    i0 = P * t
                    at = rel[p, HH * g, i0:i0 + 1, S - 1 - i0:S]
                    src = bass.AP(tensor=at.tensor, offset=at.offset,
                                  ap=[[PITCH - 1, P], [S * PITCH, HH], [1, P * (t + 1)]])
                    dst = tr[:, g, :, 0:P] if t == 0 else tr[:, g, :, P:P + S]
                    sp.dma_start(dst, src).then_inc(tr_in[g], 16)

            def scores_ahead(b, p):
                rows_out(b, p, 0)
                rows_out(b, p, 1)
                rows_in(b, p, 0)
                keys(b, p)
                rows_out(b, p, 2)
                rows_in(b, p, 1)
                if b == 1:
                    mask_rows(1, range(G // 2, G))
                rows_out(b, p, 3)
                rows_in(b, p, 2)
                rows_in(b, p, 3)

            sp.wait_ge(mask_set, 1)
            mask_rows(0, range(G))
            sp.dma_start(X_tiles[:, IT:], x_tiles[:, IT:]).then_inc(x_in[1], 16)
            mask_rows(1, range(G // 2))
            scores_ahead(0, 0)
            for b in range(B - 1):
                p = b % 2
                if b + 2 < B:
                    sp.wait_ge(ring_read, FILLS * b + VALUES + 1)
                    sp.dma_start(ctxT[:, p, :], d["ctxT"][:, bass.ds((b + 2) * S, S)]).then_inc(ctx_in[p], 16)
                scores_ahead(b + 1, 1 - p)
                if b == B - 3:
                    next(ahead["sync"])

        @block.gpsimd
        def _(pool):
            nc.gpsimd.memset(mask[:], MASKED).then_inc(mask_set, 1)
            nc.gpsimd.memset(half[:], -0.5).then_inc(half_set, 1)
            pool.dma_start(qe[:, 0], d["ErR"]).then_inc(er_in, 16)
            nc.gpsimd.memset(vaug[:], 0.0).then_inc(vaug_set, 1)
            pool.wait_ge(vaug_set, 1)
            nc.gpsimd.memset(vaug[:, :, :, :, DH:DH + 1], 1.0).then_inc(vaug_set, 1)
            pool.wait_ge(half_set, 1)

            def inverse_deviation(b, p):
                pool.wait_ge(var_ready, b + 1)
                after(pool, xn_ready, b - 1)
                nc.gpsimd.tensor_tensor(rstd[:, p, :], veps[:, p, :], half[:], ALU.pow).then_inc(rstd_ready, 1)

            def less_max(b, g):
                u = 4 * b + g
                after(pool, tt_full, 3 * (u - 1))
                for t in range(IT):
                    c = slice(0, P) if t == 0 else slice(P, P + S)
                    pool.wait_ge(t_ready, 3 * u + 1 + 2 * t)
                    nc.gpsimd.tensor_tensor(
                        Tm[:, g % 2, :, c], T[:, g % 2, :, c],
                        rowmax[:, g % 2, t, :].unsqueeze(2).to_broadcast([P, HH, P * (t + 1)]),
                        ALU.subtract).then_inc(tm_ready, 1)

            inverse_deviation(0, 0)
            for p in range(2):
                nc.gpsimd.memset(kmask[:, p].bitcast(F32), 0.0).then_inc(kmask_zero, 1)
            inverse_deviation(1, 1)
            for b in range(B):
                for g in range(G):
                    less_max(b, g)
                    if g == 1 and b + 2 < B:
                        inverse_deviation(b + 2, b % 2)
                    if g == 1 and b >= B - 2:
                        next(ahead["gpsimd"])

        @block.vector
        def _(dve):
            def statistics(b, p):
                dve.wait_ge(x_in[min(b, 1)], 16 if b else 32)
                after(dve, rstd_ready, b - 1)
                for t in range(IT):
                    ins = nc.vector.bn_stats(stats[:, p, t, :], tokens(X, b, t))
                ins.then_inc(bn_raw, 1)
                dve.wait_ge(bn_raw, b + 1)
                for t in range(IT):
                    ins = nc.vector.bn_aggr(mv[:, p, t, :], stats[:, p, t, :])
                ins.then_inc(bn_mean, 1)
                dve.wait_ge(bn_mean, b + 1)
                nc.vector.tensor_scalar(veps[:, p, :], mv[:, p, :, 1], EPS, None, ALU.add).then_inc(var_ready, 1)

            def normalize(b, p):
                dve.wait_ge(rstd_ready, b + 1)
                after(dve, ring_full, FILLS * (b - 2) + XT + 1)
                for t in range(IT):
                    ins = nc.vector.tensor_scalar(xn[:, p, t, :], tokens(X, b, t), mv[:, p, t, 0:1],
                                                  rstd[:, p, t:t + 1], ALU.subtract, ALU.mult)
                ins.then_inc(xn_ready, 1)

            def stack(b, p, c):
                n = 4 * b + c
                dve.wait_ge(ring_read, FILLS * b + CHUNK + c + 1)
                after(dve, stack_ready, n - 1)
                nc.vector.tensor_copy(high[:, c % 2], full[:, c % 2]).then_inc(high_ready, 1)
                dve.wait_ge(high_ready, n + 1)
                to = (qst[:, p] if c < 2 else kst[:])[:, 2 * (c % 2):2 * (c % 2) + 2, :]
                if c < 2:
                    after(dve, sc_full, 12 * (b - 1))
                else:
                    after(dve, kmask_in, 64 * b)
                nc.vector.scalar_tensor_tensor(
                    to, high[:, c % 2].bitcast(F32), lo[:, c // 2:c // 2 + 1], full[:, c % 2],
                    ALU.mult, ALU.add).then_inc(stack_ready, 1)

            def scores(b, p, g):
                u = 4 * b + g
                after(dve, tm_ready, 2 * (u - 1))
                dve.wait_ge(tr_in[g], 16 * IT * (b + 1))
                for f in range(3):
                    dve.wait_ge(sc_full, 3 * u + f + 1)
                    src = scb[(g + f) % 2]
                    for k in range(HH if f == 0 else 2):
                        hh = k if f == 0 else 2 * (f - 1) + k
                        n = P if f == 0 else S
                        c = slice(0, P) if f == 0 else slice(P, P + S)
                        ins = nc.vector.tensor_tensor_reduce(
                            out=T[:, g % 2, hh, c], in0=src[:, k * n:k * n + n], in1=tr[:, g, hh, c],
                            scale=1.0, scalar=LOWEST, op0=ALU.add, op1=ALU.max,
                            accum_out=rowmax[:, g % 2, min(f, 1), hh:hh + 1])
                    ins.then_inc(t_ready, 1)

            def output(b, p):
                after(dve, x_new, b)
                for t in range(IT):
                    dve.wait_ge(o_full, IT * b + t + 1)
                    o = outp[t][:].rearrange("p (h e) -> p h e", e=QUAD)
                    nc.vector.reciprocal(rden[:, t, :], o[:, :, DH]).then_inc(rden_ready, 1)
                    dve.wait_ge(rden_ready, IT * b + t + 1)
                    nc.vector.tensor_tensor(att[:, t, :].rearrange("p (h e) -> p h e", e=DH), o[:, :, 0:DH],
                                            rden[:, t, :].unsqueeze(2).to_broadcast([P, H, DH]),
                                            ALU.mult).then_inc(att_ready, 1)
                dve.wait_ge(att_ready, IT * b + IT)
                nc.vector.tensor_tensor(tokens(X, b, 0, IT), tokens(X, b, 0, IT),
                                        att[:].rearrange("p t d -> p (t d)"), ALU.add).then_inc(x_new, 1)

            nc.vector.memset(ones[:], 1.0).then_inc(ones_set, 1)
            statistics(0, 0)
            normalize(0, 0)
            dve.wait_ge(er_in, 16)
            erh = high[:].rearrange("p a b s -> p (a b s)")
            nc.vector.tensor_copy(erh, qe[:, 0].rearrange("p h s -> p (h s)")).then_inc(er_high, 1)
            dve.wait_ge(er_high, 1)
            dve.wait_ge(weights, 16 * 3)
            nc.vector.scalar_tensor_tensor(ErM[:].rearrange("p h s -> p (h s)"), erh.bitcast(F32), lo[:, 1:2],
                                           qe[:, 0].rearrange("p h s -> p (h s)"),
                                           ALU.mult, ALU.add).then_inc(er_ready, 1)
            dve.wait_ge(er_ready, 1)
            for c in range(4):
                stack(0, 0, c)
            statistics(1, 1)
            normalize(1, 1)
            for b in range(B):
                p = b % 2
                begun, more, further = b >= 1, b + 1 < B, b + 2 < B
                if more:
                    stack(b + 1, 1 - p, 0)
                scores(b, p, 0)
                if more:
                    stack(b + 1, 1 - p, 1)
                scores(b, p, 1)
                if more:
                    stack(b + 1, 1 - p, 2)
                    stack(b + 1, 1 - p, 3)
                if further:
                    statistics(b + 2, p)
                elif more:
                    dve.wait_ge(x_new, 2)
                    next(ahead["vector"])
                scores(b, p, 2)
                if further:
                    normalize(b + 2, p)
                if begun:
                    output(b - 1, 1 - p)
                scores(b, p, 3)
                if more and not further:
                    next(ahead["vector"])
            next(ahead["vector"])
            next(ahead["vector"])
            output(B - 1, 1)

        @block.scalar
        def _(act):
            act.dma_start(ident[:], d["ident"]).then_inc(x_in[0], 16)
            act.wait_ge(ones_set, 1)
            nc.scalar.activation(table[:], ones[:, 0:1], ACT.Exp)
            act.dma_start(lo[:], d["lo"]).then_inc(weights, 16)
            act.dma_start(bqR[:], d["bqR0"]).then_inc(weights, 16)
            act.dma_start(bkR[:], d["bkR0"]).then_inc(extras, 16)
            act.wait_ge(weights, 16 * 3)

            def read(b, fill):
                return act.wait_ge(ring_full, FILLS * b + fill + 1)

            def xT(b, p):
                read(b, XT)
                after(act, ring_full, FILLS * (b - 2) + CHUNK + 2)
                nc.scalar.copy(xnT[:, p, :], bank_of(XT)[:, 0:S]).then_inc(ring_read, 1)

            def chunk(b, c):
                read(b, CHUNK + c)
                after(act, stack_ready, 4 * b + c - 1)
                if c == 2:
                    act.wait_ge(extras, 16 * 2)
                for j in range(2):
                    g = 2 * (c % 2) + j
                    ins = nc.scalar.activation(full[:, c % 2, j, :], bank_of(CHUNK + c)[:, j * S:j * S + S],
                                               ACT.Identity, bias=(bqR if c < 2 else bkR)[:, g:g + 1])
                ins.then_inc(ring_read, 1)

            def values(b, p):
                read(b, VALUES)
                if b == 0:
                    act.wait_ge(vaug_set, 2)
                after(act, pv_done, 4 * (b - 1))
                nc.scalar.copy(vaug[:, p, :, :, 0:DH],
                               bank_of(VALUES)[:, 0:S].rearrange("p (t h e) -> p t h e", h=H, e=DH)
                               ).then_inc(ring_read, 1)

            def relative(b, g, fills):
                for f in fills:
                    t = min(f, 1)
                    n = (2 * g + t) % 4
                    fill = RELATIVE + 3 * g + f
                    read(b, fill)
                    after(act, qe_out[n], 16 * (2 * b + g // 2))
                    if b == 0 and g == 0:
                        act.wait_ge(er_ready, 1)
                    src = bank_of(fill)[:].rearrange("p (h l) -> p h l", l=P if f == 0 else S)
                    to = qe[:, n, :, P:S] if f == 0 else qe[:, n, 2 * (f - 1):2 * f, :]
                    nc.scalar.copy(to, src).then_inc(ring_read, 1)

            def exps(b, g, fills):
                u = 4 * b + g
                after(act, pv_done, u - 1)
                for f in fills:
                    act.wait_ge(tt_full, 3 * u + f + 1)
                    to = PT[:, g % 2, 0, :, 0:P] if f == 0 else PT[:, g % 2, f - 1, :, P:S]
                    nc.scalar.activation(to, ttb[(g + f) % 2][:].rearrange("p (h i) -> p h i", i=P), ACT.Exp,
                                         scale=SCALE).then_inc(pt_ready, 1)

            def oT(b, k):
                act.wait_ge(pv_done, 4 * b + 2 * k + 2)
                after(act, o_full, IT * b)
                nc.scalar.copy(OT[:, 2 * k:2 * k + 2, :], outp[k][:].rearrange("p (g i) -> p g i", i=S)
                               ).then_inc(ot_ready, 1)

            xT(0, 0)
            for c in range(4):
                chunk(0, c)
            for g in range(G):
                relative(0, g, range(3))
            values(0, 0)
            xT(1, 1)
            chunk(1, 0)
            chunk(1, 1)
            two, third = range(2), range(2, 3)
            for b in range(B):
                p = b % 2
                begun, more, further = b >= 1, b + 1 < B, b + 2 < B
                if begun:
                    oT(b - 1, 0)
                    exps(b - 1, 3, two)
                if more:
                    chunk(b + 1, 2)
                else:
                    next(ahead["scalar"])
                    next(ahead["scalar"])
                if begun:
                    exps(b - 1, 3, third)
                if more:
                    chunk(b + 1, 3)
                    relative(b + 1, 0, two)
                exps(b, 0, two)
                if more:
                    relative(b + 1, 0, third)
                exps(b, 0, third)
                if more:
                    relative(b + 1, 1, range(3))
                if begun:
                    oT(b - 1, 1)
                if more:
                    relative(b + 1, 2, two)
                exps(b, 1, two)
                if more:
                    relative(b + 1, 2, third)
                exps(b, 1, third)
                if more:
                    relative(b + 1, 3, two)
                exps(b, 2, two)
                if more:
                    relative(b + 1, 3, third)
                    values(b + 1, 1 - p)
                if further:
                    xT(b + 2, p)
                exps(b, 2, third)
                if further:
                    chunk(b + 2, 0)
                    chunk(b + 2, 1)
            oT(B - 1, 0)
            exps(B - 1, 3, range(3))
            next(ahead["scalar"])
            oT(B - 1, 1)
            next(ahead["scalar"])

        @block.tensor
        def _(pe):
            def fill(b, n):
                after(pe, ring_read, FILLS * b + n - 1)
                return bank_of(n)

            def xT(b, p):
                pe.wait_ge(xn_ready, b + 1)
                to = fill(b, XT)
                for t in range(IT):
                    ins = nc.tensor.transpose(to[:, t * P:t * P + P], xn[:, p, t, :], ident[:])
                ins.then_inc(ring_full, 1)

            def chunk(b, p, c):
                to = fill(b, CHUNK + c)
                if c == 0:
                    pe.wait_ge(ring_read, FILLS * b + XT + 1)
                if c == 2:
                    pe.wait_ge(ctx_in[p], 8 * (b - p) + 16)
                    if b == 0:
                        pe.wait_ge(extras, 16 * 2)
                for j in range(2):
                    g = 2 * (c % 2) + j
                    w, x = (WqR, xnT) if c < 2 else (WkR, ctxT)
                    ins = nc.tensor.matmul(to[:, j * S:j * S + S], w[:, g, :], x[:, p, :], start=True, stop=True)
                ins.then_inc(ring_full, 1)

            def values(b, p):
                to = fill(b, VALUES)
                for t in range(IT):
                    nc.tensor.matmul(to[:, t * P:t * P + P], ctxT[:, p, t * P:t * P + P], WvT[:],
                                     start=True, stop=False)
                    ins = nc.tensor.matmul(to[:, t * P:t * P + P], ones[:], bv[:], start=False, stop=True)
                ins.then_inc(ring_full, 1)

            def relative(b, p, g, fills):
                pe.wait_ge(stack_ready, 4 * b + g // 2 + 1)
                for f in fills:
                    to = fill(b, RELATIVE + 3 * g + f)
                    t = min(f, 1)
                    er = ErM[:, :, P:S] if f == 0 else ErM[:, 2 * (f - 1):2 * f, :]
                    nc.tensor.matmul(to[:], qst[:, p, g, t * P:t * P + P], er,
                                     start=True, stop=True).then_inc(ring_full, 1)

            def scores(b, p, g, fills):
                if g == 0:
                    pe.wait_ge(kmask_in, 64 * (b + 1))
                for f in fills:
                    n = 12 * b + 3 * g + f
                    after(pe, t_ready, n - 1)
                    t = min(f, 1)
                    k = kmask[:, p, :, g, 0:P] if f == 0 else kmask[:, p, 2 * (f - 1):2 * f, g, :]
                    nc.tensor.matmul(scb[(g + f) % 2][:], qst[:, p, g, t * P:t * P + P], k,
                                     start=True, stop=True).then_inc(sc_full, 1)

            def transposed(b, g, fills):
                u = 4 * b + g
                for f in fills:
                    pe.wait_ge(tm_ready, 2 * u + 1 + min(f, 1))
                    after(pe, pt_ready, 3 * u + f - 1)
                    for hh in range(HH):
                        ins = nc.tensor.transpose(ttb[(g + f) % 2][:, hh * P:hh * P + P],
                                                  Tm[:, g % 2, hh, f * P:f * P + P], ident[:])
                    ins.then_inc(tt_full, 1)

            def weighted(b, p, g):
                u = 4 * b + g
                pe.wait_ge(pt_ready, 3 * u + 3)
                if g == 0:
                    pe.wait_ge(ring_read, FILLS * b + VALUES + 1)
                if g % 2 == 0:
                    after(pe, att_ready, IT * (b - 1) + g // 2 + 1)
                c = (g % 2) * S
                for jt in range(IT):
                    for hh in range(HH):
                        q = slice(QUAD * hh, QUAD * hh + QUAD)
                        ins = nc.tensor.matmul(outp[g // 2][q, c + jt * P:c + S], vaug[:, p, jt, HH * g + hh, :],
                                               PT[:, g % 2, jt, hh, jt * P:S], start=(jt == 0), stop=(jt == IT - 1),
                                               skip_group_check=True)
                ins.then_inc(pv_done, 1)

            def output(b):
                pe.wait_ge(ot_ready, 2 * b + 2)
                for t in range(IT):
                    for g in range(G):
                        ins = nc.tensor.transpose(outp[t][:, g * P:g * P + P], OT[:, g, t * P:t * P + P], ident[:])
                    ins.then_inc(o_full, 1)

            xT(0, 0)
            pe.wait_ge(weights, 16 * 3)
            for c in range(4):
                chunk(0, 0, c)
            pe.wait_ge(er_ready, 1)
            for g in range(G):
                relative(0, 0, g, range(3))
            pe.wait_ge(wv_in, 32)
            pe.wait_ge(ones_set, 1)
            values(0, 0)
            xT(1, 1)
            chunk(1, 1, 0)
            chunk(1, 1, 1)
            two, third = range(2), range(2, 3)
            for b in range(B):
                p = b % 2
                begun, more, further = b >= 1, b + 1 < B, b + 2 < B
                n = b + 1, 1 - p
                scores(b, p, 0, two)
                if begun:
                    transposed(b - 1, 3, two)
                if more:
                    chunk(*n, 2)
                else:
                    pe.wait_ge(ring_read, FILLS * B)
                    next(ahead["tensor"])
                scores(b, p, 0, third)
                if begun:
                    transposed(b - 1, 3, third)
                if more:
                    chunk(*n, 3)
                if begun:
                    weighted(b - 1, 1 - p, 2)
                scores(b, p, 1, two)
                if more:
                    relative(*n, 0, two)
                transposed(b, 0, two)
                scores(b, p, 1, third)
                if more:
                    relative(*n, 0, third)
                transposed(b, 0, third)
                if more:
                    relative(*n, 1, two)
                else:
                    next(ahead["tensor"])
                if begun:
                    weighted(b - 1, 1 - p, 3)
                if more:
                    relative(*n, 1, third)
                scores(b, p, 2, two)
                if more:
                    relative(*n, 2, two)
                transposed(b, 1, two)
                scores(b, p, 2, third)
                if more:
                    relative(*n, 2, third)
                transposed(b, 1, third)
                if begun:
                    output(b - 1)
                scores(b, p, 3, two)
                weighted(b, p, 0)
                if more:
                    relative(*n, 3, two)
                transposed(b, 2, two)
                scores(b, p, 3, third)
                if more:
                    relative(*n, 3, third)
                    values(*n)
                if further:
                    xT(b + 2, p)
                transposed(b, 2, third)
                if further:
                    chunk(b + 2, p, 0)
                weighted(b, p, 1)
                if further:
                    chunk(b + 2, p, 1)
            transposed(B - 1, 3, range(3))
            weighted(B - 1, 1, 2)
            weighted(B - 1, 1, 3)
            next(ahead["tensor"])
            output(B - 1)


def attention(nc, ctx, X, ident, bank, d, ahead):
    def sb(name, shape, dt=F32, during=ctx):
        return during.enter_context(nc.sbuf_tensor("a1_" + name, shape, dt))

    def sem(name):
        return ctx.enter_context(nc.semaphore("a1_" + name))

    ctxT = sb("ctxT", [P, 2, S])
    WqR = sb("WqR", [P, G, P])
    WkR = sb("WkR", [P, G, P])
    WvT = sb("WvT", [P, D])
    WoT = sb("WoT", [P, D])
    bqR = sb("bqR", [P, G])
    bkR = sb("bkR", [P, G])
    lo = sb("lo", [P, 2])
    bv = sb("bv", [1, D])
    bo = sb("bo", [1, D])
    ones = sb("ones", [1, P])
    half = sb("half", [P, IT])
    stats = sb("stats", [P, 2, IT, 6])
    mv = sb("mv", [P, 2, IT, 2])
    veps = sb("veps", [P, 2, IT])
    rstd = sb("rstd", [P, 2, IT])
    xn = sb("xn", [P, 2, IT, D])
    xnT = sb("xnT", [P, 2, S])
    full = sb("full", [P, 2, 2, S])
    high = sb("high", [P, 2, 2, S], F32R)
    qst = sb("qst", [P, 2, G, S], F32R)
    kst = sb("kst", [P, G, S], F32R)
    kmask = [sb("kmask0", [P, HH, G, S], F32R), None]
    vaug = sb("vaug", [P, 2, IT, H, QUAD])
    nmax = qm = PT = OT = rden = att = attT = None

    def place_rest(late):
        nonlocal nmax, qm, PT, OT, rden, att, attT
        kmask[1] = sb("kmask1", [P, HH, G, S], F32R, late)
        nmax = sb("nmax", [P, 2, IT, P], F32, late)
        qm = sb("qm", [P, 2, S], F32R, late)
        PT = sb("PT", [P, 2, HH, IT, S], F32, late)
        OT = sb("OT", [P, G, S], F32, late)
        rden = sb("rden", [P, IT, H], F32, late)
        att = sb("att", [P, IT, D], F32, late)
        attT = sb("attT", [P, S], F32, late)

    ring, outp, scb, stb = bank[0:2], bank[2:4], bank[4:6], bank[6:8]

    XT, CHUNK, VALUES, FILLS = 0, 1, 5, 6
    NS = 4
    MAXIMA, UNIT = NS, NS + 1
    NT = HH

    weights, out_weights = sem("weights"), sem("out_weights")
    ones_set, vaug_set, half_set, kmask_zero, nmax_zero = (
        sem("ones_set"), sem("vaug_set"), sem("half_set"), sem("kmask_zero"), sem("nmax_zero"))
    ctx_in = [sem("ctx_in0"), sem("ctx_in1")]
    bn_raw, bn_mean, var_ready, rstd_ready = sem("bn_raw"), sem("bn_mean"), sem("var_ready"), sem("rstd_ready")
    xn_ready, ring_full, ring_read = sem("xn_ready"), sem("ring_full"), sem("ring_read")
    stack_ready, kmask_in = sem("stack_ready"), sem("kmask_in")
    sc_full, sc_read = sem("sc_full"), sem("sc_read")
    st_full, pt_ready, pv_done = sem("st_full"), sem("pt_ready"), sem("pv_done")
    ot_ready, o_full, rden_ready, att_ready = sem("ot_ready"), sem("o_full"), sem("rden_ready"), sem("att_ready")
    attT_full, attT_ready, wo_full, x_new = sem("attT_full"), sem("attT_ready"), sem("wo_full"), sem("x_new")

    def bank_of(fill):
        return ring[fill % 2]

    def place(u, f):
        return UNIT * u + f

    def score_bank(u, f):
        return scb[place(u, f) % 2]

    def sync_program(sp):
        for dst, src in ((WqR, "WqR1"), (bqR, "bqR1"), (WkR, "WkR1"), (bkR, "bkR1"), (lo, "lo")):
            sp.dma_start(dst[:], d[src]).then_inc(weights, 16)
        for b in range(2):
            sp.dma_start(ctxT[:, b, :], d["ctxT"][:, b * S:(b + 1) * S]).then_inc(ctx_in[b], 16)
        for dst, src in ((WvT, "WvT1"), (WoT, "WoT1")):
            sp.dma_start(dst[:], d[src]).then_inc(out_weights, 16)
        for dst, src in ((bv, "bv1"), (bo, "bo1")):
            sp.dma_start(dst[:], d[src].unsqueeze(0)).then_inc(out_weights, 16)

        def keys(b, p):
            sp.wait_ge(stack_ready, 4 * b + 4)
            sp.wait_ge(kmask_zero, 1 + p)
            after(sp, st_full, 4 * NT * (b - 1))
            for hh in range(HH):
                q = slice(QUAD * hh, QUAD * hh + QUAD)
                sp.dma_start(kmask[p][q, hh, :, :].bitcast(F32), kst[q, :, :].bitcast(F32)
                             ).then_inc(kmask_in, 16)

        keys(0, 0)
        yield
        for b in range(B - 1):
            p = b % 2
            if b + 2 < B:
                sp.wait_ge(ring_read, FILLS * b + VALUES + 1)
                sp.dma_start(ctxT[:, p, :], d["ctxT"][:, bass.ds((b + 2) * S, S)]).then_inc(ctx_in[p], 16)
            keys(b + 1, 1 - p)
            if b == B - 4:
                next(ahead["sync"])

    def gpsimd_program(pool):
        nc.gpsimd.memset(half[:], -0.5).then_inc(half_set, 1)
        pool.wait_ge(half_set, 1)

        def inverse_deviation(b, p):
            pool.wait_ge(var_ready, b + 1)
            after(pool, xn_ready, b - 1)
            nc.gpsimd.tensor_tensor(rstd[:, p, :], veps[:, p, :], half[:], ALU.pow).then_inc(rstd_ready, 1)

        inverse_deviation(0, 0)
        yield
        inverse_deviation(1, 1)
        yield
        nc.gpsimd.memset(vaug[:], 0.0).then_inc(vaug_set, 1)
        pool.wait_ge(vaug_set, 1)
        nc.gpsimd.memset(vaug[:, :, :, :, DH:DH + 1], 1.0).then_inc(vaug_set, 1)
        nc.gpsimd.memset(kmask[0][:].bitcast(F32), 0.0).then_inc(kmask_zero, 1)
        yield
        nc.gpsimd.memset(nmax[:], 0.0).then_inc(nmax_zero, 1)
        nc.gpsimd.memset(kmask[1][:].bitcast(F32), 0.0).then_inc(kmask_zero, 1)
        for b in range(2, B):
            inverse_deviation(b, b % 2)
        next(ahead["gpsimd"])
        next(ahead["gpsimd"])

    def vector_program(dve):
        nc.vector.memset(ones[:], 1.0).then_inc(ones_set, 1)

        def statistics(b, p):
            after(dve, rstd_ready, b - 1)
            for t in range(IT):
                ins = nc.vector.bn_stats(stats[:, p, t, :], tokens(X, b, t))
            ins.then_inc(bn_raw, 1)
            dve.wait_ge(bn_raw, b + 1)
            for t in range(IT):
                ins = nc.vector.bn_aggr(mv[:, p, t, :], stats[:, p, t, :])
            ins.then_inc(bn_mean, 1)
            dve.wait_ge(bn_mean, b + 1)
            nc.vector.tensor_scalar(veps[:, p, :], mv[:, p, :, 1], EPS, None, ALU.add).then_inc(var_ready, 1)

        def normalize(b, p):
            dve.wait_ge(rstd_ready, b + 1)
            after(dve, ring_full, FILLS * (b - 2) + XT + 1)
            for t in range(IT):
                ins = nc.vector.tensor_scalar(xn[:, p, t, :], tokens(X, b, t), mv[:, p, t, 0:1],
                                              rstd[:, p, t:t + 1], ALU.subtract, ALU.mult)
            ins.then_inc(xn_ready, 1)

        def stack(b, p, c):
            n = 4 * b + c
            dve.wait_ge(ring_read, FILLS * b + CHUNK + c + 1)
            to = (qst[:, p] if c < 2 else kst[:])[:, 2 * (c % 2):2 * (c % 2) + 2, :]
            if c < 2:
                if b >= 2:
                    dve.wait_ge(sc_full, place(G * (b - 1) - 1, NS - 1) + 1)
            else:
                after(dve, kmask_in, 64 * b)
            nc.vector.scalar_tensor_tensor(
                to, high[:, c % 2].bitcast(F32), lo[:, c // 2:c // 2 + 1], full[:, c % 2],
                ALU.mult, ALU.add).then_inc(stack_ready, 1)

        def maxima(b, g, fills):
            u = G * b + g
            if u == 0:
                dve.wait_ge(nmax_zero, 1)
            if u >= 2:
                dve.wait_ge(sc_full, place(u - 2, MAXIMA) + 1)
            for f in fills:
                dve.wait_ge(sc_full, place(u, f) + 1)
                c = QUAD * 2 * (f % 2) + MAXROW
                nc.vector.tensor_reduce(nmax[:, g % 2, f // 2, c:c + QUAD + 1:QUAD],
                                        score_bank(u, f)[:].rearrange("p (h j) -> p h j", j=S), AX.X, ALU.max,
                                        negate=True).then_inc(sc_read, 1)

        def less_max(b, p, g):
            u = G * b + g
            dve.wait_ge(sc_full, place(u, MAXIMA) + 1)
            after(dve, st_full, NT * (u - 1))
            nc.vector.tensor_tensor(qm[:, g % 2, :], score_bank(u, MAXIMA)[:, 0:S],
                                    qst[:, p, g, :].bitcast(F32), ALU.add).then_inc(sc_read, 1)

        def output(b):
            after(dve, attT_full, b)
            for t in range(IT):
                dve.wait_ge(o_full, IT * b + t + 1)
                o = outp[t][:].rearrange("p (h e) -> p h e", e=QUAD)
                nc.vector.reciprocal(rden[:, t, :], o[:, :, DH]).then_inc(rden_ready, 1)
                dve.wait_ge(rden_ready, IT * b + t + 1)
                nc.vector.tensor_tensor(att[:, t, :].rearrange("p (h e) -> p h e", e=DH), o[:, :, 0:DH],
                                        rden[:, t, :].unsqueeze(2).to_broadcast([P, H, DH]),
                                        ALU.mult).then_inc(att_ready, 1)

        def residual(b):
            dve.wait_ge(wo_full, b + 1)
            nc.vector.tensor_tensor(tokens(X, b, 0, IT), outp[1][:, S:2 * S], tokens(X, b, 0, IT),
                                    ALU.add).then_inc(x_new, 1)

        for b in range(2):
            statistics(b, b)
            yield
            normalize(b, b)
            yield
        dve.wait_ge(weights, 16 * 5)
        for c in range(4):
            stack(0, 0, c)
            yield
        one = [range(f, f + 1) for f in range(NS)]
        for b in range(B):
            p = b % 2
            begun, more, further = b >= 1, b + 1 < B, b + 2 < B
            maxima(b, 0, range(1))
            if further:
                statistics(b + 2, p)
            elif more:
                dve.wait_ge(x_new, 2)
                next(ahead["vector"])
            maxima(b, 0, range(1, 2))
            if more:
                stack(b + 1, 1 - p, 0)
            maxima(b, 0, range(2, NS))
            less_max(b, p, 0)
            maxima(b, 1, one[0])
            if more:
                stack(b + 1, 1 - p, 1)
            maxima(b, 1, range(1, 3))
            if more:
                stack(b + 1, 1 - p, 2)
            maxima(b, 1, one[3])
            less_max(b, p, 1)
            maxima(b, 2, one[0])
            if begun:
                output(b - 1)
            maxima(b, 2, one[1])
            if more:
                stack(b + 1, 1 - p, 3)
            maxima(b, 2, one[2])
            maxima(b, 2, one[3])
            less_max(b, p, 2)
            maxima(b, 3, one[0])
            if further:
                normalize(b + 2, p)
            elif more:
                next(ahead["vector"])
            maxima(b, 3, range(1, 3))
            if begun:
                residual(b - 1)
            maxima(b, 3, range(3, 4))
            less_max(b, p, 3)
        next(ahead["vector"])
        next(ahead["vector"])
        output(B - 1)
        residual(B - 1)

    def scalar_program(act):
        act.wait_ge(weights, 16 * 5)

        def read(b, fill):
            act.wait_ge(ring_full, FILLS * b + fill + 1)

        def xT(b, p):
            read(b, XT)
            after(act, ring_full, FILLS * (b - 2) + CHUNK + 2)
            nc.scalar.copy(xnT[:, p, :], bank_of(XT)[:, 0:S]).then_inc(ring_read, 1)

        def chunk(b, c):
            read(b, CHUNK + c)
            after(act, stack_ready, 4 * b + c - 1)
            for j in range(2):
                g = 2 * (c % 2) + j
                for to in (full, high):
                    ins = nc.scalar.activation(to[:, c % 2, j, :], bank_of(CHUNK + c)[:, j * S:j * S + S],
                                               ACT.Identity, bias=(bqR if c < 2 else bkR)[:, g:g + 1])
            ins.then_inc(ring_read, 1)

        def values(b, p):
            read(b, VALUES)
            if b == 0:
                act.wait_ge(vaug_set, 2)
            after(act, pv_done, 4 * (b - 1))
            nc.scalar.copy(vaug[:, p, :, :, 0:DH],
                           bank_of(VALUES)[:, 0:S].rearrange("p (t h e) -> p t h e", h=H, e=DH)
                           ).then_inc(ring_read, 1)

        def exps(b, g, fills):
            u = 4 * b + g
            after(act, pv_done, u - 1)
            for f in fills:
                act.wait_ge(st_full, NT * u + f + 1)
                nc.scalar.activation(PT[:, g % 2, f].rearrange("p j i -> p (j i)"), stb[f % 2][:], ACT.Exp,
                                     scale=SCALE).then_inc(pt_ready, 1)

        def oT(b, k):
            act.wait_ge(pv_done, 4 * b + 2 * k + 2)
            after(act, o_full, IT * b)
            nc.scalar.copy(OT[:, 2 * k:2 * k + 2, :], outp[k][:].rearrange("p (g i) -> p g i", i=S)
                           ).then_inc(ot_ready, 1)

        def attended(b):
            act.wait_ge(attT_full, b + 1)
            after(act, wo_full, b)
            nc.scalar.copy(attT[:], outp[1][:, 0:S]).then_inc(attT_ready, 1)

        xT(0, 0)
        yield
        for c in range(4):
            chunk(0, c)
            yield
        values(0, 0)
        yield
        xT(1, 1)
        yield
        chunk(1, 0)
        yield
        lower, upper = range(NT // 2), range(NT // 2, NT)
        for b in range(B):
            p = b % 2
            begun, more, further = b >= 1, b + 1 < B, b + 2 < B
            if begun:
                oT(b - 1, 0)
                exps(b - 1, 3, lower)
                exps(b - 1, 3, upper)
            if more:
                chunk(b + 1, 1)
                chunk(b + 1, 2)
            else:
                next(ahead["scalar"])
            exps(b, 0, lower)
            if begun:
                oT(b - 1, 1)
            exps(b, 0, upper)
            if more:
                chunk(b + 1, 3)
                values(b + 1, 1 - p)
            exps(b, 1, lower)
            if not more:
                next(ahead["scalar"])
            exps(b, 1, upper)
            if begun:
                attended(b - 1)
            exps(b, 2, lower)
            if further:
                xT(b + 2, p)
            exps(b, 2, upper)
            if further:
                chunk(b + 2, 0)
            elif more:
                next(ahead["scalar"])
        oT(B - 1, 0)
        exps(B - 1, 3, range(NT))
        oT(B - 1, 1)
        next(ahead["scalar"])
        attended(B - 1)

    def tensor_program(pe):
        def fill(b, n):
            after(pe, ring_read, FILLS * b + n - 1)
            return bank_of(n)

        def xT(b, p):
            pe.wait_ge(xn_ready, b + 1)
            to = fill(b, XT)
            for t in range(IT):
                ins = nc.tensor.transpose(to[:, t * P:t * P + P], xn[:, p, t, :], ident[:])
            ins.then_inc(ring_full, 1)

        def chunk(b, p, c):
            to = fill(b, CHUNK + c)
            if c == 0:
                pe.wait_ge(ring_read, FILLS * b + XT + 1)
            if c == 2:
                pe.wait_ge(ctx_in[p], 8 * (b - p) + 16)
            for j in range(2):
                g = 2 * (c % 2) + j
                w, x = (WqR, xnT) if c < 2 else (WkR, ctxT)
                ins = nc.tensor.matmul(to[:, j * S:j * S + S], w[:, g, :], x[:, p, :], start=True, stop=True)
            ins.then_inc(ring_full, 1)

        def values(b, p):
            to = fill(b, VALUES)
            for t in range(IT):
                nc.tensor.matmul(to[:, t * P:t * P + P], ctxT[:, p, t * P:t * P + P], WvT[:],
                                 start=True, stop=False)
                ins = nc.tensor.matmul(to[:, t * P:t * P + P], ones[:], bv[:], start=False, stop=True)
            ins.then_inc(ring_full, 1)

        def scores(b, p, g, fills):
            if g == 0:
                pe.wait_ge(kmask_in, 64 * (b + 1))
            for f in fills:
                after(pe, sc_read, place(G * b + g, f) - 1)
                t, k = f // 2, f % 2
                nc.tensor.matmul(score_bank(G * b + g, f)[:], qst[:, p, g, t * P:t * P + P],
                                 kmask[p][:, 2 * k:2 * k + 2, g, :], start=True, stop=True).then_inc(sc_full, 1)

        def maxima(u, g):
            pe.wait_ge(sc_read, place(u, NS - 1) + 1)
            pe.wait_ge(sc_read, place(u, MAXIMA) - 1)
            for t in range(IT):
                ins = nc.tensor.transpose(score_bank(u, MAXIMA)[:, t * P:t * P + P], nmax[:, g % 2, t, :],
                                          ident[:])
            ins.then_inc(sc_full, 1)

        def by_key(b, p, g, fills):
            u = 4 * b + g
            pe.wait_ge(sc_read, place(u, MAXIMA) + 1)
            for f in fills:
                after(pe, pt_ready, NT * u + f - 1)
                for jt in range(IT):
                    ins = nc.tensor.matmul(stb[f % 2][:, jt * S:jt * S + S], kmask[p][:, f, g, jt * P:jt * P + P],
                                           qm[:, g % 2, :], start=True, stop=True)
                ins.then_inc(st_full, 1)

        def weighted(b, p, g, jts):
            u = 4 * b + g
            pe.wait_ge(pt_ready, NT * (u + 1))
            if g == 0:
                pe.wait_ge(ring_read, FILLS * b + VALUES + 1)
                after(pe, att_ready, IT * (b - 1) + 1)
            if g == 2:
                after(pe, x_new, b)
            c = (g % 2) * S
            for jt in jts:
                for hh in range(HH):
                    q = slice(QUAD * hh, QUAD * hh + QUAD)
                    ins = nc.tensor.matmul(outp[g // 2][q, c:c + S], vaug[:, p, jt, HH * g + hh, :],
                                           PT[:, g % 2, hh, jt, :], start=(jt == 0), stop=(jt == IT - 1),
                                           skip_group_check=True)
                if jt == IT - 1:
                    ins.then_inc(pv_done, 1)

        def output(b):
            pe.wait_ge(ot_ready, 2 * b + 2)
            for t in range(IT):
                for g in range(G):
                    ins = nc.tensor.transpose(outp[t][:, g * P:g * P + P], OT[:, g, t * P:t * P + P], ident[:])
                ins.then_inc(o_full, 1)

        def attended(b):
            pe.wait_ge(att_ready, IT * b + IT)
            for t in range(IT):
                ins = nc.tensor.transpose(outp[1][:, t * P:t * P + P], att[:, t, :], ident[:])
            ins.then_inc(attT_full, 1)

        def project(b):
            pe.wait_ge(attT_ready, b + 1)
            for t in range(IT):
                to = outp[1][:, S + t * P:S + t * P + P]
                nc.tensor.matmul(to, attT[:, t * P:t * P + P], WoT[:], start=True, stop=False)
                ins = nc.tensor.matmul(to, ones[:], bo[:], start=False, stop=True)
            ins.then_inc(wo_full, 1)

        pe.wait_ge(weights, 16 * 5)
        xT(0, 0)
        yield
        for c in range(4):
            chunk(0, 0, c)
            yield
        pe.wait_ge(out_weights, 16 * 4)
        pe.wait_ge(ones_set, 1)
        values(0, 0)
        yield
        xT(1, 1)
        yield
        chunk(1, 1, 0)
        yield
        pe.wait_ge(ring_read, FILLS + CHUNK + 1)
        yield
        one = [range(f, f + 1) for f in range(NS)]
        for b in range(B):
            p = b % 2
            begun, more, further = b >= 1, b + 1 < B, b + 2 < B
            n = b + 1, 1 - p
            scores(b, p, 0, one[0])
            if begun:
                weighted(b - 1, 1 - p, 2, range(1))
                by_key(b - 1, 1 - p, 3, one[0])
            scores(b, p, 0, one[1])
            if begun:
                weighted(b - 1, 1 - p, 2, range(1, 2))
                by_key(b - 1, 1 - p, 3, one[1])
            scores(b, p, 0, one[2])
            if more:
                chunk(*n, 1)
            else:
                pe.wait_ge(ring_read, FILLS * B)
                next(ahead["tensor"])
            if begun:
                by_key(b - 1, 1 - p, 3, one[2])
            scores(b, p, 0, one[3])
            if begun:
                by_key(b - 1, 1 - p, 3, one[3])
            if more:
                chunk(*n, 2)
            maxima(4 * b + 0, 0)
            scores(b, p, 1, one[0])
            if begun:
                weighted(b - 1, 1 - p, 3, range(1))
            by_key(b, p, 0, one[0])
            scores(b, p, 1, one[1])
            if begun:
                weighted(b - 1, 1 - p, 3, range(1, 2))
            by_key(b, p, 0, one[1])
            scores(b, p, 1, one[2])
            if more:
                chunk(*n, 3)
            else:
                next(ahead["tensor"])
            by_key(b, p, 0, one[2])
            scores(b, p, 1, one[3])
            if more:
                values(*n)
            by_key(b, p, 0, one[3])
            maxima(4 * b + 1, 1)
            scores(b, p, 2, one[0])
            if begun:
                output(b - 1)
            by_key(b, p, 1, one[0])
            scores(b, p, 2, one[1])
            by_key(b, p, 1, one[1])
            scores(b, p, 2, one[2])
            weighted(b, p, 0, range(1))
            by_key(b, p, 1, one[2])
            scores(b, p, 2, one[3])
            weighted(b, p, 0, range(1, 2))
            by_key(b, p, 1, one[3])
            maxima(4 * b + 2, 2)
            scores(b, p, 3, one[0])
            if begun:
                attended(b - 1)
            weighted(b, p, 1, range(1))
            by_key(b, p, 2, one[0])
            scores(b, p, 3, one[1])
            by_key(b, p, 2, one[1])
            weighted(b, p, 1, range(1, 2))
            if further:
                xT(b + 2, p)
            scores(b, p, 3, one[2])
            if begun:
                project(b - 1)
            by_key(b, p, 2, one[2])
            scores(b, p, 3, one[3])
            if further:
                chunk(b + 2, p, 0)
            by_key(b, p, 2, one[3])
            maxima(4 * b + 3, 3)
        by_key(B - 1, 1, 3, range(NT))
        weighted(B - 1, 1, 2, range(IT))
        weighted(B - 1, 1, 3, range(IT))
        output(B - 1)
        next(ahead["tensor"])
        attended(B - 1)
        project(B - 1)

    programs = dict(sync=sync_program(nc.sync), gpsimd=gpsimd_program(nc.gpsimd), vector=vector_program(nc.vector),
                    scalar=scalar_program(nc.scalar), tensor=tensor_program(nc.tensor))

    def run():
        with ExitStack() as late:
            place_rest(late)
            run_block(nc, late, programs)

    return programs, run


def experts(nc, ctx, X, ident, bank, d, tag, E, blocks, shared, n_scaled, weights_early, ahead, ahead_at, out_dram=None,
            stored=None):
    def sb(name, shape, dt=F32, during=ctx):
        return during.enter_context(nc.sbuf_tensor(tag + "s_" + name, shape, dt))

    def sem(name, used=True):
        return ctx.enter_context(nc.semaphore(tag + name)) if used else None

    W = BANK
    T = W // P
    CHUNKS = B * S // W
    pairs = E // 2
    LAG = 2
    PAD = 6

    Wr = sb("Wr", [P, E])
    Wg = sb("Wg", [P, blocks, P])
    Wu = sb("Wu", [P, blocks, P])
    Wd = parts = None

    def place_weights(during):
        nonlocal Wd, parts
        Wd = sb("Wd", [P, blocks, P], F32, during)
        parts = sb("parts", [P, 2, 2, blocks, P], F32R, during)

    sel = sb("sel", [2 * E, pairs, 2 if n_scaled else 1, P], F32R)
    half = sb("half", [P, T])
    stats = sb("stats", [P, T, 6])
    mv = sb("mv", [P, T, 2])
    veps = sb("veps", [P, T])
    rstd = sb("rstd", [P, T])
    xn = sb("xn", [P, T, D])
    xnT = sb("xnT", [P, 2, W])
    xparts = sb("xparts", [P, 2, 2, W], F32R)
    lg = sb("lg", [P, T, E + PAD])
    top = sb("top", [P, T, 8])
    match = sb("match", [P, T, 8])
    rep = sb("rep", [P, T, E + PAD])
    chosen = sb("chosen", [P, T, E])
    diff = sb("diff", [P, T])
    th = sb("th", [P, T])
    w2 = sb("w2", [P, T])
    ez = sb("ez", [P, T, E])
    cw = sb("cw", [P, T, E])
    split = sb("split", [P, T, 2 * E], F32R)
    combT = sb("combT", [2 * E, 2, W], F32R)
    misc, route, gate_bank, up_bank, bc, acc = bank[0], bank[1], bank[2:4], bank[4:6], bank[6], bank[7]
    xs = xsparts = bcS = tanh = gated = scaled = hid = outT = None

    def place_rest(late):
        nonlocal xs, xsparts, bcS, tanh, gated, scaled, hid, outT
        if not weights_early:
            place_weights(late)
        if n_scaled:
            xs = sb("xs", [P, 4, W], F32, late)
            xsparts = sb("xsparts", [P, 4, 2, W], F32R, late)
        else:
            bcS = sb("bcS", [P, 2, W], F32, late)
            scaled = sb("scaled", [P, 2, W], F32, late)
        tanh = sb("tanh", [P, 2, W], F32, late)
        gated = sb("gated", [P, 2, W], F32, late)
        hid = sb("hid", [P, LAG + 1, W], F32, late)
        outT = sb("outT", [P, W], F32, late)

    router_in, sel_set, pads = sem("router_in"), sem("sel_set"), sem("pads")
    weights = [sem("Wg_in"), sem("Wu_in"), sem("Wd_in")]
    bn_raw, bn_mean, var_ready = sem("bn_raw"), sem("bn_mean"), sem("var_ready")
    half_set, rstd_ready = sem("half_set"), sem("rstd_ready")
    xn_ready, xT_full, xT_read = sem("xn_ready"), sem("xT_full"), sem("xT_read")
    logits_full, logits_read = sem("logits_full"), sem("logits_read", n_scaled)
    gate_in, gate_out = sem("gate_in", n_scaled), sem("gate_out")
    w_high, w_low, x_high, x_low = sem("w_high"), sem("w_low"), sem("x_high"), sem("x_low")
    xs_high, xs_low, bc_copied = sem("xs_high", n_scaled), sem("xs_low", n_scaled), sem("bc_copied", not n_scaled)
    chain, split_ready = sem("chain"), sem("split_ready")
    combT_full, combT_read = sem("combT_full"), sem("combT_read")
    bc_full, bc_read = sem("bc_full"), sem("bc_read", n_scaled)
    gate_full, up_full, tanh_ready, gated_ready = (
        sem("gate_full"), sem("up_full"), sem("tanh_ready"), sem("gated_ready"))
    scaled_ready, hid_ready, hid_used = sem("scaled_ready", not n_scaled), sem("hid_ready"), sem("hid_used")
    hid_weighed = sem("hid_weighed", not n_scaled)
    outT_read, out_full, x_new = sem("outT_read"), sem("out_full"), sem("x_new")

    FILLS = E if n_scaled else pairs

    def expert_ahead(c, i):
        n = E * c + 2 * (i // 3 + 1) + i % 3
        return n if n_scaled and i % 3 < 2 and n < E * CHUNKS else None

    def piece_ahead(c, i):
        k = i // PIECE + 1
        return k if not weights_early and c == 0 and i % PIECE == 0 and k < blocks // PIECE else None

    def unscaled(i):
        return n_scaled or i >= blocks - shared

    def hidden_done(n):
        c, i = n // blocks, n % blocks
        if not unscaled(i):
            return scaled_ready, (blocks - shared) * c + i + 1
        return hid_ready, (n + 1 if n_scaled else shared * c + i - (blocks - shared) + 1)

    def hidden_written(n):
        c, i = n // blocks, n % blocks
        return hidden_done(n) if unscaled(i) else (hid_weighed, (blocks - shared) * c + i + 1)

    sel_in = xnT[0:2 * E].rearrange("p c w -> p (c w)")

    def X_chunk(c, t=0, n=T):
        return X[:, c * W + t * P:c * W + (t + n) * P]

    NORMALIZE, TURN, LOGITS, CHOOSE, WEIGH, SPLIT = 0, 2, 3, 4, 7 if n_scaled else 6, 8
    OUT = LAG + 1
    PIECE = 3

    def sync_program(sp):
        sp.dma_start(Wr[:], d[tag + "Wr"]).then_inc(router_in, 16)
        sp.dma_start(sel_in, d[tag + "sel"].rearrange("e i j p -> e (i j p)")).then_inc(router_in, 16)
        sp.dma_start(Wg[:], d[tag + "Wg"]).then_inc(weights[0], 16)
        sp.dma_start(Wu[:], d[tag + "Wu"]).then_inc(weights[1], 16)
        yield
        sp.dma_start(Wd[:], d[tag + "Wd"]).then_inc(weights[2], 16)
        if ahead_at["tensor"]:
            next(ahead["sync"])
        if out_dram is not None:
            to = out_dram.rearrange("(t p) d -> p t d", p=P)
            for c in range(CHUNKS):
                sp.wait_ge(x_new, c + 1)
                sp.dma_start(to[:, T * c:T * c + T], X_chunk(c).rearrange("p (t d) -> p t d", d=D)).then_inc(stored, 16)
            sp.wait_ge(stored, 16 * CHUNKS)

    def gpsimd_program(pool):
        nc.gpsimd.memset(half[:], -0.5).then_inc(half_set, 1)
        pool.wait_ge(half_set, 1)

        def inverse_deviation(c):
            pool.wait_ge(var_ready, c + 1)
            after(pool, xn_ready, c)
            nc.gpsimd.tensor_tensor(rstd[:], veps[:], half[:], ALU.pow).then_inc(rstd_ready, 1)

        def weight_low(k):
            piece = slice(PIECE * k, PIECE * k + PIECE)
            for i, w in enumerate((Wg, Wu)):
                pool.wait_ge(w_high, 2 * k + i + 1)
                nc.gpsimd.tensor_tensor(parts[:, i, 1, piece, :], w[:, piece, :],
                                        parts[:, i, 0, piece, :].bitcast(F32), ALU.subtract).then_inc(w_low, 1)

        def input_low(c):
            pool.wait_ge(x_high, c + 1)
            nc.gpsimd.tensor_tensor(xparts[:, c % 2, 1, :], xnT[:, c % 2, :], xparts[:, c % 2, 0, :].bitcast(F32),
                                    ALU.subtract).then_inc(x_low, 1)

        def scaled_low(n):
            pool.wait_ge(xs_high, n + 1)
            nc.gpsimd.tensor_tensor(xsparts[:, n % 4, 1, :], xs[:, n % 4, :], xsparts[:, n % 4, 0, :].bitcast(F32),
                                    ALU.subtract).then_inc(xs_low, 1)

        def weigh_hidden(c, i):
            n, m = blocks * c + i, (blocks - shared) * c + i
            pool.wait_ge(scaled_ready, m + 1)
            pool.wait_ge(bc_copied, m + 1)
            after(pool, hid_used, n - LAG)
            nc.gpsimd.tensor_tensor(hid[:, n % (LAG + 1), :], scaled[:, m % 2, :], bcS[:, m % 2, :],
                                    ALU.mult).then_inc(hid_weighed, 1)

        inverse_deviation(0)
        yield
        if weights_early:
            for k in range(blocks // PIECE):
                weight_low(k)
        input_low(0)
        yield
        if not weights_early:
            weight_low(0)
        if n_scaled:
            scaled_low(0)
            scaled_low(1)
        for c in range(CHUNKS):
            more = c + 1 < CHUNKS
            for i in range(blocks):
                if more and i == TURN:
                    input_low(c + 1)
                if not unscaled(i):
                    weigh_hidden(c, i)
                if more and i == NORMALIZE:
                    inverse_deviation(c + 1)
                if expert_ahead(c, i):
                    scaled_low(expert_ahead(c, i))
                if piece_ahead(c, i):
                    weight_low(piece_ahead(c, i))
                if c == CHUNKS - 1 and i in ahead_at["gpsimd"]:
                    next(ahead["gpsimd"])

    def vector_program(dve):
        links = [0]

        def link(ins):
            links[0] += 1
            ins.then_inc(chain, 1)
            dve.wait_ge(chain, links[0])

        def statistics(c):
            after(dve, rstd_ready, c)
            for t in range(T):
                ins = nc.vector.bn_stats(stats[:, t, :], X_chunk(c, t, 1))
            ins.then_inc(bn_raw, 1)
            dve.wait_ge(bn_raw, c + 1)
            after(dve, xn_ready, c)
            for t in range(T):
                ins = nc.vector.bn_aggr(mv[:, t, :], stats[:, t, :])
            ins.then_inc(bn_mean, 1)
            dve.wait_ge(bn_mean, c + 1)
            nc.vector.tensor_scalar(veps[:], mv[:, :, 1], EPS, None, ALU.add).then_inc(var_ready, 1)

        def normalize(c):
            dve.wait_ge(rstd_ready, c + 1)
            after(dve, xT_full, c)
            for t in range(T):
                ins = nc.vector.tensor_scalar(xn[:, t, :], X_chunk(c, t, 1), mv[:, t, 0:1],
                                              rstd[:, t:t + 1], ALU.subtract, ALU.mult)
            ins.then_inc(xn_ready, 1)

        def choose():
            for t in range(T):
                ins = nc.vector.max(top[:, t, :], lg[:, t, 0:E])
            link(ins)
            link(nc.vector.tensor_copy(match[:, :, 0:2], top[:, :, 0:2]))
            for t in range(T):
                ins = nc.vector.match_replace(rep[:, t, :], match[:, t, :], lg[:, t, :], -LOWEST)
            link(ins)
            link(nc.vector.tensor_tensor(chosen[:], rep[:, :, 0:E], lg[:, :, 0:E], ALU.not_equal))

        def wide(x):
            return x.unsqueeze(2).to_broadcast([P, T, E])

        def route_start(c):
            if not n_scaled:
                dve.wait_ge(gate_out, c + 1)
                link(nc.vector.tensor_scalar(ez[:], ez[:], 1.0, None, ALU.add))
                link(nc.vector.reciprocal(lg[:, :, 0:E], ez[:]))
                choose()
                return
            dve.wait_ge(logits_full, c + 1)
            nc.vector.tensor_copy(lg[:, :, 0:E], route[:, 0:T * E].rearrange("p (t e) -> p t e", e=E)
                                  ).then_inc(logits_read, 1)
            dve.wait_ge(logits_read, c + 1)
            choose()
            nc.vector.tensor_tensor(diff[:], top[:, :, 0], top[:, :, 1], ALU.subtract).then_inc(gate_in, 1)

        def route_end(c):
            if n_scaled:
                dve.wait_ge(gate_out, c + 1)
                link(nc.vector.tensor_scalar(w2[:], th[:], -0.25, 0.25, ALU.mult, ALU.add))
                link(nc.vector.tensor_tensor(cw[:], lg[:, :, 0:E], wide(top[:, :, 0]), ALU.is_ge))
                link(nc.vector.tensor_tensor(cw[:], cw[:], wide(th[:]), ALU.mult))
                link(nc.vector.tensor_scalar(cw[:], cw[:], 0.5, None, ALU.mult))
                link(nc.vector.tensor_tensor(cw[:], cw[:], wide(w2[:]), ALU.add))
                link(nc.vector.tensor_tensor(cw[:], cw[:], chosen[:], ALU.mult))
            else:
                link(nc.vector.tensor_tensor(diff[:], top[:, :, 0], top[:, :, 1], ALU.add))
                link(nc.vector.tensor_scalar(diff[:], diff[:], 1e-20, None, ALU.add))
                link(nc.vector.reciprocal(w2[:], diff[:]))
                link(nc.vector.tensor_tensor(cw[:], lg[:, :, 0:E], chosen[:], ALU.mult))
                link(nc.vector.tensor_tensor(cw[:], cw[:], wide(w2[:]), ALU.mult))
                link(nc.vector.tensor_scalar(cw[:], cw[:], 0.5 * 2.5, None, ALU.mult))
            after(dve, combT_full, c)
            link(nc.vector.tensor_copy(split[:, :, 0:E], cw[:]))
            nc.vector.tensor_tensor(split[:, :, E:2 * E], cw[:], split[:, :, 0:E].bitcast(F32),
                                    ALU.subtract).then_inc(split_ready, 1)

        def scale_input(n):
            c, e = n // E, n % E
            dve.wait_ge(bc_full, n + 1)
            if n >= 4:
                dve.wait_ge(up_full, blocks * c + 3 * (e // 2 - 1))
            nc.vector.tensor_tensor(xs[:, e % 4, :], bc[:], xnT[:, c % 2, :], ALU.mult).then_inc(bc_read, 1)

        def hidden(c, i):
            n = blocks * c + i
            dve.wait_ge(tanh_ready, n + 1)
            if n >= 2:
                dve.wait_ge(*hidden_done(n - 2))
            nc.vector.scalar_tensor_tensor(gated[:, n % 2, :], tanh[:, n % 2, :], 1.0, gate_bank[n % 2][:],
                                           ALU.add, ALU.mult).then_inc(gated_ready, 1)
            dve.wait_ge(gated_ready, n + 1)
            dve.wait_ge(up_full, n + 1)
            if unscaled(i):
                after(dve, hid_used, n - LAG)
                nc.vector.scalar_tensor_tensor(hid[:, n % (LAG + 1), :], gated[:, n % 2, :], 1.0 if n_scaled else 0.5,
                                               up_bank[n % 2][:], ALU.mult, ALU.mult).then_inc(hid_ready, 1)
            else:
                m = (blocks - shared) * c + i
                after(dve, hid_weighed, m - 1)
                nc.vector.tensor_tensor(scaled[:, m % 2, :], gated[:, n % 2, :], up_bank[n % 2][:],
                                        ALU.mult).then_inc(scaled_ready, 1)

        def output(c):
            dve.wait_ge(out_full, c + 1)
            nc.vector.tensor_tensor(X_chunk(c), X_chunk(c), misc[:], ALU.add).then_inc(x_new, 1)

        statistics(0)
        nc.vector.memset(lg[:], LOWEST).then_inc(pads, 1)
        nc.vector.memset(match[:], LOWEST).then_inc(pads, 1)
        dve.wait_ge(router_in, 32)
        nc.vector.tensor_copy(sel[:].rearrange("e i j p -> e (i j p)"), sel_in).then_inc(sel_set, 1)
        yield
        normalize(0)
        yield
        dve.wait_ge(pads, 2)
        route_start(0)
        yield
        route_end(0)
        yield
        if n_scaled:
            scale_input(0)
            scale_input(1)
        for c in range(CHUNKS):
            more = c + 1 < CHUNKS
            for i in range(blocks):
                hidden(c, i)
                if c == CHUNKS - 1 and i in ahead_at["vector"]:
                    next(ahead["vector"])
                if expert_ahead(c, i):
                    scale_input(expert_ahead(c, i))
                if more and i == NORMALIZE:
                    statistics(c + 1)
                    normalize(c + 1)
                if i == OUT and c >= 1:
                    output(c - 1)
                if more and i == CHOOSE:
                    route_start(c + 1)
                if more and i == WEIGH:
                    route_end(c + 1)
        output(CHUNKS - 1)

    def scalar_program(act):
        def xT(c):
            act.wait_ge(xT_full, c + 1)
            if c == 0:
                act.wait_ge(sel_set, 1)
            if c >= 2:
                act.wait_ge(gate_full, blocks * (c - 1))
                act.wait_ge(up_full, blocks * (c - 1))
                act.wait_ge(x_low, c - 1)
                if n_scaled:
                    act.wait_ge(bc_read, FILLS * (c - 1))
            nc.scalar.copy(xnT[:, c % 2, :], misc[:]).then_inc(xT_read, 1)
            act.wait_ge(xT_read, c + 1)
            nc.scalar.copy(xparts[:, c % 2, 0, :], xnT[:, c % 2, :]).then_inc(x_high, 1)

        def gate(c):
            if n_scaled:
                act.wait_ge(gate_in, c + 1)
                nc.scalar.activation(th[:], diff[:], ACT.Tanh, scale=0.5).then_inc(gate_out, 1)
            else:
                act.wait_ge(logits_full, c + 1)
                after(act, split_ready, c)
                nc.scalar.activation(ez[:].rearrange("p t e -> p (t e)"), route[:, 0:T * E], ACT.Exp,
                                     scale=-1.0).then_inc(gate_out, 1)

        def comb(c):
            act.wait_ge(combT_full, c + 1)
            after(act, bc_full, FILLS * (c - 1))
            nc.scalar.copy(combT[:, c % 2, :], route[0:2 * E, :]).then_inc(combT_read, 1)

        def tanhs(c, i):
            n = blocks * c + i
            act.wait_ge(gate_full, n + 1)
            after(act, gated_ready, n - 1)
            nc.scalar.activation(tanh[:, n % 2, :], gate_bank[n % 2][:], ACT.Tanh, scale=0.5
                                 ).then_inc(tanh_ready, 1)

        def out(c):
            act.wait_ge(hid_used, blocks * (c + 1))
            after(act, out_full, c)
            nc.scalar.copy(outT[:], acc[:]).then_inc(outT_read, 1)

        def weight_high(k):
            piece = slice(PIECE * k, PIECE * k + PIECE)
            for i, w in enumerate((Wg, Wu)):
                act.wait_ge(weights[i], 16)
                nc.scalar.copy(parts[:, i, 0, piece, :], w[:, piece, :]).then_inc(w_high, 1)

        def scaled_high(n):
            act.wait_ge(bc_read, n + 1)
            if n >= 4:
                act.wait_ge(up_full, blocks * (n // E) + 3 * (n % E // 2 - 1))
            nc.scalar.copy(xsparts[:, n % 4, 0, :], xs[:, n % 4, :]).then_inc(xs_high, 1)

        def weights_copied(c, i):
            m = FILLS * c + i
            act.wait_ge(bc_full, m + 1)
            after(act, hid_weighed, m - 1)
            nc.scalar.copy(bcS[:, m % 2, :], bc[:]).then_inc(bc_copied, 1)

        if weights_early:
            for k in range(blocks // PIECE):
                weight_high(k)
        yield
        xT(0)
        yield
        gate(0)
        yield
        comb(0)
        yield
        if not weights_early:
            weight_high(0)
        if n_scaled:
            scaled_high(0)
            scaled_high(1)
        for c in range(CHUNKS):
            more = c + 1 < CHUNKS
            for i in range(blocks):
                tanhs(c, i)
                if piece_ahead(c, i):
                    weight_high(piece_ahead(c, i))
                if not unscaled(i):
                    weights_copied(c, i)
                if i and expert_ahead(c, i - 1):
                    scaled_high(expert_ahead(c, i - 1))
                if i == LAG - 1 and c >= 1:
                    out(c - 1)
                if more and i == TURN:
                    xT(c + 1)
                if more and i == CHOOSE:
                    gate(c + 1)
                if more and i == SPLIT:
                    comb(c + 1)
                if c == CHUNKS - 1 and i in ahead_at["scalar"]:
                    next(ahead["scalar"])
        out(CHUNKS - 1)

    def tensor_program(pe):
        def xT(c):
            pe.wait_ge(xn_ready, c + 1)
            after(pe, xT_read, c)
            after(pe, x_new, c - 2)
            for t in range(T):
                ins = nc.tensor.transpose(misc[:, t * P:t * P + P], xn[:, t, :], ident[:])
            ins.then_inc(xT_full, 1)

        def logits(c):
            pe.wait_ge(xT_read, c + 1)
            after(pe, combT_read, c)
            for t in range(T):
                ins = nc.tensor.matmul(route[:, t * E:t * E + E], xnT[:, c % 2, t * P:t * P + P], Wr[:],
                                       start=True, stop=True)
            ins.then_inc(logits_full, 1)

        def comb(c):
            pe.wait_ge(split_ready, c + 1)
            for t in range(T):
                ins = nc.tensor.transpose(route[0:2 * E, t * P:t * P + P], split[:, t, :].bitcast(F32), ident[:])
            ins.then_inc(combT_full, 1)

        def spread(c, f):
            pe.wait_ge(combT_read, c + 1)
            if n_scaled:
                after(pe, bc_read, FILLS * c + f)
                w = sel[:, f // 2, f % 2, :]
            else:
                after(pe, bc_copied, FILLS * c + f)
                w = sel[:, f, 0, :]
            nc.tensor.matmul(bc[:], w, combT[:, c % 2, :], start=True, stop=True).then_inc(bc_full, 1)

        def product(to, which, i, x, signal):
            for n, (wp, xp) in enumerate(((0, 0), (1, 0), (0, 1))):
                ins = nc.tensor.matmul(to, parts[:, which, wp, i, :], x[:, xp, :], start=(n == 0), stop=(n == 2))
            ins.then_inc(signal, 1)

        def up(c, i):
            n = blocks * c + i
            x = xparts[:, c % 2]
            if c == 0:
                pe.wait_ge(w_low, 2 * (i // PIECE) + 2)
            pe.wait_ge(x_low, c + 1)
            after(pe, gated_ready, n - 1)
            product(gate_bank[n % 2][:], 0, i, x, gate_full)
            if n >= 2:
                pe.wait_ge(*hidden_done(n - 2))
            to = up_bank[n % 2]
            if not n_scaled:
                product(to[:], 1, i, x, up_full)
                return
            q, part = i // 3, i % 3
            e = 2 * q + min(part, 1)
            pe.wait_ge(xs_low, E * c + e + 1)
            if part < 2:
                product(to[:], 1, i, xsparts[:, e % 4], up_full)
            else:
                nc.tensor.matmul(to[0:64, :], Wu[:, i, 0:64], xs[:, (e - 1) % 4, :], start=True, stop=True)
                nc.tensor.matmul(to[64:P, :], Wu[:, i, 64:P], xs[:, e % 4, :], start=True,
                                 stop=True).then_inc(up_full, 1)

        def down(c, i):
            n = blocks * c + i
            pe.wait_ge(*hidden_written(n))
            if i == 0:
                after(pe, outT_read, c)
                if c == 0:
                    pe.wait_ge(weights[2], 16)
            nc.tensor.matmul(acc[:], Wd[:, i, :], hid[:, n % (LAG + 1), :], start=(i == 0),
                             stop=(i == blocks - 1)).then_inc(hid_used, 1)

        def out(c):
            pe.wait_ge(outT_read, c + 1)
            pe.wait_ge(xT_read, min(c + 3, CHUNKS))
            for t in range(T):
                ins = nc.tensor.transpose(misc[:, t * P:t * P + P], outT[:, t * P:t * P + P], ident[:])
            ins.then_inc(out_full, 1)

        xT(0)
        yield
        pe.wait_ge(router_in, 32)
        logits(0)
        yield
        comb(0)
        yield
        pe.wait_ge(sel_set, 1)
        if n_scaled:
            spread(0, 0)
            spread(0, 1)
        for c in range(CHUNKS):
            more = c + 1 < CHUNKS
            for i in range(blocks):
                up(c, i)
                if expert_ahead(c, i):
                    spread(expert_ahead(c, i) // E, expert_ahead(c, i) % E)
                if not unscaled(i):
                    spread(c, i)
                if i >= LAG:
                    down(c, i - LAG)
                elif c:
                    down(c - 1, blocks - LAG + i)
                if more and i == TURN:
                    xT(c + 1)
                if i == OUT and c >= 1:
                    out(c - 1)
                if more and i == LOGITS:
                    logits(c + 1)
                if more and i == SPLIT:
                    comb(c + 1)
                if c == CHUNKS - 1 and i in ahead_at["tensor"]:
                    pe.wait_ge(x_new, CHUNKS - 1)
                    pe.wait_ge(combT_read, CHUNKS)
                    next(ahead["tensor"])
        for i in range(blocks - LAG, blocks):
            down(CHUNKS - 1, i)
        if ahead_at["tensor"]:
            next(ahead["tensor"])
        out(CHUNKS - 1)

    programs = dict(sync=sync_program(nc.sync), gpsimd=gpsimd_program(nc.gpsimd), vector=vector_program(nc.vector),
                    scalar=scalar_program(nc.scalar), tensor=tensor_program(nc.tensor))

    def run():
        with ExitStack() as late:
            place_rest(late)
            run_block(nc, late, programs)

    return programs, place_weights, run


def expert_pairs(w):
    w = w.transpose(1, 0, 2).reshape(D, -1, 2, w.shape[2])
    rest = w[..., P:].reshape(D, w.shape[1], 1, P)
    return np.ascontiguousarray(np.concatenate([w[..., :P], rest], 2).reshape(D, -1, P))


def selectors(E, half_blocks):
    out = np.zeros((2, E, E // 2, 2, P), np.float32)
    for e in range(E):
        out[:, e, e // 2, e % 2] = 1.0
    if half_blocks:
        half = np.zeros((2, E, E // 2, 1, P), np.float32)
        for j in range(2):
            half[:, :, :, 0, j * P // 2:(j + 1) * P // 2] = out[:, :, :, j, 0:P // 2]
        out = half
    return out.reshape((2 * E,) + out.shape[2:])


def quadrants(w):
    w = w.reshape(G, HH, DH, -1)
    out = np.zeros((w.shape[-1], G, HH, QUAD), np.float32)
    for r in range(3):
        out[:, :, :, r * DH:(r + 1) * DH] = w.transpose(3, 0, 1, 2)
    return out.reshape(w.shape[-1], G, P)


def low_rows(r):
    out = np.zeros((HH, QUAD), np.float32)
    out[:, r * DH:(r + 1) * DH] = -1.0
    return out.reshape(P)


def er_quadrants(Er):
    out = np.zeros((HH, QUAD, HH, S), np.float32)
    for hh in range(HH):
        for r in range(3):
            out[hh, r * DH:(r + 1) * DH, hh] = Er.T
    return out.reshape(P, HH, S)


def xattn_ffn_twice_kernel(nc, x, out, **d):
    rel = nc.dram_tensor("relative_scores", [2, H, S, PITCH], F32).ap()
    with ExitStack() as ctx:
        X = ctx.enter_context(nc.sbuf_tensor("X", [P, B * IT * D], F32))
        ident = ctx.enter_context(nc.sbuf_tensor("identity", [P, P], F32))
        bank = [ctx.enter_context(nc.psum_tensor(f"bank{i}", [P, BANK], F32)) for i in range(8)]
        stored = ctx.enter_context(nc.semaphore("stored"))
        steps = dict(gpsimd=(0, 2, 8), vector=(0, 1, 2, 3, 6, 7, 8, 9), scalar=range(4, 12), tensor=range(4, 12))
        no_steps = dict(gpsimd=(), vector=(), scalar=(), tensor=())
        attention1, experts1 = {}, {}
        experts0, _, run_experts0 = experts(
            nc, ctx, X, ident, bank, d, tag="m0_", E=8, blocks=12, shared=0, n_scaled=True,
            weights_early=False, ahead=attention1, ahead_at=steps)
        relative_attention(nc, X, ident, bank, x, d, rel, experts0)
        programs, place_weights1, run_experts1 = experts(
            nc, ctx, X, ident, bank, d, tag="m1_", E=16, blocks=9, shared=1, n_scaled=False,
            weights_early=True, ahead={}, ahead_at=no_steps, out_dram=out, stored=stored)
        experts1.update(programs)
        programs, run_attention1 = attention(nc, ctx, X, ident, bank, d, experts1)
        attention1.update(programs)
        run_experts0()
        place_weights1(ctx)
        run_attention1()
        run_experts1()


def laid_out(inputs):
    def quad_bias(b):
        return quadrants(b[:, None])[0].T

    def halves(w, ws):
        blocks = np.zeros((D, E1 // 2 + 1, P), np.float32)
        blocks[:, :-1] = w.transpose(1, 0, 2).reshape(D, E1 // 2, P)
        blocks[:, -1, :P // 2] = ws
        return blocks

    i = inputs
    E0, E1 = i["L0_ffn_Wr"].shape[1], i["L1_ffn_gate_w"].shape[0]
    bk1 = quad_bias(i["L1_xattn_bk"]).copy()
    bk1[MAXROW::QUAD] = 1.0
    return dict(
        x=i["x"].reshape(B * S, D), ctxT=i["ctx_1024"].reshape(B * S, D).T,
        ident=np.eye(P, dtype=np.float32), lo=np.stack([low_rows(1), low_rows(2)], 1),
        WqR0=quadrants(i["L0_xattn_Wq"]), bqR0=quad_bias(i["L0_xattn_bq"]),
        WkR0=quadrants(i["L0_xattn_Wk"]), bkR0=quad_bias(i["L0_xattn_bk"]),
        WvT0=i["L0_xattn_Wv"].T, bv0=i["L0_xattn_bv"], ErR=er_quadrants(i["L0_xattn_Er"]),
        m0_Wr=i["L0_ffn_Wr"], m0_sel=selectors(E0, False), m0_Wg=expert_pairs(i["L0_ffn_W1"]),
        m0_Wu=expert_pairs(i["L0_ffn_W3"]),
        m0_Wd=expert_pairs(i["L0_ffn_W2"].transpose(0, 2, 1)).transpose(2, 1, 0),
        WqR1=quadrants(i["L1_xattn_Wq"]), bqR1=quad_bias(i["L1_xattn_bq"]),
        WkR1=quadrants(i["L1_xattn_Wk"]), bkR1=bk1,
        WvT1=i["L1_xattn_Wv"].T, bv1=i["L1_xattn_bv"], WoT1=i["L1_xattn_Wo"].T, bo1=i["L1_xattn_bo"],
        m1_Wr=i["L1_ffn_gate_w"].T, m1_sel=selectors(E1, True),
        m1_Wg=halves(i["L1_ffn_w_gate"], i["L1_ffn_ws_gate"]),
        m1_Wu=halves(i["L1_ffn_w_up"], i["L1_ffn_ws_up"]),
        m1_Wd=halves(i["L1_ffn_w_down"].transpose(0, 2, 1), i["L1_ffn_ws_down"].T).transpose(2, 1, 0))


def kernel(**inputs):
    import numpy as _np
    import concourse.bacc as _bacc
    from concourse import mybir as _mybir
    from concourse.bass_utils import run_bass_kernel_spmd as _run

    nc = _bacc.Bacc("TRN2", target_bir_lowering=False, num_devices=1)
    arrays, args = {}, {}
    for name, a in laid_out({k: _np.asarray(v) for k, v in inputs.items()}).items():
        a = _np.ascontiguousarray(a)
        arrays[f"in_{name}_dram"] = a
        args[name] = nc.dram_tensor(f"in_{name}_dram", a.shape, _mybir.dt.from_np(a.dtype), kind="ExternalInput").ap()
    out = nc.dram_tensor("out_0_dram", (B * S, D), F32, kind="ExternalOutput").ap()
    xattn_ffn_twice_kernel(nc, out=out, **args)
    r = _run(nc, [arrays], core_ids=[0])
    return r.results[0]["out_0_dram"].reshape(B, S, D)
```
